# Optimizing a Trainium2 kernel written in Bass

```python
import numpy as np
import jax
import jax.numpy as jnp

def _softmax(x, axis=-1):
    return jax.nn.softmax(x, axis=axis)

def _gelu(x):
    return jax.nn.gelu(x, approximate=True)

def _silu(x):
    return jax.nn.silu(x)

def _sigmoid(x):
    return jax.nn.sigmoid(x)

def _layernorm(x, axis=-1, eps=1e-05):
    m = jnp.mean(x, axis=axis, keepdims=True)
    v = jnp.var(x, axis=axis, keepdims=True)
    return (x - m) / jnp.sqrt(v + eps)

def _scatter_add(tgt, idx, src, axis=0):
    return tgt.at[idx].add(src)

def _segment_sum(src, seg, n):
    return jax.ops.segment_sum(src, seg, n)
kernel_name = 'mk_xattn_ffn_d1_seqx_r8_50bb1d'

def setup_inputs(seed: int=0):
    np.random.seed(seed)
    _w = jnp.asarray

    def _rec_inputs():
        import jax
        import jax.numpy as jnp
        _rk = jax.random.key(seed)
        x = -0.000125 + 0.9999 * jax.random.normal(jax.random.fold_in(_rk, 1), (64, 64, 256), jnp.float32)
        _lenS = 64 - jax.random.randint(jax.random.fold_in(_rk, 7), (64,), 0, max(1, 64 // 4) + 1, jnp.int32)
        _lenS2 = 64 - jax.random.randint(jax.random.fold_in(_rk, 8), (64,), 0, max(1, 64 // 4) + 1, jnp.int32)
        _ctx_2048P = jax.random.normal(jax.random.fold_in(_rk, 11), (64, 16, 256), jnp.float32)
        _ctx_2048c = jax.random.dirichlet(jax.random.fold_in(_rk, 511), 0.3 * jnp.ones((16,), jnp.float32), (64, 64))
        _ctx_2048t = jnp.einsum('bsk,bkd->bsd', _ctx_2048c, _ctx_2048P)
        _ctx_2048t = _ctx_2048t * jax.lax.rsqrt(jnp.mean(jnp.square(_ctx_2048t)) + 1e-12) * 0.953939
        ctx_2048 = 1.72703e-05 + 1.00003 * (_ctx_2048t + 0.3 * jax.random.normal(jax.random.fold_in(_rk, 611), (64, 64, 256), jnp.float32))
        return (x, ctx_2048)
    x, ctx_2048 = _rec_inputs()

    def _L0_xattn_setup():
        import jax, jax.numpy as jnp
        import numpy as np
        DIM = 256
        NH = 16
        HD = DIM // NH
        EPS = 1e-06
        IMG_LEN = 257

        def rms_norm(x, w, eps=EPS):
            xf = x.astype(jnp.float32)
            y = xf * jax.lax.rsqrt(jnp.mean(xf * xf, axis=-1, keepdims=True) + eps)
            return y.astype(x.dtype) * w

        def linear(x, w, b):
            return jnp.einsum('blc,oc->blo', x, w) + b

        def attention(q, k, v):
            scale = 1.0 / jnp.sqrt(jnp.asarray(HD, q.dtype))
            scores = jnp.einsum('bqhd,bkhd->bhqk', q, k) * scale
            probs = jax.nn.softmax(scores, axis=-1)
            return jnp.einsum('bhqk,bkhd->bqhd', probs, v)
        key = jax.random.key(seed)
        ks = jax.random.split(key, 12)
        B, L = (2, 1024)
        s = 0.02
        inp = {'x': jax.random.normal(ks[0], (B, L, DIM), jnp.float32), 'context': jax.random.normal(ks[1], (B, 769, DIM), jnp.float32), 'q_w': jax.random.normal(ks[2], (DIM, DIM), jnp.float32) * s, 'q_b': jnp.zeros((DIM,), jnp.float32), 'k_w': jax.random.normal(ks[3], (DIM, DIM), jnp.float32) * s, 'k_b': jnp.zeros((DIM,), jnp.float32), 'v_w': jax.random.normal(ks[4], (DIM, DIM), jnp.float32) * s, 'v_b': jnp.zeros((DIM,), jnp.float32), 'k_img_w': jax.random.normal(ks[5], (DIM, DIM), jnp.float32) * s, 'k_img_b': jnp.zeros((DIM,), jnp.float32), 'v_img_w': jax.random.normal(ks[6], (DIM, DIM), jnp.float32) * s, 'v_img_b': jnp.zeros((DIM,), jnp.float32), 'o_w': jax.random.normal(ks[7], (DIM, DIM), jnp.float32) * s, 'o_b': jnp.zeros((DIM,), jnp.float32), 'norm_q_w': jnp.ones((DIM,), jnp.float32), 'norm_k_w': jnp.ones((DIM,), jnp.float32), 'norm_k_img_w': jnp.ones((DIM,), jnp.float32)}
        return inp
    _L0_xattn_all = _L0_xattn_setup()
    _L0_xattn_in = {k: v for k, v in _L0_xattn_all.items() if k in ('q_w', 'q_b', 'k_w', 'k_b', 'v_w', 'v_b', 'k_img_w', 'k_img_b', 'v_img_w', 'v_img_b', 'o_w', 'o_b', 'norm_q_w', 'norm_k_w', 'norm_k_img_w')}
    del _L0_xattn_all

    def _L0_ffn_setup():
        import jax, jax.numpy as jnp
        import numpy as np
        TOP_K = 2
        key = jax.random.key(seed)
        k1, k2, k3, k4 = jax.random.split(key, 4)
        B, S, H, I, E = (2, 128, 256, 176, 8)
        hidden_states = jax.random.normal(k1, (B, S, H), dtype=jnp.float32)
        gate_w = jax.random.normal(k2, (E, H), dtype=jnp.float32) * (1.0 / np.sqrt(H))
        w1 = jax.random.normal(k3, (E, 2 * I, H), dtype=jnp.float32) * (1.0 / np.sqrt(H))
        w2 = jax.random.normal(k4, (E, H, I), dtype=jnp.float32) * (1.0 / np.sqrt(I))
        return {'hidden_states': hidden_states, 'gate_w': gate_w, 'w1': w1, 'w2': w2}
    _L0_ffn_all = _L0_ffn_setup()
    _L0_ffn_in = {k: v for k, v in _L0_ffn_all.items() if k in ('gate_w', 'w1', 'w2')}
    del _L0_ffn_all
    return {'x': x, 'ctx_2048': ctx_2048, 'L0_xattn_q_w': _L0_xattn_in['q_w'], 'L0_xattn_q_b': _L0_xattn_in['q_b'], 'L0_xattn_k_w': _L0_xattn_in['k_w'], 'L0_xattn_k_b': _L0_xattn_in['k_b'], 'L0_xattn_v_w': _L0_xattn_in['v_w'], 'L0_xattn_v_b': _L0_xattn_in['v_b'], 'L0_xattn_k_img_w': _L0_xattn_in['k_img_w'], 'L0_xattn_k_img_b': _L0_xattn_in['k_img_b'], 'L0_xattn_v_img_w': _L0_xattn_in['v_img_w'], 'L0_xattn_v_img_b': _L0_xattn_in['v_img_b'], 'L0_xattn_o_w': _L0_xattn_in['o_w'], 'L0_xattn_o_b': _L0_xattn_in['o_b'], 'L0_xattn_norm_q_w': _L0_xattn_in['norm_q_w'], 'L0_xattn_norm_k_w': _L0_xattn_in['norm_k_w'], 'L0_xattn_norm_k_img_w': _L0_xattn_in['norm_k_img_w'], 'L0_ffn_gate_w': _L0_ffn_in['gate_w'], 'L0_ffn_w1': _L0_ffn_in['w1'], 'L0_ffn_w2': _L0_ffn_in['w2']}

def reference(x, ctx_2048, L0_xattn_q_w, L0_xattn_q_b, L0_xattn_k_w, L0_xattn_k_b, L0_xattn_v_w, L0_xattn_v_b, L0_xattn_k_img_w, L0_xattn_k_img_b, L0_xattn_v_img_w, L0_xattn_v_img_b, L0_xattn_o_w, L0_xattn_o_b, L0_xattn_norm_q_w, L0_xattn_norm_k_w, L0_xattn_norm_k_img_w, L0_ffn_gate_w, L0_ffn_w1, L0_ffn_w2):
    import jax
    import jax.numpy as jnp

    def _L0_xattn_ref(x, context, q_w, q_b, k_w, k_b, v_w, v_b, k_img_w, k_img_b, v_img_w, v_img_b, o_w, o_b, norm_q_w, norm_k_w, norm_k_img_w):
        import jax, jax.numpy as jnp
        import numpy as np
        DIM = 256
        NH = 16
        HD = DIM // NH
        EPS = 1e-06
        IMG_LEN = 257

        def rms_norm(x, w, eps=EPS):
            xf = x.astype(jnp.float32)
            y = xf * jax.lax.rsqrt(jnp.mean(xf * xf, axis=-1, keepdims=True) + eps)
            return y.astype(x.dtype) * w

        def linear(x, w, b):
            return jnp.einsum('blc,oc->blo', x, w) + b

        def attention(q, k, v):
            scale = 1.0 / jnp.sqrt(jnp.asarray(HD, q.dtype))
            scores = jnp.einsum('bqhd,bkhd->bhqk', q, k) * scale
            probs = jax.nn.softmax(scores, axis=-1)
            return jnp.einsum('bhqk,bkhd->bqhd', probs, v)
        B, L, _ = x.shape
        ctx_img = context[:, :IMG_LEN]
        ctx_txt = context[:, IMG_LEN:]
        q = rms_norm(linear(x, q_w, q_b), norm_q_w).reshape(B, L, NH, HD)
        k = rms_norm(linear(ctx_txt, k_w, k_b), norm_k_w).reshape(B, -1, NH, HD)
        v = linear(ctx_txt, v_w, v_b).reshape(B, -1, NH, HD)
        k_img = rms_norm(linear(ctx_img, k_img_w, k_img_b), norm_k_img_w).reshape(B, -1, NH, HD)
        v_img = linear(ctx_img, v_img_w, v_img_b).reshape(B, -1, NH, HD)
        img_x = attention(q, k_img, v_img)
        txt_x = attention(q, k, v)
        out = (txt_x + img_x).reshape(B, L, DIM)
        return linear(out, o_w, o_b)

    def _L0_ffn_ref(hidden_states, gate_w, w1, w2):
        import jax, jax.numpy as jnp
        import numpy as np
        TOP_K = 2
        B, S, H = hidden_states.shape
        E = gate_w.shape[0]
        T = B * S
        x = hidden_states.reshape(T, H)
        logits = jnp.einsum('th,eh->te', x, gate_w)
        probs = jax.nn.softmax(logits, axis=-1)
        topw, sel = jax.lax.top_k(probs, TOP_K)
        topw = topw / jnp.sum(topw, axis=-1, keepdims=True)
        combine = jnp.zeros((T, E), dtype=x.dtype).at[jnp.arange(T)[:, None], sel].add(topw)
        gate_up = jnp.einsum('th,eoh->eto', x, w1)
        g, u = jnp.split(gate_up, 2, axis=-1)
        act = jax.nn.silu(g) * u
        expert_out = jnp.einsum('eti,ehi->eth', act, w2)
        out = jnp.einsum('eth,te->th', expert_out, combine)
        return out.reshape(B, S, H)
    x = x + _L0_xattn_ref(_layernorm(x, axis=-1), ctx_2048, L0_xattn_q_w, L0_xattn_q_b, L0_xattn_k_w, L0_xattn_k_b, L0_xattn_v_w, L0_xattn_v_b, L0_xattn_k_img_w, L0_xattn_k_img_b, L0_xattn_v_img_w, L0_xattn_v_img_b, L0_xattn_o_w, L0_xattn_o_b, L0_xattn_norm_q_w, L0_xattn_norm_k_w, L0_xattn_norm_k_img_w)
    x = x + _L0_ffn_ref(_layernorm(x, axis=-1), L0_ffn_gate_w, L0_ffn_w1, L0_ffn_w2)
    return x

_drawn_inputs = setup_inputs


def setup_inputs(seed=0):
    import zlib

    import numpy as np

    out = dict(_drawn_inputs(seed))
    spreads = {'L0_xattn_q_b': (0.0, 0.289),
     'L0_xattn_k_b': (0.0, 0.1),
     'L0_xattn_v_b': (0.0, 0.1),
     'L0_xattn_k_img_b': (0.0, 0.797),
     'L0_xattn_v_img_b': (0.0, 0.1),
     'L0_xattn_o_b': (0.0, 0.1),
     'L0_xattn_norm_q_w': (1.0, 0.6),
     'L0_xattn_norm_k_w': (1.0, 0.2),
     'L0_xattn_norm_k_img_w': (1.0, 0.6)}
    factors = {}
    for name, (base, spread) in spreads.items():
        noise = np.random.default_rng([zlib.crc32(name.encode()), seed]).standard_normal(out[name].shape)
        drawn = base * np.exp(spread * noise) if base else spread * noise
        out[name] = jnp.asarray(drawn.astype(out[name].dtype))
    for name, factor in factors.items():
        out[name] = (out[name] * factor).astype(out[name].dtype)
    return out
```

```python
from contextlib import ExitStack

import numpy as np

import concourse.bass as bass
from concourse import mybir

ALU = mybir.AluOpType
ACT = mybir.ActivationFunctionType
AX = mybir.AxisListType
F32 = mybir.dt.float32
F32R = mybir.dt.float32r
F16 = mybir.dt.float16
BF16 = mybir.dt.bfloat16
I32 = mybir.dt.int32
U32 = mybir.dt.uint32

P = 128
B, L, D = 64, 64, 256
NH, HD = 16, 16
NE, FI = 8, 176
KC = D // P
NB = P // L
T = B * L
NT = T // P
NPAIR = NH // 2
VW = HD + 1
IMG_LEN = 257
assert L <= IMG_LEN

REG = T + P
ROWS = NE * REG + P
ROW = D + 2
NSLOT = 72
RING = 8
assert NSLOT * P >= 2 * T + NE * (P - 1) - P + 1 and NSLOT % RING == 0
EW = 2 * KC * FI + 2 * D
FA, FB = P, FI - P
WS = NE * EW // NT
assert WS * NT == NE * EW

SKEW = 4
LAST = NT + 6


class Tile:

    def __init__(self, j, s):
        self.n = j * SKEW + s
        self.slot = s % SKEW
        self.par = s % 2
        self.quad = j + s // SKEW
        self.pair = j * 2 + s // 2
        self.live = not isinstance(j, int) or 0 <= self.n < NT
        self.twins = j * 2 + s // 2


def need(eng, sem, value):
    if isinstance(value, int) and value <= 0:
        return
    eng.wait_ge(sem, value)


def need_alone(eng, passed, sem, value):
    need(eng, sem, value)
    if not isinstance(value, int):
        eng.sem_inc(passed, 1)


def turns(eng, turn):
    first, last = 2, NT // SKEW
    for j in range(first):
        for s in range(SKEW):
            turn(j, s)
    with eng.Fori(first, last) as j:
        for s in range(SKEW):
            turn(j, s)
    for i in range(last * SKEW, LAST):
        turn(i // SKEW, i % SKEW)


def build(nc, x, ctx_t, w_proj, w_exp, w_gate, bias, norm_q, norm_k, out):
    sorted_rows = nc.dram_tensor("sorted_rows", (ROWS, ROW), F32, kind="Internal").ap()
    expert_out = nc.dram_tensor("expert_out", (2 * T, D), F32, kind="Internal").ap()
    with ExitStack() as stack:
        build_in(nc, stack, x, ctx_t, w_proj, w_exp, w_gate, bias, norm_q, norm_k, out,
                 sorted_rows, expert_out)


def build_in(nc, stack, x, ctx_t, w_proj, w_exp, w_gate, bias, norm_q, norm_k, out,
             sorted_rows, expert_out):
    def sb(name, shape, dt):
        return stack.enter_context(nc.sbuf_tensor(name, shape, dt))

    def sem(name):
        return stack.enter_context(nc.semaphore(name))

    bank = stack.enter_context(nc.psum_tensor("bank", [P, 8, 512], F32))

    ident = sb("ident", [P, P], F32)
    ident_b = sb("ident_b", [P, P], BF16)
    below = sb("below", [P, P], BF16)
    ones_b = sb("ones_b", [P, P], BF16)
    head_of = sb("head_of", [32, NPAIR, P], BF16)
    expert_no = sb("expert_no", [P, NE], F32)
    slot_no = sb("slot_no", [1, NSLOT], F32)
    result_row = sb("result_row", [P, 2, NT], I32)
    half_neg = sb("half_neg", [P, 2], F32)
    zero_one = sb("zero_one", [2, 2], F32)
    ones_row_f = sb("ones_row_f", [2, P], F32)
    ones_row = sb("ones_row", [2, P], F32R)
    bias_hl = sb("bias_hl", [2, 4 * D], F32R)
    wp_h = sb("wp_h", [P, 4, KC, D], F32R)
    wp_l = sb("wp_l", [P, 4, KC, D], F32R)
    gate_w = sb("gate_w", [P, KC, NE], F32)
    qk_norm = sb("qk_norm", [P, D], F32)
    we_f = sb("we_f", [P, 2, WS], F32)
    we_h = sb("we_h", [P, NE * EW], F32R)
    we_l = sb("we_l", [P, NE * EW], F32R)

    x1 = sb("x1", [P, NT, D], F32)
    ctx_in = sb("ctx_in", [P, 2, KC * P], F32)
    stats = sb("stats", [P, 2, 6], F32)
    mean_var = sb("mean_var", [P, 2, 2], F32)
    veps = sb("veps", [P, 2, 1], F32)
    rstd = sb("rstd", [P, 2, 1], F32)
    xn = sb("xn", [P, 2, D], F32)
    xt_h = sb("xt_h", [P, 2, KC, P], F32R)
    xt_l = sb("xt_l", [P, 2, KC, P], F32R)
    ct_h = sb("ct_h", [P, 2, KC, P], F32R)
    ct_l = sb("ct_l", [P, 2, KC, P], F32R)
    square = sb("square", [P, 2, D], BF16)
    sumsq = sb("sumsq", [P, 2, 2], F32)
    ms_eps = sb("ms_eps", [P, 2, 2], F32)
    r_qk = sb("r_qk", [P, 2, 2], F32)
    qn = sb("qn", [P, 2, D], F32)
    kn = sb("kn", [P, 2, D], F32)
    v_sb = sb("v_sb", [P, 2, 2, NPAIR, VW], F32)
    v_bd = sb("v_bd", [P, 2, NB, 2, NPAIR * VW], F32)
    qkt_h = sb("qkt_h", [P, 2, 2, KC, P], F16)
    qt_l = sb("qt_l", [P, 2, KC, P], F16)
    kt_l = sb("kt_l", [P, 2, KC, P], F16)
    k_bd = sb("k_bd", [P, 2, 2, KC, NB, 8, L], F16)
    row_max = sb("row_max", [P, 2, NH], F32)
    neg_max = sb("neg_max", [P, 2, 2 * NH], BF16)
    neg_max_t = sb("neg_max_t", [2 * NH, 2, P], BF16)
    probs = sb("probs", [P, 2, NB * NPAIR * L], F32)
    wp_f = probs[:, :, :].rearrange("p a b -> p (a b)")
    r_sum = sb("r_sum", [P, 2, NH], F32)
    att = sb("att", [P, 2, NH, HD], F32)
    at_h = sb("at_h", [P, 2, KC, P], F32R)
    at_l = sb("at_l", [P, 2, KC, P], F32R)
    stats2 = sb("stats2", [P, 2, 6], F32)
    mean_var2 = sb("mean_var2", [P, 2, 2], F32)
    veps2 = sb("veps2", [P, 2, 1], F32)
    rstd2 = sb("rstd2", [P, 2, 1], F32)
    row = sb("row", [P, 2, SKEW, ROW], F32)
    ht = sb("ht", [P, 2, KC, P], F32)
    logit = sb("logit", [P, 2, NE], F32)
    top8 = sb("top8", [P, 2, 8], F32)
    top8_no = sb("top8_no", [P, 2, 8], U32)
    top_no = sb("top_no", [P, 2, 2], F32)
    gap = sb("gap", [P, 2, 2], F32)
    e_gap = sb("e_gap", [P, 2, 2], F32)
    one_e = sb("one_e", [P, 2], F32)
    chosen = sb("chosen", [P, 2, 2, 2, NE], F32)
    chosen_b = sb("chosen_b", [P, 2, 2, NE], BF16)
    filled = sb("filled", [P, NE], F32)
    place = sb("place", [P, 2, NE], F32)
    place_of = sb("place_of", [P, 2, 2, NE], F32)
    place_f = sb("place_f", [P, 2, 2], F32)
    place_i = sb("place_i", [P, 2, 2, 2], I32)

    pad_rows = sb("pad_rows", [P, ROW], F32)
    region_no = sb("region_no", [1, NE], F32)
    count = sb("count", [1, NE], F32)
    count_i = sb("count_i", [1, NE], I32)
    tiles_i = sb("tiles_i", [1, NE], I32)
    tiles = sb("tiles", [1, NE], F32)
    cum = sb("cum", [1, 4, NE], F32)
    slot_row = sb("slot_row", [1, NSLOT], I32)
    slot_w = sb("slot_w", [1, NSLOT], I32)
    pad_at = sb("pad_at", [1, NE], I32)

    k_norm = row[:, 1, 0, 0:D]
    bias_f = row[0:2, 0, :, 0:D]

    def words(t, pattern):
        return t.rearrange(pattern)

    hs = words(k_bd[:, :, :, :, :, :, :], "p a b c d e f -> p (a b c d e f)").bitcast(F32)[:, 0:RING * ROW].rearrange(
        "p (r d) -> p r d", r=RING)
    hst_h, hst_l, au_h, au_l = xt_h, xt_l, at_h, at_l
    silu_g, act_u = xn[:, :, 0:FI], qn[:, :, 0:FI]
    y_sb = words(probs[:, :, :], "p a b -> p (a b)")[:, 0:4 * D].rearrange("p (r d) -> p r d", r=4)
    past = words(we_f[0:1, :, :], "p a b -> p (a b)")[:, 0:NSLOT * NE].rearrange("p (s e) -> p s e", e=NE)
    past_n = words(v_bd[0:1, :, :, :, :], "p a b c d -> p (a b c d)")[:, 0:NSLOT * NE].rearrange("p (s e) -> p s e", e=NE)
    slot_e = words(ctx_in[0:1, :, :], "p a b -> p (a b)")[:, 0:4 * NSLOT].rearrange("p (a s) -> p a s", a=4)
    fin_in = k_bd[:, :, :, :, :, :, :].rearrange("p a b c d e f -> p (a b c d e f)").bitcast(F32).rearrange(
        "p (r k m d) -> p r k m d", r=4, k=2, m=2)

    x_first, x_second, x_rest = sem("x_first"), sem("x_second"), sem("x_rest")
    consts_loaded = sem("consts_loaded")
    ctx_loaded = [sem(f"ctx_loaded{p}") for p in range(2)]
    we_loaded = [sem(f"we_loaded{p}") for p in range(2)]
    v_spread = [sem(f"v_spread{p}") for p in range(2)]
    k_spread = [sem(f"k_spread{p}") for p in range(2)]
    row_sent = [sem(f"row_sent{s}") for s in range(SKEW)]
    pads_sent = sem("pads_sent")
    sp_passed, pool_passed, dve_passed, pe_passed = (sem(n) for n in ("sp_passed", "pool_passed", "dve_passed", "pe_passed"))
    pool_setup = sem("pool_setup")
    dve_setup = sem("dve_setup")
    names = """ln1_stats ln1_mean ln1_veps ln1_rstd xn_ready x_transposed xt_h_ready xt_l_ready
        ct_h_ready ct_ready projected v_ready q_squared k_squared qk_veps qk_rstd qn_ready kn_ready
        qk_transposed qkt_h_ready qt_l_ready kt_l_ready max_scored max_found neg_hi_ready neg_max_ready
        neg_max_transposed neg_max_t_ready scored probs_ready weighed sum_inverted att_ready
        att_transposed at_h_ready at_l_ready o_projected x1_ready ln2_stats ln2_mean ln2_veps
        ln2_rstd row_ready row2_ready h_transposed ht_ready gated logit_ready we_h_ready we_ready""".split()
    S = {n: sem(n) for n in names}
    pair_names = "tops no_ready gap_ready choice_ready e_gap_ready routed place_ready filled_new place_sel place_sum place_set weight_set1 weight_set2 weight_set3 ids_set".split()
    R = {n: sem(n) for n in pair_names}
    plan = sem("plan")
    hs_loaded = [sem(f"hs_loaded{r}") for r in range(RING)]
    y_sent = [sem(f"y_sent{r}") for r in range(4)]
    names2 = """h2_transposed h2_h_ready h2_l_ready gate_up silu_ready act_ready act_transposed
        au_h_ready au_l_ready y_done y_ready""".split()
    F = {n: sem(n) for n in names2}
    fin_loaded = [sem(f"fin_loaded{r}") for r in range(4)]
    fin_stored = [sem(f"fin_stored{r}") for r in range(4)]
    fin_sum1, fin_sum2 = sem("fin_sum1"), sem("fin_sum2")

    tr_bank = bank[:, 0, :]
    qv_bank = bank[:, 1, :]
    k_bank = bank[:, 2, :]
    qkt_bank = bank[:, 3, :]
    score_bank = bank[:, 4:6, :].rearrange("p a b -> p (a b)")
    av_bank = bank[:, 6, :]
    mo_bank = bank[:, 7, :]

    block = stack.enter_context(nc.Block())

    SETUP_POOL = 18
    SETUP_DVE = 12

    @block.sync
    def _(sp):
        x_v = x.rearrange("(t p) d -> p t d", p=P)
        sp.dma_start(x1[:, 0:2, :], x_v[:, 0:2, :]).then_inc(x_first, 16)
        sp.dma_start(wp_f, w_proj).then_inc(consts_loaded, 16)
        for p in range(2):
            sp.dma_start(ctx_in[:, p, :], ctx_t[p * P:(p + 1) * P, :]).then_inc(ctx_loaded[p], 16)
        sp.dma_start(bias_f, bias.rearrange("r (m d) -> r m d", m=4)).then_inc(consts_loaded, 16)
        sp.dma_start(qk_norm[:, :], norm_q.partition_broadcast(P)).then_inc(consts_loaded, 16)
        sp.dma_start(k_norm, norm_k.partition_broadcast(P)).then_inc(consts_loaded, 16)
        sp.dma_start(gate_w[:, :, :], w_gate.rearrange("p (c e) -> p c e", c=KC)).then_inc(consts_loaded, 16)
        sp.dma_start(x1[:, 2:8, :], x_v[:, 2:8, :]).then_inc(x_second, 16)
        for p in range(2):
            sp.dma_start(we_f[:, p, :], w_exp[p * P:(p + 1) * P, :]).then_inc(we_loaded[p], 16)
        sp.dma_start(x1[:, 8:NT, :], x_v[:, 8:NT, :]).then_inc(x_rest, 16)

        def load_next(t, i):
            need_alone(sp, sp_passed, S["ct_ready"], t.n - 1)
            sp.dma_start(ctx_in[:, t.par, :], ctx_t[bass.ds(t.n * P, P), :]).then_inc(ctx_loaded[t.par], 16)
            need_alone(sp, sp_passed, S["we_ready"], t.n - 1)
            sp.dma_start(we_f[:, t.par, :], w_exp[bass.ds(t.n * P, P), :]).then_inc(we_loaded[t.par], 16)

        def spread_v(t):
            need_alone(sp, sp_passed, S["v_ready"], t.n + 1)
            need_alone(sp, sp_passed, S["weighed"], t.n - 1)
            for b in range(NB):
                for q in range(2):
                    sp.dma_start(v_bd[q * L:(q + 1) * L, t.par, b, q, :],
                                 v_sb[b * L:(b + 1) * L, t.par, q, :, :].rearrange("p g d -> p (g d)")
                                 ).then_inc(v_spread[t.par], 16)

        def spread_k(t):
            need_alone(sp, sp_passed, S["qkt_h_ready"], t.n + 1)
            need_alone(sp, sp_passed, S["kt_l_ready"], t.n + 1)
            need_alone(sp, sp_passed, S["scored"], t.n - 1)
            for h in range(8):
                r = slice(h * HD, (h + 1) * HD)
                for part, src in ((0, qkt_h[r, t.par, 1, :, :]), (1, kt_l[r, t.par, :, :])):
                    sp.dma_start(k_bd[r, t.par, part, :, :, h, :],
                                 src.rearrange("p c (b l) -> p c b l", b=NB)).then_inc(k_spread[t.par], 16)

        sp.wait_ge(dve_setup, SETUP_DVE)
        sp.wait_ge(pool_setup, SETUP_POOL)

        def turn(j, s):
            if Tile(j, s - 1).live:
                spread_k(Tile(j, s - 1))
            if Tile(j, s).live:
                spread_v(Tile(j, s))
            if Tile(j, s + 2).live and (isinstance(j, int) and j * SKEW + s + 2 < NT or not isinstance(j, int)):
                load_next(Tile(j, s + 2), None)

        turns_sp(sp, turn)

        sp.wait_ge(plan, PLAN)
        for e in range(NE):
            at = sp.value_load(pad_at[0:1, e:e + 1], min_val=0, max_val=NE * REG)
            sp.dma_start(sorted_rows[bass.ds(at, P), :], pad_rows[:, :]).then_inc(pads_sent, 16)
        sp.dma_start(sorted_rows[NE * REG:ROWS, :], pad_rows[:, :]).then_inc(pads_sent, 16)
        sp.wait_ge(pads_sent, 16 * (NE + 1))
        for s in range(SKEW):
            sp.wait_ge(row_sent[s], 2 * 16 * (NT // SKEW))

        def load_slot(j, r):
            at = sp.value_load(slot_row[0:1, bass.ds(j * RING + r, 1)], min_val=0, max_val=NE * REG)
            sp.dma_start(hs[:, r, :], sorted_rows[bass.ds(at, P), :]).then_inc(hs_loaded[r], 16)

        for r in range(RING):
            load_slot(0, r)
        with sp.Fori(1, NSLOT // RING) as j:
            for r in range(RING):
                need_alone(sp, sp_passed, y_sent[r % 4], (2 * j - 1 + r // 4) * 16)
                load_slot(j, r)
        for r in range(4):
            sp.wait_ge(y_sent[r], 16 * NSLOT // 4)

        ev = expert_out.rearrange("(k t p) d -> p k t d", k=2, p=P)
        ov = out.rearrange("(t p) d -> p t d", p=P)
        for g in range(NT // 2):
            if g >= 4:
                sp.wait_ge(fin_stored[g % 4], 16 * (g // 4))
            for k in range(2):
                sp.dma_start(fin_in[:, g % 4, k, :, :], ev[:, k, 2 * g:2 * g + 2, :]).then_inc(fin_loaded[g % 4], 16)
            if g >= 3:
                h = g - 3
                sp.wait_ge(fin_sum2, h + 1)
                sp.dma_start(ov[:, 2 * h:2 * h + 2, :], fin_in[:, h % 4, 0, :, :]).then_inc(fin_stored[h % 4], 16)
        for h in range(NT // 2 - 3, NT // 2):
            sp.wait_ge(fin_sum2, h + 1)
            sp.dma_start(ov[:, 2 * h:2 * h + 2, :], fin_in[:, h % 4, 0, :, :]).then_inc(fin_stored[h % 4], 16)
        for r in range(4):
            sp.wait_ge(fin_stored[r], 16 * (NT // 8))

    @block.gpsimd
    def _(pool):
        done = [0]

        def setup(ins):
            done[0] += 1
            ins.then_inc(pool_setup, 1)

        def after():
            pool.wait_ge(pool_setup, done[0])

        setup(pool.memset(ident[:, :], 0.0))
        setup(pool.memset(below[:, :], 0.0))
        setup(pool.memset(head_of[:, :, :], 0.0))
        setup(pool.memset(half_neg[:, :], -0.5))
        setup(pool.memset(ones_b[:, :], 1.0))
        after()
        setup(pool.affine_select(out=ident[:, :], in_=ident[:, :], compare_op=ALU.not_equal, fill=1.0,
                                 base=0, pattern=[[-1, P]], channel_multiplier=1))
        setup(pool.affine_select(out=below[:, :], in_=below[:, :], compare_op=ALU.is_ge, fill=1.0,
                                 base=0, pattern=[[-1, P]], channel_multiplier=1))
        for base in (0, -NH):
            after()
            v = head_of[:, :, :].rearrange("r g (q m) -> r g q m", q=2)
            setup(pool.affine_select(out=v, in_=v, compare_op=ALU.not_equal, fill=1.0, base=base,
                                     pattern=[[-2, NPAIR], [-1, 2], [0, L]], channel_multiplier=1))
        setup(pool.tensor_copy(ident_b[:, :], ident[:, :]))
        setup(pool.iota(expert_no[:, :], [[1, NE]], base=0, channel_multiplier=0,
                        allow_small_or_imprecise_dtypes=True))
        setup(pool.iota(slot_no[:, :], [[1, NSLOT]], base=0, channel_multiplier=0,
                        allow_small_or_imprecise_dtypes=True))
        setup(pool.iota(filled[:, :], [[REG, NE]], base=0, channel_multiplier=0,
                        allow_small_or_imprecise_dtypes=True))
        setup(pool.iota(region_no[:, :], [[REG, NE]], base=0, channel_multiplier=0,
                        allow_small_or_imprecise_dtypes=True))
        setup(pool.iota(result_row[:, :, :], [[T, 2], [P, NT]], base=0, channel_multiplier=1))
        setup(pool.iota(zero_one[:, 1:2], [[0, 1]], base=0, channel_multiplier=1,
                        allow_small_or_imprecise_dtypes=True))
        setup(pool.memset(pad_rows[:, :], 0.0))
        after()
        setup(pool.iota(pad_rows[:, D:D + 1].bitcast(I32), [[0, 1]], base=2 * T, channel_multiplier=1))
        assert done[0] == SETUP_POOL, done[0]

        def split_ctx(t):
            need_alone(pool, pool_passed, ctx_loaded[t.par], (t.twins + 1) * 16)
            need_alone(pool, pool_passed, S["projected"], t.n - 1)
            src = ctx_in[:, t.par, :].rearrange("p (c n) -> p c n", c=KC)
            pool.tensor_scalar(ct_h[:, t.par, :, :], src, 1.0, 1.0, ALU.mult, ALU.mult).then_inc(S["ct_h_ready"], 1)
            need_alone(pool, pool_passed, S["ct_h_ready"], t.n + 1)
            pool.tensor_tensor(ct_l[:, t.par, :, :], src, ct_h[:, t.par, :, :].bitcast(F32),
                               ALU.subtract).then_inc(S["ct_ready"], 1)

        def split_weights(t):
            need_alone(pool, pool_passed, we_loaded[t.par], (t.twins + 1) * 16)
            cols = bass.ds(t.n * WS, WS)
            pool.tensor_copy(we_h[:, cols], we_f[:, t.par, :]).then_inc(S["we_h_ready"], 1)
            need_alone(pool, pool_passed, S["we_h_ready"], t.n + 1)
            pool.tensor_tensor(we_l[:, cols], we_f[:, t.par, :], we_h[:, cols].bitcast(F32),
                               ALU.subtract).then_inc(S["we_ready"], 1)

        def inv_sqrt(t, out_, tmp, in_, scale, eps, ready, mid, done_):
            need_alone(pool, pool_passed, ready, t.n + 1)
            pool.tensor_scalar(tmp, in_, scale, eps, ALU.mult, ALU.add).then_inc(mid, 1)
            need_alone(pool, pool_passed, mid, t.n + 1)
            pool.tensor_tensor(out_, tmp, half_neg[:, 0:tmp.shape[1]], ALU.pow).then_inc(done_, 1)

        def ln1(t):
            need_alone(pool, pool_passed, S["xn_ready"], t.n - 1)
            inv_sqrt(t, rstd[:, t.par, :], veps[:, t.par, :], mean_var[:, t.par, 1:2], 1.0, 1e-5,
                     S["ln1_mean"], S["ln1_veps"], S["ln1_rstd"])

        def qk_rms(t):
            need_alone(pool, pool_passed, S["qn_ready"], t.n - 1)
            need_alone(pool, pool_passed, S["kn_ready"], t.n - 1)
            need_alone(pool, pool_passed, S["q_squared"], t.n + 1)
            inv_sqrt(t, r_qk[:, t.par, :], ms_eps[:, t.par, :], sumsq[:, t.par, :], 1.0 / D, 1e-6,
                     S["k_squared"], S["qk_veps"], S["qk_rstd"])

        def ln2(t):
            need_alone(pool, pool_passed, S["row_ready"], t.n - 1)
            inv_sqrt(t, rstd2[:, t.par, :], veps2[:, t.par, :], mean_var2[:, t.par, 1:2], 1.0, 1e-5,
                     S["ln2_mean"], S["ln2_veps"], S["ln2_rstd"])

        def send(a, b):
            need_alone(pool, pool_passed, S["row2_ready"], b.n + 1)
            for k in range(2):
                pool.tensor_copy(row[:, k, a.slot:a.slot + 2, D:D + 1].bitcast(I32),
                                 result_row[:, k, bass.ds(a.n, 2)].unsqueeze(2)
                                 ).then_inc(R["ids_set"], 1)
            need_alone(pool, pool_passed, R["ids_set"], a.pair * 2 + 2)
            need_alone(pool, pool_passed, R["place_set"], a.pair + 1)
            need_alone(pool, pool_passed, R["weight_set3"], a.pair + 1)
            for m, t in enumerate((a, b)):
                for k in range(2):
                    pool.indirect_dma_start(
                        sorted_rows, bass.IndirectOffsetOnAxis(ap=place_i[:, a.pair_par, k, m:m + 1], axis=0),
                        row[:, k, t.slot, :], None, bounds_check=ROWS - 1, oob_is_err=False
                    ).then_inc(row_sent[t.slot], 16)

        split_ctx(Tile(0, 0))

        def turn(j, s):
            if Tile(j, s + 1).live and not (isinstance(j, int) and j * SKEW + s + 1 >= NT):
                split_ctx(Tile(j, s + 1))
            if Tile(j, s + 2).live and not (isinstance(j, int) and j * SKEW + s + 2 >= NT):
                ln1(Tile(j, s + 2))
            if Tile(j, s).live:
                qk_rms(Tile(j, s))
                split_weights(Tile(j, s))
            if s % 2 == 1 and Tile(j, s - 7).live:
                a, b = Tile(j, s - 7), Tile(j, s - 6)
                a.pair_par = (s - 7) // 2 % 2
                send(a, b)
            if Tile(j, s - 3).live:
                ln2(Tile(j, s - 3))

        ln1(Tile(0, 0))
        ln1(Tile(0, 1))
        turns_sp(pool, turn)

        def send_y(j, r):
            need_alone(pool, pool_passed, F["y_ready"], j * RING + r + 1)
            pool.indirect_dma_start(
                expert_out, bass.IndirectOffsetOnAxis(ap=hs[:, r, D:D + 1].bitcast(U32), axis=0),
                y_sb[:, r % 4, :], None, bounds_check=2 * T - 1, oob_is_err=False
            ).then_inc(y_sent[r % 4], 16)

        with pool.Fori(0, NSLOT // RING) as j:
            for r in range(RING):
                send_y(j, r)

    @block.scalar
    def _(act):
        def xt_hi(t):
            act.wait_ge(S["x_transposed"], t.n + 1)
            need(act, S["projected"], t.n - 1)
            act.copy(xt_h[:, t.par, :, :], tr_bank[:, 0:D].rearrange("p (c n) -> p c n", c=KC)
                     ).then_inc(S["xt_h_ready"], 1)

        def qkt_hi(t):
            act.wait_ge(S["qk_transposed"], t.n + 1)
            need(act, S["scored"], t.n - 1)
            if t.twins_ok:
                act.wait_ge(k_spread[t.par], t.twins * 16 * 16)
            act.copy(qkt_h[:, t.par, :, :, :], qkt_bank.rearrange("p (a c n) -> p a c n", a=2, c=KC)
                     ).then_inc(S["qkt_h_ready"], 1)

        def row_copy(t):
            act.wait_ge(S["row_ready"], t.n + 1)
            if t.quads_ok:
                act.wait_ge(row_sent[t.slot], t.quad * 32)
            act.copy(row[:, 1, t.slot, 0:D], row[:, 0, t.slot, 0:D]).then_inc(S["row2_ready"], 1)

        def neg_max_rows(t):
            act.wait_ge(S["neg_max_transposed"], t.n + 1)
            need(act, S["scored"], t.n - 1)
            act.copy(neg_max_t[:, t.par, :], mo_bank[0:2 * NH, 0:P // 2].bitcast(BF16)
                     ).then_inc(S["neg_max_t_ready"], 1)

        def v_and_squares(t):
            act.wait_ge(S["projected"], t.n + 1)
            if t.twins_ok:
                act.wait_ge(v_spread[t.par], t.twins * 64)
            else:
                act.wait_ge(dve_setup, SETUP_DVE)
            act.copy(v_sb[:, t.par, :, :, 0:HD],
                     qv_bank[:, D:2 * D].rearrange("p (q g d) -> p q g d", q=2, g=NPAIR)
                     ).then_inc(S["v_ready"], 1)
            need(act, S["q_squared"], t.n)
            need(act, S["qk_veps"], t.n - 1)
            act.activation(square[:, 0, :], qv_bank[:, 0:D], ACT.Square,
                           accum_out=sumsq[:, t.par, 0:1]).then_inc(S["q_squared"], 1)
            need(act, S["k_squared"], t.n)
            act.activation(square[:, 1, :], k_bank[:, 0:D], ACT.Square,
                           accum_out=sumsq[:, t.par, 1:2]).then_inc(S["k_squared"], 1)

        def att_hi(t):
            act.wait_ge(S["att_transposed"], t.n + 1)
            need(act, S["o_projected"], t.n - 1)
            act.copy(at_h[:, t.par, :, :], av_bank[:, 0:D].rearrange("p (c n) -> p c n", c=KC)
                     ).then_inc(S["at_h_ready"], 1)

        def ht_copy(t):
            act.wait_ge(S["h_transposed"], t.n + 1)
            need(act, S["gated"], t.n - 1)
            act.copy(ht[:, t.par, :, :], tr_bank[:, 0:D].rearrange("p (c n) -> p c n", c=KC)
                     ).then_inc(S["ht_ready"], 1)

        def softmax_exp(t):
            act.wait_ge(S["scored"], t.n + 1)
            need(act, S["weighed"], t.n - 1)
            act.activation(probs[:, t.par, :], score_bank, ACT.Exp).then_inc(S["probs_ready"], 1)

        def k_scale(t):
            act.wait_ge(S["qk_rstd"], t.n + 1)
            need(act, S["qk_transposed"], t.n - 1)
            act.activation(kn[:, t.par, :], k_bank[:, 0:D], ACT.Copy, scale=r_qk[:, t.par, 1:2]
                           ).then_inc(S["kn_ready"], 1)

        def gap_exp(pair, pp):
            act.wait_ge(R["gap_ready"], pair + 1)
            act.activation(e_gap[:, pp, :], gap[:, pp, :], ACT.Exp).then_inc(R["e_gap_ready"], 1)

        def turn(j, s):
            def tile(lag):
                t = Tile(j, s - lag)
                static = isinstance(j, int)
                t.twins_ok = not static or t.n >= 2
                t.quads_ok = not static or t.n >= 4
                return t
            if tile(0).live:
                xt_hi(tile(0))
            if tile(1).live:
                qkt_hi(tile(1))
            if tile(4).live:
                row_copy(tile(4))
            if tile(2).live:
                neg_max_rows(tile(2))
            if tile(0).live:
                v_and_squares(tile(0))
            if tile(3).live:
                att_hi(tile(3))
            if tile(4).live:
                ht_copy(tile(4))
            if tile(2).live:
                softmax_exp(tile(2))
            if s % 2 == 0 and tile(6).live:
                gap_exp(tile(6).pair, (s - 6) // 2 % 2)
            if tile(0).live:
                k_scale(tile(0))

        turns_sp(act, turn)

        def hst_hi(m, p):
            act.wait_ge(F["h2_transposed"], m + 1)
            need(act, F["gate_up"], m - 1)
            act.copy(hst_h[:, p, :, :], bank[:, p, 0:D].rearrange("p (c n) -> p c n", c=KC)
                     ).then_inc(F["h2_h_ready"], 1)

        def silu(m, p):
            act.wait_ge(F["gate_up"], m + 1)
            need(act, F["act_ready"], m - 1)
            act.activation(silu_g[:, p, :], bank[:, 2 + p, 0:FI], ACT.Silu).then_inc(F["silu_ready"], 1)

        def au_hi(m, p):
            act.wait_ge(F["act_transposed"], m + 1)
            need(act, F["y_done"], m - 1)
            act.copy(au_h[:, p, 0, :], bank[:, 4 + p, 0:P]).then_inc(F["au_h_ready"], 1)
            act.copy(au_h[0:FB, p, 1, :], bank[0:FB, 4 + p, P:2 * P]).then_inc(F["au_h_ready"], 1)

        def y_copy(m, r, reuse, q):
            act.wait_ge(F["y_done"], m + 1)
            if reuse is not None:
                act.wait_ge(y_sent[r], reuse)
            act.copy(y_sb[:, r, :], bank[:, 6 + q, 0:D]).then_inc(F["y_ready"], 1)

        def turn2(j, r, static):
            i = j * RING + r
            if not static or i < NSLOT:
                hst_hi(i, r % 2)
            if not static or 0 <= i - 1 < NSLOT:
                silu(i - 1, (r - 1) % 2)
            if not static or 0 <= i - 2 < NSLOT:
                au_hi(i - 2, r % 2)
            if not static or 0 <= i - 3 < NSLOT:
                m = i - 3
                turnsback = (j * 2 + (r - 3) // 4) * 16
                y_copy(m, (r - 3) % 4, turnsback if not static or m >= 4 else None, (r - 3) % 2)

        slots(act, turn2)

    @block.vector
    def _(dve):
        done = [0]

        def setup(ins):
            done[0] += 1
            ins.then_inc(dve_setup, 1)

        def after():
            dve.wait_ge(dve_setup, done[0])

        bias_h4 = bias_hl[:, :].rearrange("r (m d) -> r m d", m=4)
        setup(dve.memset(ones_row_f[:, :], 1.0))
        setup(dve.memset(v_sb[:, :, :, :, :], 1.0))
        setup(dve.memset(v_bd[:, :, :, :, :], 0.0))
        setup(dve.memset(k_bd[:, :, :, :, :, :, :].rearrange("p a b c d e f -> p (a b c d e f)").bitcast(F32), 0.0))
        after()
        setup(dve.tensor_copy(ones_row[:, :], ones_row_f[:, :]))
        dve.wait_ge(consts_loaded, 16 * 5)
        setup(dve.tensor_copy(wp_h[:, :, :, :].rearrange("p m c n -> p (m c n)"), wp_f))
        setup(dve.tensor_copy(bias_h4, bias_f))
        dve.wait_ge(pool_setup, SETUP_POOL)
        setup(dve.tensor_scalar(zero_one[:, 0:1], zero_one[:, 1:2], -1.0, 1.0, ALU.mult, ALU.add))
        setup(dve.scalar_tensor_tensor(qk_norm[:, :], qk_norm[:, :], HD ** -0.5, k_norm, ALU.mult, ALU.mult))
        after()
        setup(dve.tensor_tensor(wp_l[:, :, :, :].rearrange("p m c n -> p (m c n)"), wp_f,
                                wp_h[:, :, :, :].rearrange("p m c n -> p (m c n)").bitcast(F32), ALU.subtract))
        setup(dve.tensor_tensor(bias_f, bias_f, bias_h4.bitcast(F32), ALU.subtract))
        after()
        dve.tensor_scalar(bias_f, bias_f, zero_one[:, 1:2], None, ALU.mult).then_inc(plan, 1)
        dve.wait_ge(plan, 1)
        setup(dve.scalar_tensor_tensor(bias_hl[:, :].rearrange("r (m d) -> r m d", m=4), bias_h4.bitcast(F32),
                                       zero_one[:, 0:1], bias_f,
                                       ALU.mult, ALU.add))
        assert done[0] == SETUP_DVE, done[0]

        def ln1_stats(t, loaded):
            if loaded is not None:
                dve.wait_ge(loaded, 16)
            dve.bn_stats(stats[:, t.par, :], x1[:, t.at, :]).then_inc(S["ln1_stats"], 1)
            need(dve, S["xn_ready"], t.n - 1)
            need_alone(dve, dve_passed, S["ln1_stats"], t.n + 1)
            dve.bn_aggr(mean_var[:, t.par, :], stats[:, t.par, :]).then_inc(S["ln1_mean"], 1)

        def ln1_norm(t):
            dve.wait_ge(S["ln1_rstd"], t.n + 1)
            need(dve, S["x_transposed"], t.n - 1)
            dve.tensor_scalar(xn[:, t.par, :], x1[:, t.at, :], mean_var[:, t.par, 0:1], rstd[:, t.par, :],
                              ALU.subtract, ALU.mult).then_inc(S["xn_ready"], 1)

        def xt_lo(t):
            dve.wait_ge(S["xt_h_ready"], t.n + 1)
            need(dve, S["projected"], t.n - 1)
            dve.tensor_tensor(xt_l[:, t.par, :, :], tr_bank[:, 0:D].rearrange("p (c n) -> p c n", c=KC),
                              xt_h[:, t.par, :, :].bitcast(F32), ALU.subtract).then_inc(S["xt_l_ready"], 1)

        def qkt_lo(t):
            dve.wait_ge(S["qkt_h_ready"], t.n + 1)
            need(dve, S["scored"], t.n - 1)
            if t.twins_ok:
                dve.wait_ge(k_spread[t.par], t.twins * 16 * 16)
            v = qkt_bank.rearrange("p (a c n) -> p a c n", a=2, c=KC)
            dve.tensor_tensor(kt_l[:, t.par, :, :], v[:, 1], qkt_h[:, t.par, 1, :, :],
                              ALU.subtract).then_inc(S["kt_l_ready"], 1)
            dve.tensor_tensor(qt_l[:, t.par, :, :], v[:, 0], qkt_h[:, t.par, 0, :, :],
                              ALU.subtract).then_inc(S["qt_l_ready"], 1)

        def find_max(t):
            dve.wait_ge(S["max_scored"], t.n + 1)
            dve.tensor_reduce(row_max[:, t.par, :], score_bank.rearrange("p (h k) -> p h k", h=NH),
                              AX.X, ALU.max).then_inc(S["max_found"], 1)
            dve.wait_ge(S["max_found"], t.n + 1)
            need(dve, S["neg_max_transposed"], t.n - 1)
            dve.tensor_scalar(neg_max[:, t.par, 0:NH], row_max[:, t.par, :], -1.0, None, ALU.mult
                              ).then_inc(S["neg_hi_ready"], 1)
            dve.wait_ge(S["neg_hi_ready"], t.n + 1)
            dve.scalar_tensor_tensor(neg_max[:, t.par, NH:2 * NH], row_max[:, t.par, :], -1.0,
                                     neg_max[:, t.par, 0:NH], ALU.mult, ALU.subtract
                                     ).then_inc(S["neg_max_ready"], 1)

        def normalise(t):
            dve.wait_ge(S["weighed"], t.n + 1)
            v = av_bank[:, 0:NH * VW].rearrange("p (h d) -> p h d", h=NH)
            dve.reciprocal(r_sum[:, t.par, :], v[:, :, HD:VW].rearrange("p h d -> p (h d)")).then_inc(S["sum_inverted"], 1)
            dve.wait_ge(S["sum_inverted"], t.n + 1)
            need(dve, S["att_transposed"], t.n - 1)
            dve.tensor_tensor(att[:, t.par, :, :], v[:, :, 0:HD],
                              r_sum[:, t.par, :].unsqueeze(2).to_broadcast([P, NH, HD]), ALU.mult
                              ).then_inc(S["att_ready"], 1)

        def att_lo(t):
            dve.wait_ge(S["at_h_ready"], t.n + 1)
            need(dve, S["o_projected"], t.n - 1)
            dve.tensor_tensor(at_l[:, t.par, :, :], av_bank[:, 0:D].rearrange("p (c n) -> p c n", c=KC),
                              at_h[:, t.par, :, :].bitcast(F32), ALU.subtract).then_inc(S["at_l_ready"], 1)

        def q_scale(t):
            dve.wait_ge(S["qk_rstd"], t.n + 1)
            need(dve, S["qk_transposed"], t.n - 1)
            dve.scalar_tensor_tensor(qn[:, t.par, :], qv_bank[:, 0:D], r_qk[:, t.par, 0:1], qk_norm[:, :],
                                     ALU.mult, ALU.mult).then_inc(S["qn_ready"], 1)

        def residual(t):
            dve.wait_ge(S["o_projected"], t.n + 1)
            dve.tensor_tensor(x1[:, t.at, :], mo_bank[:, 0:D], x1[:, t.at, :], ALU.add).then_inc(S["x1_ready"], 1)
            need_alone(dve, dve_passed, S["x1_ready"], t.n + 1)
            dve.bn_stats(stats2[:, t.par, :], x1[:, t.at, :]).then_inc(S["ln2_stats"], 1)
            need(dve, S["row_ready"], t.n - 1)
            need_alone(dve, dve_passed, S["ln2_stats"], t.n + 1)
            dve.bn_aggr(mean_var2[:, t.par, :], stats2[:, t.par, :]).then_inc(S["ln2_mean"], 1)

        def ln2_norm(t):
            dve.wait_ge(S["ln2_rstd"], t.n + 1)
            if t.quads_ok:
                dve.wait_ge(row_sent[t.slot], t.quad * 32)
            dve.tensor_scalar(row[:, 0, t.slot, 0:D], x1[:, t.at, :], mean_var2[:, t.par, 0:1], rstd2[:, t.par, :],
                              ALU.subtract, ALU.mult).then_inc(S["row_ready"], 1)

        def logits_copy(t):
            dve.wait_ge(S["gated"], t.n + 1)
            dve.tensor_copy(logit[:, t.par, :], qkt_bank[:, 0:NE]).then_inc(S["logit_ready"], 1)

        def choose(a, b, pp):
            need_alone(dve, dve_passed, S["logit_ready"], b.n + 1)
            for m in range(2):
                dve.max(top8[:, m, :], logit[:, m, :]).then_inc(R["tops"], 1)
            need_alone(dve, dve_passed, R["tops"], (a.pair + 1) * 2)
            for m in range(2):
                dve.max_index(top8_no[:, m, :], top8[:, m, :], logit[:, m, :]).then_inc(R["no_ready"], 1)
            dve.tensor_tensor(gap[:, pp, :], top8[:, :, 1], top8[:, :, 0], ALU.subtract).then_inc(R["gap_ready"], 1)
            dve.wait_ge(R["no_ready"], a.pair * 3 + 2)
            dve.tensor_copy(top_no[:, :, :], top8_no[:, :, 0:2]).then_inc(R["no_ready"], 1)
            dve.wait_ge(R["no_ready"], a.pair * 3 + 3)
            for k in range(2):
                dve.tensor_tensor(chosen[:, pp, k, :, :], expert_no[:, :].unsqueeze(1).to_broadcast([P, 2, NE]),
                                  top_no[:, :, k:k + 1].to_broadcast([P, 2, NE]), ALU.is_equal
                                  ).then_inc(R["choice_ready"], 1)
            dve.wait_ge(R["choice_ready"], a.pair * 3 + 2)
            dve.tensor_tensor(chosen_b[:, pp, :, :], chosen[:, pp, 0, :, :], chosen[:, pp, 1, :, :], ALU.add
                              ).then_inc(R["choice_ready"], 1)

        def route(a, b, pp):
            dve.wait_ge(R["routed"], a.pair + 1)
            dve.tensor_tensor(place[:, :, :], qkt_bank[:, 0:2 * NE].rearrange("p (m e) -> p m e", m=2),
                              filled[:, :].unsqueeze(1).to_broadcast([P, 2, NE]), ALU.add
                              ).then_inc(R["place_ready"], 1)
            dve.wait_ge(R["place_ready"], a.pair + 1)
            dve.tensor_tensor(filled[:, :], filled[:, :], qkt_bank[:, 2 * NE:3 * NE], ALU.add
                              ).then_inc(R["filled_new"], 1)
            dve.tensor_tensor(place_of[:, :, :, :], chosen[:, pp, :, :, :],
                              place[:, :, :].unsqueeze(1).to_broadcast([P, 2, 2, NE]), ALU.mult
                              ).then_inc(R["place_sel"], 1)
            dve.wait_ge(R["place_sel"], a.pair + 1)
            dve.tensor_reduce(place_f[:, :, :], place_of[:, :, :, :], AX.X, ALU.add).then_inc(R["place_sum"], 1)
            dve.wait_ge(R["place_sum"], a.pair + 1)
            if a.sent is not None:
                dve.wait_ge(row_sent[a.slot], a.sent)
                dve.wait_ge(row_sent[b.slot], a.sent)
            dve.tensor_copy(place_i[:, pp, :, :], place_f[:, :, :]).then_inc(R["place_set"], 1)
            dve.wait_ge(R["e_gap_ready"], a.pair + 1)
            dve.tensor_scalar(one_e[:, :], e_gap[:, pp, :], 1.0, None, ALU.add).then_inc(R["weight_set1"], 1)
            dve.wait_ge(R["weight_set1"], a.pair + 1)
            w = row[:, :, a.slot:a.slot + 2, D + 1:D + 2].rearrange("p k m d -> p k (m d)")
            dve.reciprocal(w[:, 0, :], one_e[:, :]).then_inc(R["weight_set2"], 1)
            dve.wait_ge(R["weight_set2"], a.pair + 1)
            dve.tensor_tensor(w[:, 1, :], e_gap[:, pp, :], w[:, 0, :], ALU.mult).then_inc(R["weight_set3"], 1)

        def turn(j, s):
            def tile(lag):
                t = Tile(j, s - lag)
                static = isinstance(j, int)
                t.twins_ok = not static or t.n >= 2
                t.quads_ok = not static or t.n >= 4
                t.at = t.n if static else bass.ds(t.n, 1)
                t.sent = t.quad * 32 if t.quads_ok else None
                return t
            if tile(4).live:
                ln2_norm(tile(4))
            if s % 2 == 1 and tile(7).live:
                route(tile(7), tile(6), (s - 7) // 2 % 2)
            if tile(0).live:
                xt_lo(tile(0))
            if tile(1).live:
                qkt_lo(tile(1))
            if tile(2).live:
                find_max(tile(2))
            if tile(-2).live and not (isinstance(j, int) and j * SKEW + s + 2 >= NT):
                n = j * SKEW + s + 2 if isinstance(j, int) else None
                ln1_stats(tile(-2), {2: x_second, 8: x_rest}.get(n))
            if tile(3).live:
                normalise(tile(3))
            if tile(-1).live and not (isinstance(j, int) and j * SKEW + s + 1 >= NT):
                ln1_norm(tile(-1))
            if tile(3).live:
                att_lo(tile(3))
            if tile(0).live:
                q_scale(tile(0))
            if tile(4).live:
                logits_copy(tile(4))
            if s % 2 == 1 and tile(5).live:
                choose(tile(5), tile(4), (s - 5) // 2 % 2)
            if tile(3).live:
                residual(tile(3))

        for n in range(2):
            t = Tile(0, n)
            t.at = n
            ln1_stats(t, x_first)
        t = Tile(0, 0)
        t.at = 0
        ln1_norm(t)
        turns_sp(dve, turn)

        steps = [1]

        def step(ins):
            steps[0] += 1
            ins.then_inc(plan, 1)
            dve.wait_ge(plan, steps[0])

        dve.wait_ge(R["filled_new"], NT // 2)
        step(dve.tensor_tensor(count[:, :], filled[0:1, :], region_no[:, :], ALU.subtract))
        step(dve.tensor_scalar(count[:, :], count[:, :], float(P - 1), None, ALU.add))
        step(dve.tensor_copy(count_i[:, :], count[:, :]))
        step(dve.tensor_copy(pad_at[:, :], filled[0:1, :]))
        step(dve.tensor_scalar(tiles_i[:, :], count_i[:, :], 7, None, ALU.arith_shift_right))
        step(dve.tensor_copy(tiles[:, :], tiles_i[:, :]))
        step(dve.tensor_copy(cum[:, 0, :], tiles[:, :]))
        for n, d in enumerate((1, 2, 4)):
            step(dve.tensor_copy(cum[:, n + 1, 0:d], cum[:, n, 0:d]))
            step(dve.tensor_tensor(cum[:, n + 1, d:NE], cum[:, n, d:NE], cum[:, n, 0:NE - d], ALU.add))
        step(dve.tensor_tensor(past[:, :, :], slot_no[:, :].unsqueeze(2).to_broadcast([1, NSLOT, NE]),
                               cum[:, 3, :].unsqueeze(1).to_broadcast([1, NSLOT, NE]), ALU.is_ge))
        step(dve.tensor_tensor(past_n[:, :, :], past[:, :, :],
                               tiles[:, :].unsqueeze(1).to_broadcast([1, NSLOT, NE]), ALU.mult))
        step(dve.tensor_reduce(slot_e[:, 0, :], past[:, :, :], AX.X, ALU.add))
        step(dve.tensor_reduce(slot_e[:, 1, :], past_n[:, :, :], AX.X, ALU.add))
        step(dve.tensor_tensor(slot_e[:, 2, :], slot_no[:, :], slot_e[:, 1, :], ALU.subtract))
        step(dve.tensor_scalar(slot_e[:, 3, :], slot_e[:, 0, :], float(REG), None, ALU.mult))
        step(dve.scalar_tensor_tensor(slot_e[:, 1, :], slot_e[:, 2, :], float(P), slot_e[:, 3, :], ALU.mult, ALU.add))
        step(dve.tensor_scalar(slot_row[:, :], slot_e[:, 1, :], float(NE * REG), None, ALU.min))
        step(dve.tensor_scalar(slot_w[:, :], slot_e[:, 0, :], float(NE - 1), float(EW), ALU.min, ALU.mult))
        assert steps[0] == PLAN, steps[0]

        def hst_lo(m, p):
            dve.wait_ge(F["h2_h_ready"], m + 1)
            need(dve, F["gate_up"], m - 1)
            dve.tensor_tensor(hst_l[:, p, :, :], bank[:, p, 0:D].rearrange("p (c n) -> p c n", c=KC),
                              hst_h[:, p, :, :].bitcast(F32), ALU.subtract).then_inc(F["h2_l_ready"], 1)

        def gate_mult(m, p, r):
            dve.wait_ge(F["silu_ready"], m + 1)
            need(dve, F["act_transposed"], m - 1)
            dve.scalar_tensor_tensor(act_u[:, p, :], silu_g[:, p, :], hs[:, r, D + 1:D + 2], bank[:, 2 + p, FI:2 * FI],
                                     ALU.mult, ALU.mult).then_inc(F["act_ready"], 1)

        def au_lo(m, p):
            dve.wait_ge(F["au_h_ready"], m * 2 + 2)
            need(dve, F["y_done"], m - 1)
            dve.tensor_tensor(au_l[:, p, 0, :], bank[:, 4 + p, 0:P], au_h[:, p, 0, :].bitcast(F32),
                              ALU.subtract).then_inc(F["au_l_ready"], 1)
            dve.tensor_tensor(au_l[0:FB, p, 1, :], bank[0:FB, 4 + p, P:2 * P], au_h[0:FB, p, 1, :].bitcast(F32),
                              ALU.subtract).then_inc(F["au_l_ready"], 1)

        def turn2(j, r, static):
            i = j * RING + r
            if not static or i < NSLOT:
                hst_lo(i, r % 2)
            if not static or 0 <= i - 1 < NSLOT:
                gate_mult(i - 1, (r - 1) % 2, (r - 1) % RING)
            if not static or 0 <= i - 2 < NSLOT:
                au_lo(i - 2, r % 2)

        slots(dve, turn2)

        for g in range(NT // 2):
            dve.wait_ge(fin_loaded[g % 4], 32 * (g // 4 + 1))
            v = fin_in[:, g % 4, 0, :, :]
            dve.tensor_tensor(v, v, fin_in[:, g % 4, 1, :, :], ALU.add).then_inc(fin_sum1, 1)
            dve.wait_ge(fin_sum1, g + 1)
            dve.tensor_tensor(v, v, x1[:, 2 * g:2 * g + 2, :], ALU.add).then_inc(fin_sum2, 1)

    @block.tensor
    def _(pe):
        pe.wait_ge(pool_setup, SETUP_POOL)
        pe.wait_ge(dve_setup, SETUP_DVE)
        QM, KM, VM, OM = range(4)

        def three(dst, a_h, a_l, b_h, b_l, start, stop):
            pe.matmul(dst, a_h, b_h, start=start, stop=False)
            pe.matmul(dst, a_h, b_l, start=False, stop=False)
            return pe.matmul(dst, a_l, b_h, start=False, stop=stop)

        def project(dst, a_h, a_l, m):
            for c in range(KC):
                three(dst, a_h[:, c, :], a_l[:, c, :], wp_h[:, m, c, :], wp_l[:, m, c, :], c == 0, False)
            return pe.matmul(dst, ones_row[:, :], bias_hl[:, m * D:(m + 1) * D], start=False, stop=True)

        def tr_x(t):
            pe.wait_ge(S["xn_ready"], t.n + 1)
            need(pe, S["xt_l_ready"], t.n)
            need(pe, S["ht_ready"], t.n - 4)
            for c in range(KC):
                ins = pe.transpose(tr_bank[:, c * P:(c + 1) * P], xn[:, t.par, c * P:(c + 1) * P], ident[:, :])
            ins.then_inc(S["x_transposed"], 1)

        def tr_qk(t):
            pe.wait_ge(S["qn_ready"], t.n + 1)
            pe.wait_ge(S["kn_ready"], t.n + 1)
            need(pe, S["qt_l_ready"], t.n)
            need(pe, S["logit_ready"], t.n - 3)
            if t.route_read is not None:
                need(pe, R["filled_new"], t.route_read)
            for a, src in enumerate((qn, kn)):
                for c in range(KC):
                    at = (a * KC + c) * P
                    ins = pe.transpose(qkt_bank[:, at:at + P], src[:, t.par, c * P:(c + 1) * P], ident[:, :])
            ins.then_inc(S["qk_transposed"], 1)

        def score_max(t):
            pe.wait_ge(k_spread[t.par], (t.twins + 1) * 16 * 16)
            pe.wait_ge(S["qkt_h_ready"], t.n + 1)
            need(pe, S["probs_ready"], t.n)
            for c in range(KC):
                for b in range(NB):
                    ins = pe.matmul(score_bank[b * L:(b + 1) * L, c * 512:(c + 1) * 512],
                                    qkt_h[:, t.par, 0, c, b * L:(b + 1) * L],
                                    k_bd[:, t.par, 0, c, b, :, :].rearrange("p h l -> p (h l)"), start=True, stop=True)
            ins.then_inc(S["max_scored"], 1)

        def weigh(t):
            pe.wait_ge(S["probs_ready"], t.n + 1)
            pe.wait_ge(v_spread[t.par], (t.twins + 1) * 64)
            need(pe, S["at_l_ready"], t.n)
            for b in range(NB):
                for g in range(NPAIR):
                    at = (b * NPAIR + g) * L
                    ins = pe.matmul(av_bank[b * L:(b + 1) * L, g * 2 * VW:(g + 1) * 2 * VW],
                                    probs[:, t.par, at:at + L],
                                    v_bd[:, t.par, b, :, g * VW:(g + 1) * VW], start=True, stop=True)
            ins.then_inc(S["weighed"], 1)

        def project_qkv(t):
            pe.wait_ge(S["xt_h_ready"], t.n + 1)
            pe.wait_ge(S["xt_l_ready"], t.n + 1)
            pe.wait_ge(S["ct_ready"], t.n + 1)
            need(pe, S["qn_ready"], t.n)
            need(pe, S["kn_ready"], t.n)
            project(qv_bank[:, 0:D], xt_h[:, t.par], xt_l[:, t.par], QM)
            project(k_bank[:, 0:D], ct_h[:, t.par], ct_l[:, t.par], KM)
            project(qv_bank[:, D:2 * D], ct_h[:, t.par], ct_l[:, t.par], VM).then_inc(S["projected"], 1)

        def tr_max(t):
            pe.wait_ge(S["neg_max_ready"], t.n + 1)
            need(pe, S["x1_ready"], t.n - 1)
            pe.transpose(mo_bank[0:2 * NH, 0:P // 2].bitcast(BF16), neg_max[:, t.par, :], ident_b[:, :]
                         ).then_inc(S["neg_max_transposed"], 1)

        def tr_att(t):
            pe.wait_ge(S["att_ready"], t.n + 1)
            for c in range(KC):
                ins = pe.transpose(av_bank[:, c * P:(c + 1) * P],
                                   att[:, t.par, c * 8:(c + 1) * 8, :].rearrange("p h d -> p (h d)"), ident[:, :])
            ins.then_inc(S["att_transposed"], 1)

        def tr_h(t):
            pe.wait_ge(S["row_ready"], t.n + 1)
            if t.xt_read is not None:
                pe.wait_ge(S["xt_l_ready"], t.xt_read)
            need(pe, S["ht_ready"], t.n)
            for c in range(KC):
                ins = pe.transpose(tr_bank[:, c * P:(c + 1) * P], row[:, 0, t.slot, c * P:(c + 1) * P], ident[:, :])
            ins.then_inc(S["h_transposed"], 1)

        def score(t):
            pe.wait_ge(S["neg_max_t_ready"], t.n + 1)
            pe.wait_ge(S["qt_l_ready"], t.n + 1)
            pe.wait_ge(S["max_found"], t.n + 1)
            for b in range(NB):
                for g in range(NPAIR):
                    c, h = g // 4, 2 * (g % 4)
                    dst = score_bank[:, (b * NPAIR + g) * L:(b * NPAIR + g + 1) * L]
                    k_h, k_l = (k_bd[:, t.par, n, c, b, h:h + 2, :].rearrange("p h l -> p (h l)") for n in range(2))
                    seq = slice(b * L, (b + 1) * L)
                    pe.matmul(dst, k_h, qkt_h[:, t.par, 0, c, seq], start=True, stop=False)
                    pe.matmul(dst, k_h, qt_l[:, t.par, c, seq], start=False, stop=False)
                    pe.matmul(dst, k_l, qkt_h[:, t.par, 0, c, seq], start=False, stop=False)
                    ins = pe.matmul(dst, head_of[:, g, :], neg_max_t[:, t.par, seq], start=False, stop=True)
            ins.then_inc(S["scored"], 1)

        def gate(t):
            pe.wait_ge(S["ht_ready"], t.n + 1)
            if t.qkt_read is not None:
                pe.wait_ge(S["qt_l_ready"], t.qkt_read)
            need(pe, S["logit_ready"], t.n)
            for half in range(2):
                rows = slice(half * 64, half * 64 + 64)
                for c in range(KC):
                    ins = pe.matmul(qkt_bank[rows, 0:NE], ht[:, t.par, c, rows], gate_w[:, c, :],
                                    start=(c == 0), stop=(c == KC - 1))
            ins.then_inc(S["gated"], 1)

        def project_out(t):
            pe.wait_ge(S["at_h_ready"], t.n + 1)
            pe.wait_ge(S["at_l_ready"], t.n + 1)
            if t.max_read is not None:
                pe.wait_ge(S["neg_max_t_ready"], t.max_read)
            project(mo_bank[:, 0:D], at_h[:, t.par], at_l[:, t.par], OM).then_inc(S["o_projected"], 1)

        def count_rows(pair, pp, logits_read):
            pe.wait_ge(R["choice_ready"], pair * 3 + 3)
            pe.wait_ge(S["logit_ready"], logits_read)
            a, b = chosen_b[:, pp, 0, :], chosen_b[:, pp, 1, :]
            c = qkt_bank
            pe.matmul(c[:, 0:NE], below[:, :], a, start=True, stop=True)
            pe.matmul(c[:, NE:2 * NE], below[:, :], b, start=True, stop=False)
            pe.matmul(c[:, NE:2 * NE], ones_b[:, :], a, start=False, stop=True)
            pe.matmul(c[:, 2 * NE:3 * NE], ones_b[:, :], a, start=True, stop=False)
            pe.matmul(c[:, 2 * NE:3 * NE], ones_b[:, :], b, start=False, stop=True).then_inc(R["routed"], 1)

        def turn(j, s):
            static = isinstance(j, int)
            i = j * SKEW + s

            def tile(lag):
                return Tile(j, s - lag)

            def seen(value):
                return min(value, NT) if static else value

            if tile(0).live:
                tr_x(tile(0))
            if tile(1).live:
                t = tile(1)
                t.route_read = (j * 2 + (s - 7) // 2 + 1) if s % 2 == 1 and (not static or i >= 7) else None
                tr_qk(t)
            if tile(2).live:
                score_max(tile(2))
            if tile(3).live:
                weigh(tile(3))
            if tile(0).live:
                project_qkv(tile(0))
            if tile(2).live:
                tr_max(tile(2))
            if tile(3).live:
                tr_att(tile(3))
            if tile(4).live:
                t = tile(4)
                t.xt_read = seen(i + 1)
                tr_h(t)
            if tile(2).live:
                score(tile(2))
            if tile(4).live:
                t = tile(4)
                t.qkt_read = seen(i)
                if s % 2 == 1 and (not static or i >= 7):
                    pe.wait_ge(R["filled_new"], j * 2 + (s - 7) // 2 + 1)
                gate(t)
            if tile(3).live:
                t = tile(3)
                t.max_read = seen(i - 1)
                project_out(t)
            if s % 2 == 0 and tile(6).live:
                count_rows(tile(6).pair, (s - 6) // 2 % 2, seen(i - 3))

        turns_sp(pe, turn)

        def tr_hs(m, p, j, r):
            pe.wait_ge(hs_loaded[r], (j + 1) * 16)
            need(pe, F["h2_l_ready"], m - 1)
            for c in range(KC):
                ins = pe.transpose(bank[:, p, c * P:(c + 1) * P], hs[:, r, c * P:(c + 1) * P], ident[:, :])
            ins.then_inc(F["h2_transposed"], 1)

        def gate_up(m, p):
            pe.wait_ge(F["h2_h_ready"], m + 1)
            pe.wait_ge(F["h2_l_ready"], m + 1)
            need_alone(pe, pe_passed, F["act_ready"], m - 1)
            w = pe.value_load(slot_w[0:1, bass.ds(m, 1)], min_val=0, max_val=(NE - 1) * EW)
            for c in range(KC):
                cols = bass.ds(w + c * 2 * FI, 2 * FI)
                ins = three(bank[:, 2 + p, 0:2 * FI], hst_h[:, p, c, :], hst_l[:, p, c, :], we_h[:, cols], we_l[:, cols],
                            c == 0, c == KC - 1)
            ins.then_inc(F["gate_up"], 1)

        def tr_act(m, p):
            pe.wait_ge(F["act_ready"], m + 1)
            need(pe, F["au_l_ready"], m * 2 - 2)
            pe.transpose(bank[:, 4 + p, 0:P], act_u[:, p, 0:FA], ident[:, :])
            pe.transpose(bank[0:FB, 4 + p, P:2 * P], act_u[:, p, FA:FI], ident[:, :]).then_inc(F["act_transposed"], 1)

        def down(m, p):
            pe.wait_ge(F["au_h_ready"], m * 2 + 2)
            pe.wait_ge(F["au_l_ready"], m * 2 + 2)
            need_alone(pe, pe_passed, F["y_ready"], m - 1)
            w = pe.value_load(slot_w[0:1, bass.ds(m, 1)], min_val=0, max_val=(NE - 1) * EW)
            for n, rows in enumerate((FA, FB)):
                cols = bass.ds(w + 2 * KC * FI + n * D, D)
                ins = three(bank[:, 6 + p, 0:D], au_h[0:rows, p, n, :], au_l[0:rows, p, n, :], we_h[0:rows, cols],
                            we_l[0:rows, cols], n == 0, n == 1)
            ins.then_inc(F["y_done"], 1)

        pe.wait_ge(plan, PLAN)
        pe.wait_ge(S["we_ready"], NT)
        pe.wait_ge(S["ht_ready"], NT)
        pe.wait_ge(R["filled_new"], NT // 2)

        def turn2(j, r, static):
            i = j * RING + r
            if not static or i < NSLOT:
                tr_hs(i, r % 2, j, r)
            if not static or 0 <= i - 2 < NSLOT:
                tr_act(i - 2, r % 2)
            if not static or 0 <= i - 1 < NSLOT:
                gate_up(i - 1, (r - 1) % 2)
            if not static or 0 <= i - 3 < NSLOT:
                down(i - 3, (r - 3) % 2)

        slots(pe, turn2)


PLAN = 23


def turns_sp(eng, turn):
    first, last = 2, NT // SKEW - 1
    for j in range(first):
        for s in range(SKEW):
            turn(j, s)
    with eng.Fori(first, last) as j:
        for s in range(SKEW):
            turn(j, s)
    for i in range(last * SKEW, LAST):
        turn(i // SKEW, i % SKEW)


def slots(eng, turn):
    for r in range(RING):
        turn(0, r, True)
    with eng.Fori(1, NSLOT // RING) as j:
        for r in range(RING):
            turn(j, r, False)
    for r in range(3):
        turn(NSLOT // RING, r, True)


def kernel(**inputs):
    import concourse.bacc as bacc
    from concourse.bass_utils import run_bass_kernel_spmd

    def get(name):
        return np.ascontiguousarray(inputs[name])

    def weight(name):
        return get(name).T.reshape(KC, P, D).transpose(1, 0, 2)

    v_order = np.arange(D).reshape(NPAIR, 2, HD).transpose(1, 0, 2).reshape(D)
    w_v = weight("L0_xattn_v_img_w")[:, :, v_order]
    w_proj = np.stack([weight("L0_xattn_q_w"), weight("L0_xattn_k_img_w"), w_v, weight("L0_xattn_o_w")], 1)
    bias = np.concatenate([get("L0_xattn_q_b"), get("L0_xattn_k_img_b"), get("L0_xattn_v_img_b")[v_order],
                           get("L0_xattn_o_b")])
    w1 = get("L0_ffn_w1").reshape(NE, 2 * FI, KC, P).transpose(3, 0, 2, 1).reshape(P, NE, KC * 2 * FI)
    w2 = get("L0_ffn_w2").transpose(2, 0, 1)
    w2b = np.zeros((P, NE, D), w2.dtype)
    w2b[:FB] = w2[FA:]
    w_exp = np.concatenate([w1, w2[:FA], w2b], 2).reshape(P, NT, WS).transpose(1, 0, 2).reshape(NT * P, WS)
    ctx_t = get("ctx_2048").reshape(NT, P, KC, P).transpose(0, 3, 2, 1).reshape(NT * P, KC * P)
    w_gate = get("L0_ffn_gate_w").T.reshape(KC, P, NE).transpose(1, 0, 2).reshape(P, KC * NE)
    arrays = {
        "x": get("x").reshape(T, D),
        "ctx_t": ctx_t,
        "w_proj": w_proj.reshape(P, 4 * KC * D),
        "w_exp": w_exp,
        "w_gate": w_gate,
        "bias": np.stack([bias, bias]),
        "norm_q": get("L0_xattn_norm_q_w"),
        "norm_k": get("L0_xattn_norm_k_img_w"),
    }
    arrays = {n: np.ascontiguousarray(a) for n, a in arrays.items()}
    nc = bacc.Bacc("TRN2", target_bir_lowering=False, num_devices=1)
    args = [nc.dram_tensor(n, a.shape, mybir.dt.from_np(a.dtype), kind="ExternalInput").ap()
            for n, a in arrays.items()]
    out = nc.dram_tensor("out", (T, D), F32, kind="ExternalOutput").ap()
    build(nc, *args, out)
    r = run_bass_kernel_spmd(nc, [arrays], core_ids=[0])
    return r.results[0]["out"].reshape(B, L, D)
```

```python
from contextlib import ExitStack

import numpy as np

import concourse.bass as bass
from concourse import mybir

ALU = mybir.AluOpType
ACT = mybir.ActivationFunctionType
AX = mybir.AxisListType
F32 = mybir.dt.float32
F32R = mybir.dt.float32r
F16 = mybir.dt.float16
BF16 = mybir.dt.bfloat16
I32 = mybir.dt.int32
U32 = mybir.dt.uint32

P = 128
B, L, D = 64, 64, 256
NH, HD = 16, 16
NE, FI = 8, 176
KC = D // P
NB = P // L
T = B * L
NT = T // P
NPAIR = NH // 2
NQ = NPAIR // KC
QC = P + 2 * HD
QN = NPAIR * QC
KX = D + HD
VW = HD + 1
IMG_LEN = 257
assert L <= IMG_LEN

REG = T + P
ROWS = NE * REG + P
ROW = D + 2
NSLOT = 72
RING = 8
assert NSLOT * P >= 2 * T + NE * (P - 1) - P + 1 and NSLOT % RING == 0
EW = 2 * KC * FI + 2 * D
FA, FB = P, FI - P
WS = NE * EW // NT
assert WS * NT == NE * EW

SKEW = 4
LAST = NT + 7


class Tile:

    def __init__(self, j, s):
        self.n = j * SKEW + s
        self.slot = s % SKEW
        self.par = s % 2
        self.quad = j + s // SKEW
        self.pair = j * 2 + s // 2
        self.live = not isinstance(j, int) or 0 <= self.n < NT
        self.twins = j * 2 + s // 2


def need(eng, sem, value):
    if isinstance(value, int) and value <= 0:
        return
    eng.wait_ge(sem, value)


def need_alone(eng, passed, sem, value):
    need(eng, sem, value)
    if not isinstance(value, int):
        eng.sem_inc(passed, 1)


def build(nc, x, ctx_t, w_proj, w_exp, w_gate, bias, norm_q, norm_k, out):
    sorted_rows = nc.dram_tensor("sorted_rows", (ROWS, ROW), F32, kind="Internal").ap()
    expert_out = nc.dram_tensor("expert_out", (2 * T, D), F32, kind="Internal").ap()
    with ExitStack() as stack:
        build_in(nc, stack, x, ctx_t, w_proj, w_exp, w_gate, bias, norm_q, norm_k, out,
                 sorted_rows, expert_out)


def build_in(nc, stack, x, ctx_t, w_proj, w_exp, w_gate, bias, norm_q, norm_k, out,
             sorted_rows, expert_out):
    def sb(name, shape, dt):
        return stack.enter_context(nc.sbuf_tensor(name, shape, dt))

    def sem(name):
        return stack.enter_context(nc.semaphore(name))

    bank = stack.enter_context(nc.psum_tensor("bank", [P, 8, 512], F32))

    ident = sb("ident", [P, P], F32)
    ident_b = sb("ident_b", [P, P], BF16)
    below = sb("below", [P, P], BF16)
    ones_b = sb("ones_b", [P, P], BF16)
    head_of = sb("head_of", [32, NPAIR, P], BF16)
    expert_no = sb("expert_no", [P, NE], F32)
    slot_no = sb("slot_no", [1, NSLOT], F32)
    result_row = sb("result_row", [P, 2, NT], I32)
    half_neg = sb("half_neg", [P, 2], F32)
    one_neg = sb("one_neg", [P, 2], F32)
    zero_one = sb("zero_one", [2, 2], F32)
    ones_row_f = sb("ones_row_f", [2, P], F32)
    ones_row = sb("ones_row", [2, P], F32R)
    bias_hl = sb("bias_hl", [2, 4 * D], F32R)
    wp_h = sb("wp_h", [P, 4, KC, D], F32R)
    wp_l = sb("wp_l", [P, 4, KC, D], F32R)
    gate_w = sb("gate_w", [P, KC, NE], F32)
    qk_norm = sb("qk_norm", [P, D], F32)
    we_f = sb("we_f", [P, 2, WS], F32)
    we_h = sb("we_h", [P, NE * EW], F32R)
    we_l = sb("we_l", [P, NE * EW], F32R)

    x1 = sb("x1", [P, NT, D], F32)
    ctx_in = sb("ctx_in", [P, 2, KC * P], F32)
    stats = sb("stats", [P, 2, 6], F32)
    mean_var = sb("mean_var", [P, 2, 2], F32)
    veps = sb("veps", [P, 2, 1], F32)
    rstd = sb("rstd", [P, 2, 1], F32)
    shift = sb("shift", [P, 2, 1], F32)
    xn = sb("xn", [P, 2, D], F32)
    xt_h = sb("xt_h", [P, 2, KC, P], F32R)
    xt_l = sb("xt_l", [P, 2, KC, P], F32R)
    ct_h = sb("ct_h", [P, 2, KC, P], F32R)
    ct_l = sb("ct_l", [P, 2, KC, P], F32R)
    square = sb("square", [P, 2, D], BF16)
    sumsq = sb("sumsq", [P, 2, 2], F32)
    ms_eps = sb("ms_eps", [P, 2, 2], F32)
    r_qk = sb("r_qk", [P, 2, 2], F32)
    v_sb = sb("v_sb", [P, 2, 2, NPAIR, VW], F32)
    v_bd = sb("v_bd", [P, 2, NB, 2, NPAIR * VW], F32)
    qp_h = sb("qp_h", [P, 2, NB, KC, NQ, L], F16)
    qp_l = sb("qp_l", [P, 2, NB, KC, NQ, L], F16)
    late = sb("late", [P, 4096], F32)
    qn = late[:, 0:QN]
    kn = late[:, QN:QN + 2 * 2 * KX].rearrange("p (b x) -> p b x", b=2)
    kp = late[:, QN + 4 * KX:QN + 4 * KX + 4 * 2 * P].bitcast(F16).rearrange(
        "p (u n b c q l) -> p u n b c q l", u=2, n=2, b=NB, c=KC, q=2)
    row_max = sb("row_max", [P, 2, NH], F32)
    neg_max = sb("neg_max", [P, 2, 2 * NH], BF16)
    neg_max_t = sb("neg_max_t", [2 * NH, 2, P], BF16)
    probs = sb("probs", [P, 2, NB * NPAIR * L], F32)
    wp_f = probs[:, :, :].rearrange("p a b -> p (a b)")
    r_sum = sb("r_sum", [P, 2, NH], F32)
    att = sb("att", [P, 2, NH, HD], F32)
    at_h = sb("at_h", [P, 2, KC, P], F32R)
    at_l = sb("at_l", [P, 2, KC, P], F32R)
    stats2 = sb("stats2", [P, 2, 6], F32)
    mean_var2 = sb("mean_var2", [P, 2, 2], F32)
    veps2 = sb("veps2", [P, 2, 1], F32)
    rstd2 = sb("rstd2", [P, 2, 1], F32)
    row = sb("row", [P, 2, SKEW, ROW], F32)
    ht = sb("ht", [P, 2, KC, P], F32)
    logit = sb("logit", [P, 2, NE], F32)
    top8 = sb("top8", [P, 2, 8], F32)
    top8_no = sb("top8_no", [P, 2, 8], U32)
    top_no = sb("top_no", [P, 2, 2], F32)
    gap = sb("gap", [P, 2, 2], F32)
    e_gap = sb("e_gap", [P, 2, 2], F32)
    one_e = sb("one_e", [P, 2], F32)
    chosen = sb("chosen", [P, 2, 2, 2, NE], F32)
    chosen_b = sb("chosen_b", [P, 2, 2, NE], BF16)
    counts = sb("counts", [P, 3 * NE], F32)
    filled = sb("filled", [P, NE], F32)
    place = sb("place", [P, 2, NE], F32)
    place_of = sb("place_of", [P, 2, 2, NE], F32)
    place_f = sb("place_f", [P, 2, 2], F32)
    place_i = sb("place_i", [P, 2, 2, 2], I32)

    pad_rows = sb("pad_rows", [P, ROW], F32)
    region_no = sb("region_no", [1, NE], F32)
    count = sb("count", [1, NE], F32)
    count_i = sb("count_i", [1, NE], I32)
    tiles_i = sb("tiles_i", [1, NE], I32)
    tiles = sb("tiles", [1, NE], F32)
    cum = sb("cum", [1, 4, NE], F32)
    tables = square[0:1, :, :].rearrange("p a d -> p (a d)").bitcast(I32)
    slot_row, slot_w = tables[:, 0:NSLOT], tables[:, NSLOT:2 * NSLOT]
    pad_at = sb("pad_at", [1, NE], I32)

    k_norm = row[:, 1, 0, 0:D]
    bias_f = row[0:2, 0, :, 0:D]

    def words(t, pattern):
        return t.rearrange(pattern)

    hs = late[:, 0:RING * ROW].rearrange("p (r d) -> p r d", r=RING)
    hst_h, hst_l, au_h, au_l = xt_h, xt_l, at_h, at_l
    silu_g = xn[:, :, 0:FI]
    act_u = words(v_sb[:, :, :, :, :], "p a b c d -> p a (b c d)")[:, :, 0:FI]
    y_sb = words(probs[:, :, :], "p a b -> p (a b)")[:, 0:4 * D].rearrange("p (r d) -> p r d", r=4)
    past = words(we_f[0:1, :, :], "p a b -> p (a b)")[:, 0:NSLOT * NE].rearrange("p (s e) -> p s e", e=NE)
    past_n = words(v_bd[0:1, :, :, :, :], "p a b c d -> p (a b c d)")[:, 0:NSLOT * NE].rearrange("p (s e) -> p s e", e=NE)
    slot_e = words(ctx_in[0:1, :, :], "p a b -> p (a b)")[:, 0:4 * NSLOT].rearrange("p (a s) -> p a s", a=4)
    fin_in = late[:, :].rearrange("p (r k m d) -> p r k m d", r=4, k=2, m=2)

    def flat(t):
        return t.rearrange("p q l -> p (q l)")

    def k_parts(t, part):
        return kp[:, t.par, part].rearrange("p b c q l -> p (c q) b l")

    def q_part(dst, t, c):
        return dst[:, t.par, :, c, :, :].rearrange("p b g l -> p g b l")

    x_first, x_second, x_rest = sem("x_first"), sem("x_second"), sem("x_rest")
    consts_loaded = sem("consts_loaded")
    ctx_loaded = [sem(f"ctx_loaded{p}") for p in range(2)]
    we_loaded = [sem(f"we_loaded{p}") for p in range(2)]
    v_spread = [sem(f"v_spread{p}") for p in range(2)]
    row_sent = [sem(f"row_sent{s}") for s in range(SKEW)]
    pads_sent = sem("pads_sent")
    sp_passed, pool_passed, dve_passed, pe_passed = (sem(n) for n in ("sp_passed", "pool_passed", "dve_passed", "pe_passed"))
    pool_setup = sem("pool_setup")
    dve_setup = sem("dve_setup")
    names = """ln1_stats ln1_mean ln1_veps ln1_rstd ln1_shift xn_ready x_transposed xt_h_ready xt_l_ready
        ct_h_ready ct_ready k_projected projected v_ready q_squared k_squared qk_veps qk_rstd qn_ready kn_ready
        k_transposed k_h_ready k_l_ready q0_transposed q0_h_ready q0_l_ready q1_transposed
        q1_h_ready q1_l_ready max_scored max_found neg_hi_ready neg_max_ready
        neg_max_transposed neg_max_t_ready scored probs_ready weighed sum_inverted att_ready
        att_transposed at_h_ready at_l_ready o_projected x1_ready ln2_stats ln2_mean ln2_veps
        ln2_rstd row_ready row2_ready h_transposed ht_ready gated logit_ready we_h_ready we_ready ids_set""".split()
    S = {n: sem(n) for n in names}
    pair_names = "tops no_ready gap_ready choice_ready e_gap_ready routed counts_ready place_ready filled_new place_sel place_sum place_set weight_set1 weight_set2 weight_set3".split()
    R = {n: sem(n) for n in pair_names}
    plan = sem("plan")
    hs_loaded = [sem(f"hs_loaded{r}") for r in range(RING)]
    y_sent = [sem(f"y_sent{r}") for r in range(4)]
    names2 = """h2_transposed h2_h_ready h2_l_ready gate_up silu_ready act_ready act_transposed
        au_h_ready au_l_ready y_done y_ready""".split()
    F = {n: sem(n) for n in names2}
    fin_loaded = [sem(f"fin_loaded{r}") for r in range(4)]
    fin_stored = [sem(f"fin_stored{r}") for r in range(4)]
    fin_sum1, fin_sum2 = sem("fin_sum1"), sem("fin_sum2")

    tr_bank = bank[:, 0, :]
    qv_bank = bank[:, 1, :]
    k_bank = bank[:, 2, :]
    kq_bank = bank[:, 3, :]
    score_bank = bank[:, 4:6, :].rearrange("p a b -> p (a b)")
    av_bank = bank[:, 6, :]
    mo_bank = bank[:, 7, :]

    block = stack.enter_context(nc.Block())

    SETUP_POOL = 19
    SETUP_DVE = 12

    @block.sync
    def _(sp):
        x_v = x.rearrange("(t p) d -> p t d", p=P)
        sp.dma_start(x1[:, 0:2, :], x_v[:, 0:2, :]).then_inc(x_first, 16)
        sp.dma_start(wp_f, w_proj).then_inc(consts_loaded, 16)
        for p in range(2):
            sp.dma_start(ctx_in[:, p, :], ctx_t[p * P:(p + 1) * P, :]).then_inc(ctx_loaded[p], 16)
        sp.dma_start(bias_f, bias.rearrange("r (m d) -> r m d", m=4)).then_inc(consts_loaded, 16)
        sp.dma_start(qk_norm[:, :], norm_q.partition_broadcast(P)).then_inc(consts_loaded, 16)
        sp.dma_start(k_norm, norm_k.partition_broadcast(P)).then_inc(consts_loaded, 16)
        sp.dma_start(gate_w[:, :, :], w_gate.rearrange("p (c e) -> p c e", c=KC)).then_inc(consts_loaded, 16)
        sp.dma_start(x1[:, 2:8, :], x_v[:, 2:8, :]).then_inc(x_second, 16)
        for p in range(2):
            sp.dma_start(we_f[:, p, :], w_exp[p * P:(p + 1) * P, :]).then_inc(we_loaded[p], 16)
        sp.dma_start(x1[:, 8:NT, :], x_v[:, 8:NT, :]).then_inc(x_rest, 16)

        def load_ctx(t):
            need_alone(sp, sp_passed, S["ct_ready"], t.n - 1)
            sp.dma_start(ctx_in[:, t.par, :], ctx_t[bass.ds(t.n * P, P), :]).then_inc(ctx_loaded[t.par], 16)

        def load_weights(t):
            need_alone(sp, sp_passed, S["we_ready"], t.n - 1)
            sp.dma_start(we_f[:, t.par, :], w_exp[bass.ds(t.n * P, P), :]).then_inc(we_loaded[t.par], 16)

        def spread_v(t):
            need_alone(sp, sp_passed, S["v_ready"], t.n + 1)
            need_alone(sp, sp_passed, S["weighed"], t.n - 1)
            for b in range(NB):
                for q in range(2):
                    sp.dma_start(v_bd[q * L:(q + 1) * L, t.par, b, q, :],
                                 v_sb[b * L:(b + 1) * L, t.par, q, :, :].rearrange("p g d -> p (g d)")
                                 ).then_inc(v_spread[t.par], 16)

        sp.wait_ge(dve_setup, SETUP_DVE)
        sp.wait_ge(pool_setup, SETUP_POOL)

        def turn(j, s):
            if Tile(j, s + 2).live:
                load_ctx(Tile(j, s + 2))
            if Tile(j, s + 1).live and (not isinstance(j, int) or j * SKEW + s + 1 >= 2):
                load_weights(Tile(j, s + 1))
            if Tile(j, s).live:
                spread_v(Tile(j, s))

        turns_sp(sp, turn)

        sp.wait_ge(plan, PLAN)
        for e in range(NE):
            at = sp.value_load(pad_at[0:1, e:e + 1], min_val=0, max_val=NE * REG)
            sp.dma_start(sorted_rows[bass.ds(at, P), :], pad_rows[:, :]).then_inc(pads_sent, 16)
        sp.dma_start(sorted_rows[NE * REG:ROWS, :], pad_rows[:, :]).then_inc(pads_sent, 16)
        sp.wait_ge(pads_sent, 16 * (NE + 1))
        for s in range(SKEW):
            sp.wait_ge(row_sent[s], 2 * 16 * (NT // SKEW))

        def load_slot(j, r):
            at = sp.value_load(slot_row[0:1, bass.ds(j * RING + r, 1)], min_val=0, max_val=NE * REG)
            sp.dma_start(hs[:, r, :], sorted_rows[bass.ds(at, P), :]).then_inc(hs_loaded[r], 16)

        for r in range(RING):
            load_slot(0, r)
        with sp.Fori(1, NSLOT // RING) as j:
            for r in range(RING):
                need_alone(sp, sp_passed, y_sent[r % 4], (2 * j - 1 + r // 4) * 16)
                load_slot(j, r)
        for r in range(4):
            sp.wait_ge(y_sent[r], 16 * NSLOT // 4)

        ev = expert_out.rearrange("(k t p) d -> p k t d", k=2, p=P)
        ov = out.rearrange("(t p) d -> p t d", p=P)
        for g in range(NT // 2):
            if g >= 4:
                sp.wait_ge(fin_stored[g % 4], 16 * (g // 4))
            for k in range(2):
                sp.dma_start(fin_in[:, g % 4, k, :, :], ev[:, k, 2 * g:2 * g + 2, :]).then_inc(fin_loaded[g % 4], 16)
            if g >= 3:
                h = g - 3
                sp.wait_ge(fin_sum2, h + 1)
                sp.dma_start(ov[:, 2 * h:2 * h + 2, :], fin_in[:, h % 4, 0, :, :]).then_inc(fin_stored[h % 4], 16)
        for h in range(NT // 2 - 3, NT // 2):
            sp.wait_ge(fin_sum2, h + 1)
            sp.dma_start(ov[:, 2 * h:2 * h + 2, :], fin_in[:, h % 4, 0, :, :]).then_inc(fin_stored[h % 4], 16)
        for r in range(4):
            sp.wait_ge(fin_stored[r], 16 * (NT // 8))

    @block.gpsimd
    def _(pool):
        done = [0]

        def setup(ins):
            done[0] += 1
            ins.then_inc(pool_setup, 1)

        def after():
            pool.wait_ge(pool_setup, done[0])

        setup(pool.memset(ident[:, :], 0.0))
        setup(pool.memset(below[:, :], 0.0))
        setup(pool.memset(head_of[:, :, :], 0.0))
        setup(pool.memset(half_neg[:, :], -0.5))
        setup(pool.memset(one_neg[:, :], -1.0))
        setup(pool.memset(ones_b[:, :], 1.0))
        after()
        setup(pool.affine_select(out=ident[:, :], in_=ident[:, :], compare_op=ALU.not_equal, fill=1.0,
                                 base=0, pattern=[[-1, P]], channel_multiplier=1))
        setup(pool.affine_select(out=below[:, :], in_=below[:, :], compare_op=ALU.is_ge, fill=1.0,
                                 base=0, pattern=[[-1, P]], channel_multiplier=1))
        for base in (0, -NH):
            after()
            v = head_of[:, :, :].rearrange("r g (q m) -> r g q m", q=2)
            setup(pool.affine_select(out=v, in_=v, compare_op=ALU.not_equal, fill=1.0, base=base,
                                     pattern=[[-2, NPAIR], [-1, 2], [0, L]], channel_multiplier=1))
        setup(pool.tensor_copy(ident_b[:, :], ident[:, :]))
        setup(pool.iota(expert_no[:, :], [[1, NE]], base=0, channel_multiplier=0,
                        allow_small_or_imprecise_dtypes=True))
        setup(pool.iota(slot_no[:, :], [[1, NSLOT]], base=0, channel_multiplier=0,
                        allow_small_or_imprecise_dtypes=True))
        setup(pool.iota(filled[:, :], [[REG, NE]], base=0, channel_multiplier=0,
                        allow_small_or_imprecise_dtypes=True))
        setup(pool.iota(region_no[:, :], [[REG, NE]], base=0, channel_multiplier=0,
                        allow_small_or_imprecise_dtypes=True))
        setup(pool.iota(result_row[:, :, :], [[T, 2], [P, NT]], base=0, channel_multiplier=1))
        setup(pool.iota(zero_one[:, 1:2], [[0, 1]], base=0, channel_multiplier=1,
                        allow_small_or_imprecise_dtypes=True))
        setup(pool.memset(pad_rows[:, :], 0.0))
        after()
        setup(pool.iota(pad_rows[:, D:D + 1].bitcast(I32), [[0, 1]], base=2 * T, channel_multiplier=1))
        assert done[0] == SETUP_POOL, done[0]

        def split_ctx(t):
            need_alone(pool, pool_passed, ctx_loaded[t.par], (t.twins + 1) * 16)
            need_alone(pool, pool_passed, S["projected"], t.n - 1)
            src = ctx_in[:, t.par, :].rearrange("p (c n) -> p c n", c=KC)
            pool.tensor_scalar(ct_h[:, t.par, :, :], src, 1.0, 1.0, ALU.mult, ALU.mult).then_inc(S["ct_h_ready"], 1)
            need_alone(pool, pool_passed, S["ct_h_ready"], t.n + 1)
            pool.tensor_tensor(ct_l[:, t.par, :, :], src, ct_h[:, t.par, :, :].bitcast(F32),
                               ALU.subtract).then_inc(S["ct_ready"], 1)

        def split_weights(t):
            need_alone(pool, pool_passed, we_loaded[t.par], (t.twins + 1) * 16)
            cols = bass.ds(t.n * WS, WS)
            pool.tensor_copy(we_h[:, cols], we_f[:, t.par, :]).then_inc(S["we_h_ready"], 1)
            need_alone(pool, pool_passed, S["we_h_ready"], t.n + 1)
            pool.tensor_tensor(we_l[:, cols], we_f[:, t.par, :], we_h[:, cols].bitcast(F32),
                               ALU.subtract).then_inc(S["we_ready"], 1)

        def inv_sqrt(t, out_, tmp, in_, scale, eps, ready, mid, done_):
            need_alone(pool, pool_passed, ready, t.n + 1)
            pool.tensor_scalar(tmp, in_, scale, eps, ALU.mult, ALU.add).then_inc(mid, 1)
            need_alone(pool, pool_passed, mid, t.n + 1)
            pool.tensor_tensor(out_, tmp, half_neg[:, 0:tmp.shape[1]], ALU.pow).then_inc(done_, 1)

        def ln1(t):
            need_alone(pool, pool_passed, S["xn_ready"], t.n - 1)
            inv_sqrt(t, rstd[:, t.par, :], veps[:, t.par, :], mean_var[:, t.par, 1:2], 1.0, 1e-5,
                     S["ln1_mean"], S["ln1_veps"], S["ln1_rstd"])
            need_alone(pool, pool_passed, S["ln1_rstd"], t.n + 1)
            pool.tensor_scalar(shift[:, t.par, :], mean_var[:, t.par, 0:1], rstd[:, t.par, :], -1.0, ALU.mult, ALU.mult
                               ).then_inc(S["ln1_shift"], 1)

        def qk_rms(t):
            need_alone(pool, pool_passed, S["qn_ready"], t.n - 1)
            need_alone(pool, pool_passed, S["kn_ready"], t.n - 1)
            need_alone(pool, pool_passed, S["q_squared"], t.n + 1)
            inv_sqrt(t, r_qk[:, t.par, :], ms_eps[:, t.par, :], sumsq[:, t.par, :], 1.0 / D, 1e-6,
                     S["k_squared"], S["qk_veps"], S["qk_rstd"])

        def ln2(t):
            need_alone(pool, pool_passed, S["row_ready"], t.n - 1)
            inv_sqrt(t, rstd2[:, t.par, :], veps2[:, t.par, :], mean_var2[:, t.par, 1:2], 1.0, 1e-5,
                     S["ln2_mean"], S["ln2_veps"], S["ln2_rstd"])

        def weights(a, b, pp):
            need_alone(pool, pool_passed, R["e_gap_ready"], a.pair + 1)
            need_alone(pool, pool_passed, S["row2_ready"], b.n + 1)
            w = row[:, :, a.slot:a.slot + 2, D + 1:D + 2].rearrange("p k m d -> p k (m d)")
            pool.tensor_scalar(one_e[:, :], e_gap[:, pp, :], 1.0, 1.0, ALU.mult, ALU.add).then_inc(R["weight_set1"], 1)
            need_alone(pool, pool_passed, R["weight_set1"], a.pair + 1)
            pool.tensor_tensor(w[:, 0, :], one_e[:, :], one_neg[:, :], ALU.pow).then_inc(R["weight_set2"], 1)
            need_alone(pool, pool_passed, R["weight_set2"], a.pair + 1)
            pool.tensor_tensor(w[:, 1, :], e_gap[:, pp, :], w[:, 0, :], ALU.mult).then_inc(R["weight_set3"], 1)

        def send(t):
            need_alone(pool, pool_passed, S["row2_ready"], t.n + 1)
            pool.tensor_copy(row[:, :, t.slot, D:D + 1].bitcast(I32), result_row[:, :, bass.ds(t.n, 1)]
                             ).then_inc(S["ids_set"], 1)
            need_alone(pool, pool_passed, S["ids_set"], t.n + 1)
            need_alone(pool, pool_passed, R["place_set"], t.pair + 1)
            need_alone(pool, pool_passed, R["weight_set3"], t.pair + 1)
            for k in range(2):
                pool.indirect_dma_start(
                    sorted_rows, bass.IndirectOffsetOnAxis(ap=place_i[:, t.slot // 2, k, t.par:t.par + 1], axis=0),
                    row[:, k, t.slot, :], None, bounds_check=ROWS - 1, oob_is_err=False
                ).then_inc(row_sent[t.slot], 16)

        split_ctx(Tile(0, 0))

        def turn(j, s):
            if Tile(j, s + 1).live:
                split_ctx(Tile(j, s + 1))
            if Tile(j, s + 2).live:
                ln1(Tile(j, s + 2))
            if Tile(j, s).live:
                qk_rms(Tile(j, s))
            if s % 2 == 1 and Tile(j, s - 7).live:
                weights(Tile(j, s - 7), Tile(j, s - 6), (s - 7) // 2 % 2)
            if Tile(j, s - 7).live:
                send(Tile(j, s - 7))
            if Tile(j, s - 3).live:
                ln2(Tile(j, s - 3))
            if Tile(j, s).live:
                split_weights(Tile(j, s))

        ln1(Tile(0, 0))
        ln1(Tile(0, 1))
        turns_sp(pool, turn)

        def send_y(j, r):
            need_alone(pool, pool_passed, F["y_ready"], j * RING + r + 1)
            pool.indirect_dma_start(
                expert_out, bass.IndirectOffsetOnAxis(ap=hs[:, r, D:D + 1].bitcast(U32), axis=0),
                y_sb[:, r % 4, :], None, bounds_check=2 * T - 1, oob_is_err=False
            ).then_inc(y_sent[r % 4], 16)

        with pool.Fori(0, NSLOT // RING) as j:
            for r in range(RING):
                send_y(j, r)

    @block.scalar
    def _(act):
        def xt_hi(t):
            act.wait_ge(S["x_transposed"], t.n + 1)
            need(act, S["projected"], t.n - 1)
            act.copy(xt_h[:, t.par, :, :], tr_bank[:, 0:D].rearrange("p (c n) -> p c n", c=KC)
                     ).then_inc(S["xt_h_ready"], 1)

        def ln1_norm(t):
            act.wait_ge(S["ln1_shift"], t.n + 1)
            need(act, S["x_transposed"], t.n - 1)
            act.activation(xn[:, t.par, :], x1[:, t.at, :], ACT.Identity, bias=shift[:, t.par, :],
                           scale=rstd[:, t.par, :]).then_inc(S["xn_ready"], 1)

        def k_hi(t):
            act.wait_ge(S["k_transposed"], t.n + 1)
            need(act, S["scored"], t.n - 1)
            act.copy(k_parts(t, 0), kq_bank.rearrange("p (x b l) -> p x b l", b=NB, l=L)
                     ).then_inc(S["k_h_ready"], 1)

        def q_hi(t, c, src):
            act.wait_ge(S[f"q{c}_transposed"], t.n + 1)
            need(act, S["scored"], t.n - 1)
            act.copy(q_part(qp_h, t, c), src.rearrange("p (g b l) -> p g b l", g=NQ, b=NB)
                     ).then_inc(S[f"q{c}_h_ready"], 1)

        def row_copy(t):
            act.wait_ge(S["row_ready"], t.n + 1)
            if t.quads_ok:
                act.wait_ge(row_sent[t.slot], t.quad * 32)
            act.copy(row[:, 1, t.slot, 0:D], row[:, 0, t.slot, 0:D]).then_inc(S["row2_ready"], 1)

        def neg_max_rows(t):
            act.wait_ge(S["neg_max_transposed"], t.n + 1)
            need(act, S["scored"], t.n - 1)
            act.copy(neg_max_t[:, t.par, :], mo_bank[0:2 * NH, 0:P // 2].bitcast(BF16)
                     ).then_inc(S["neg_max_t_ready"], 1)

        def squares(t):
            act.wait_ge(S["k_projected"], t.n + 1)
            need(act, S["k_squared"], t.n)
            need(act, S["qk_veps"], t.n - 1)
            act.activation(square[:, 1, :], k_bank[:, 0:D], ACT.Square,
                           accum_out=sumsq[:, t.par, 1:2]).then_inc(S["k_squared"], 1)
            act.wait_ge(S["projected"], t.n + 1)
            need(act, S["q_squared"], t.n)
            act.activation(square[:, 0, :], qv_bank[:, 0:D], ACT.Square,
                           accum_out=sumsq[:, t.par, 0:1]).then_inc(S["q_squared"], 1)

        def v_copy(t):
            if t.twins_ok:
                act.wait_ge(v_spread[t.par], t.twins * 64)
            else:
                act.wait_ge(dve_setup, SETUP_DVE)
            act.copy(v_sb[:, t.par, :, :, 0:HD],
                     qv_bank[:, D:2 * D].rearrange("p (q g d) -> p q g d", q=2, g=NPAIR)
                     ).then_inc(S["v_ready"], 1)

        def att_hi(t):
            act.wait_ge(S["att_transposed"], t.n + 1)
            need(act, S["o_projected"], t.n - 1)
            act.copy(at_h[:, t.par, :, :], av_bank[:, 0:D].rearrange("p (c n) -> p c n", c=KC)
                     ).then_inc(S["at_h_ready"], 1)

        def ht_copy(t):
            act.wait_ge(S["h_transposed"], t.n + 1)
            need(act, S["gated"], t.n - 1)
            act.copy(ht[:, t.par, :, :], tr_bank[:, 0:D].rearrange("p (c n) -> p c n", c=KC)
                     ).then_inc(S["ht_ready"], 1)

        def softmax_exp(t):
            act.wait_ge(S["scored"], t.n + 1)
            need(act, S["weighed"], t.n - 1)
            act.activation(probs[:, t.par, :], score_bank, ACT.Exp).then_inc(S["probs_ready"], 1)

        def k_scale(t):
            act.wait_ge(S["qk_rstd"], t.n + 1)
            need(act, S["k_transposed"], t.n - 1)
            dst = kn[:, t.par, :].rearrange("p (q x) -> p q x", q=2)[:, :, 0:D].rearrange(
                "p q (g r d) -> p q g r d", g=NPAIR, r=2)[:, :, :, 0, :]
            act.activation(dst, k_bank[:, 0:D].rearrange("p (g q d) -> p q g d", g=NPAIR, q=2), ACT.Copy,
                           scale=r_qk[:, t.par, 1:2]).then_inc(S["kn_ready"], 1)

        def logits_copy(t):
            act.wait_ge(S["gated"], t.n + 1)
            if t.choice is not None:
                act.wait_ge(R["no_ready"], t.choice)
            act.copy(logit[:, t.par, :], av_bank[:, 0:NE]).then_inc(S["logit_ready"], 1)

        def counts_copy(pair, used):
            act.wait_ge(R["routed"], pair + 1)
            if used:
                act.wait_ge(R["filled_new"], pair)
                act.wait_ge(R["place_ready"], pair)
            act.copy(counts[:, :], kq_bank[:, 0:3 * NE]).then_inc(R["counts_ready"], 1)

        def gap_exp(pair, pp):
            act.wait_ge(R["gap_ready"], pair + 1)
            act.activation(e_gap[:, pp, :], gap[:, pp, :], ACT.Exp).then_inc(R["e_gap_ready"], 1)

        def turn(j, s):
            def tile(lag):
                t = Tile(j, s - lag)
                static = isinstance(j, int)
                t.twins_ok = not static or t.n >= 2
                t.quads_ok = not static or t.n >= 4
                t.at = t.n if static else bass.ds(t.n, 1)
                return t
            if s % 2 == 1 and tile(7).live:
                gap_exp(tile(7).pair, (s - 7) // 2 % 2)
            if tile(0).live:
                xt_hi(tile(0))
            if tile(1).live:
                k_hi(tile(1))
            if tile(-1).live:
                ln1_norm(tile(-1))
            if tile(1).live:
                q_hi(tile(1), 0, kq_bank)
            if tile(0).live:
                squares(tile(0))
            if tile(2).live:
                neg_max_rows(tile(2))
            if tile(1).live:
                q_hi(tile(1), 1, tr_bank)
            if tile(3).live:
                att_hi(tile(3))
            if tile(0).live:
                v_copy(tile(0))
            if tile(4).live:
                row_copy(tile(4))
            if tile(0).live:
                k_scale(tile(0))
            if s % 2 == 0 and tile(6).live:
                counts_copy(tile(6).pair, not isinstance(j, int) or tile(6).n >= 2)
            if tile(4).live:
                ht_copy(tile(4))
            if tile(2).live:
                softmax_exp(tile(2))
            if tile(4).live:
                t = tile(4)
                before = (j * 2 + (s - 6) // 2 + 1) * 3
                t.choice = before if not isinstance(j, int) or t.n >= 2 else None
                logits_copy(t)

        t = Tile(0, 0)
        t.at = 0
        ln1_norm(t)
        turns_sp(act, turn)

        def hst_hi(m, p):
            act.wait_ge(F["h2_transposed"], m + 1)
            need(act, F["gate_up"], m - 1)
            act.copy(hst_h[:, p, :, :], bank[:, p, 0:D].rearrange("p (c n) -> p c n", c=KC)
                     ).then_inc(F["h2_h_ready"], 1)

        def silu(m, p):
            act.wait_ge(F["gate_up"], m + 1)
            need(act, F["act_ready"], m - 1)
            act.activation(silu_g[:, p, :], bank[:, 2 + p, 0:FI], ACT.Silu).then_inc(F["silu_ready"], 1)

        def au_hi(m, p):
            act.wait_ge(F["act_transposed"], m + 1)
            need(act, F["y_done"], m - 1)
            act.copy(au_h[:, p, 0, :], bank[:, 4 + p, 0:P]).then_inc(F["au_h_ready"], 1)
            act.copy(au_h[0:FB, p, 1, :], bank[0:FB, 4 + p, P:2 * P]).then_inc(F["au_h_ready"], 1)

        def y_copy(m, r, reuse, q):
            act.wait_ge(F["y_done"], m + 1)
            if reuse is not None:
                act.wait_ge(y_sent[r], reuse)
            act.copy(y_sb[:, r, :], bank[:, 6 + q, 0:D]).then_inc(F["y_ready"], 1)

        def turn2(j, r, static):
            i = j * RING + r
            if not static or i < NSLOT:
                hst_hi(i, r % 2)
            if not static or 0 <= i - 1 < NSLOT:
                silu(i - 1, (r - 1) % 2)
            if not static or 0 <= i - 2 < NSLOT:
                au_hi(i - 2, r % 2)
            if not static or 0 <= i - 3 < NSLOT:
                m = i - 3
                turnsback = (j * 2 + (r - 3) // 4) * 16
                y_copy(m, (r - 3) % 4, turnsback if not static or m >= 4 else None, (r - 3) % 2)

        slots(act, turn2)

    @block.vector
    def _(dve):
        done = [0]

        def setup(ins):
            done[0] += 1
            ins.then_inc(dve_setup, 1)

        def after():
            dve.wait_ge(dve_setup, done[0])

        bias_h4 = bias_hl[:, :].rearrange("r (m d) -> r m d", m=4)
        setup(dve.memset(ones_row_f[:, :], 1.0))
        setup(dve.memset(v_sb[:, :, :, :, :], 1.0))
        setup(dve.memset(v_bd[:, :, :, :, :], 0.0))
        setup(dve.memset(late[:, 0:QN + 4 * KX], 0.0))
        after()
        setup(dve.tensor_copy(ones_row[:, :], ones_row_f[:, :]))
        dve.wait_ge(consts_loaded, 16 * 5)
        setup(dve.tensor_copy(wp_h[:, :, :, :].rearrange("p m c n -> p (m c n)"), wp_f))
        setup(dve.tensor_copy(bias_h4, bias_f))
        dve.wait_ge(pool_setup, SETUP_POOL)
        setup(dve.tensor_scalar(zero_one[:, 0:1], zero_one[:, 1:2], -1.0, 1.0, ALU.mult, ALU.add))
        setup(dve.scalar_tensor_tensor(qk_norm[:, :], qk_norm[:, :], HD ** -0.5, k_norm, ALU.mult, ALU.mult))
        after()
        setup(dve.tensor_tensor(wp_l[:, :, :, :].rearrange("p m c n -> p (m c n)"), wp_f,
                                wp_h[:, :, :, :].rearrange("p m c n -> p (m c n)").bitcast(F32), ALU.subtract))
        setup(dve.tensor_tensor(bias_f, bias_f, bias_h4.bitcast(F32), ALU.subtract))
        after()
        dve.tensor_scalar(bias_f, bias_f, zero_one[:, 1:2], None, ALU.mult).then_inc(plan, 1)
        dve.wait_ge(plan, 1)
        setup(dve.scalar_tensor_tensor(bias_hl[:, :].rearrange("r (m d) -> r m d", m=4), bias_h4.bitcast(F32),
                                       zero_one[:, 0:1], bias_f,
                                       ALU.mult, ALU.add))
        assert done[0] == SETUP_DVE, done[0]

        def ln1_stats(t, loaded):
            if loaded is not None:
                dve.wait_ge(loaded, 16)
            dve.bn_stats(stats[:, t.par, :], x1[:, t.at, :]).then_inc(S["ln1_stats"], 1)

        def ln1_mean(t):
            need(dve, S["xn_ready"], t.n - 1)
            need_alone(dve, dve_passed, S["ln1_stats"], t.n + 1)
            dve.bn_aggr(mean_var[:, t.par, :], stats[:, t.par, :]).then_inc(S["ln1_mean"], 1)

        def xt_lo(t):
            dve.wait_ge(S["xt_h_ready"], t.n + 1)
            need(dve, S["projected"], t.n - 1)
            dve.tensor_tensor(xt_l[:, t.par, :, :], tr_bank[:, 0:D].rearrange("p (c n) -> p c n", c=KC),
                              xt_h[:, t.par, :, :].bitcast(F32), ALU.subtract).then_inc(S["xt_l_ready"], 1)

        def k_lo(t):
            dve.wait_ge(S["k_h_ready"], t.n + 1)
            need(dve, S["scored"], t.n - 1)
            dve.tensor_tensor(k_parts(t, 1), kq_bank.rearrange("p (x b l) -> p x b l", b=NB, l=L), k_parts(t, 0), ALU.subtract).then_inc(S["k_l_ready"], 1)

        def q_lo(t, c, src):
            dve.wait_ge(S[f"q{c}_h_ready"], t.n + 1)
            need(dve, S["scored"], t.n - 1)
            dve.tensor_tensor(q_part(qp_l, t, c), src.rearrange("p (g b l) -> p g b l", g=NQ, b=NB), q_part(qp_h, t, c), ALU.subtract).then_inc(S[f"q{c}_l_ready"], 1)

        def find_max(t):
            dve.wait_ge(S["max_scored"], t.n + 1)
            dve.tensor_reduce(row_max[:, t.par, :], score_bank.rearrange("p (h k) -> p h k", h=NH),
                              AX.X, ALU.max).then_inc(S["max_found"], 1)

        def neg_max_hi(t):
            dve.wait_ge(S["max_found"], t.n + 1)
            need(dve, S["neg_max_transposed"], t.n - 1)
            dve.tensor_scalar(neg_max[:, t.par, 0:NH], row_max[:, t.par, :], -1.0, None, ALU.mult
                              ).then_inc(S["neg_hi_ready"], 1)

        def neg_max_lo(t):
            dve.wait_ge(S["neg_hi_ready"], t.n + 1)
            dve.scalar_tensor_tensor(neg_max[:, t.par, NH:2 * NH], row_max[:, t.par, :], -1.0,
                                     neg_max[:, t.par, 0:NH], ALU.mult, ALU.subtract
                                     ).then_inc(S["neg_max_ready"], 1)

        def invert_sums(t):
            dve.wait_ge(S["weighed"], t.n + 1)
            v = av_bank[:, 0:NH * VW].rearrange("p (h d) -> p h d", h=NH)
            dve.reciprocal(r_sum[:, t.par, :], v[:, :, HD:VW].rearrange("p h d -> p (h d)")).then_inc(S["sum_inverted"], 1)

        def normalise(t):
            v = av_bank[:, 0:NH * VW].rearrange("p (h d) -> p h d", h=NH)
            dve.wait_ge(S["sum_inverted"], t.n + 1)
            need(dve, S["att_transposed"], t.n - 1)
            dve.tensor_tensor(att[:, t.par, :, :], v[:, :, 0:HD],
                              r_sum[:, t.par, :].unsqueeze(2).to_broadcast([P, NH, HD]), ALU.mult
                              ).then_inc(S["att_ready"], 1)

        def att_lo(t):
            dve.wait_ge(S["at_h_ready"], t.n + 1)
            need(dve, S["o_projected"], t.n - 1)
            dve.tensor_tensor(at_l[:, t.par, :, :], av_bank[:, 0:D].rearrange("p (c n) -> p c n", c=KC),
                              at_h[:, t.par, :, :].bitcast(F32), ALU.subtract).then_inc(S["at_l_ready"], 1)

        def q_scale(t):
            dve.wait_ge(S["qk_rstd"], t.n + 1)
            dve.wait_ge(S["v_ready"], t.n + 1)
            need(dve, S["q1_transposed"], t.n)
            dst = qn.rearrange("p (g x) -> p g x", x=QC)[:, :, 0:2 * HD]
            src, norm = (a.rearrange("p (g y) -> p g y", g=NPAIR) for a in (qv_bank[:, 0:D], qk_norm[:, :]))
            dve.scalar_tensor_tensor(dst, src, r_qk[:, t.par, 0:1], norm, ALU.mult, ALU.mult).then_inc(S["qn_ready"], 1)

        def residual(t):
            dve.wait_ge(S["o_projected"], t.n + 1)
            dve.tensor_tensor(x1[:, t.at, :], mo_bank[:, 0:D], x1[:, t.at, :], ALU.add).then_inc(S["x1_ready"], 1)
            need_alone(dve, dve_passed, S["x1_ready"], t.n + 1)
            dve.bn_stats(stats2[:, t.par, :], x1[:, t.at, :]).then_inc(S["ln2_stats"], 1)
            need(dve, S["row_ready"], t.n - 1)
            need_alone(dve, dve_passed, S["ln2_stats"], t.n + 1)
            dve.bn_aggr(mean_var2[:, t.par, :], stats2[:, t.par, :]).then_inc(S["ln2_mean"], 1)

        def ln2_norm(t):
            dve.wait_ge(S["ln2_rstd"], t.n + 1)
            if t.quads_ok:
                dve.wait_ge(row_sent[t.slot], t.quad * 32)
            dve.tensor_scalar(row[:, 0, t.slot, 0:D], x1[:, t.at, :], mean_var2[:, t.par, 0:1], rstd2[:, t.par, :],
                              ALU.subtract, ALU.mult).then_inc(S["row_ready"], 1)

        def choose(a, b, pp):
            need_alone(dve, dve_passed, S["logit_ready"], b.n + 1)
            for m in range(2):
                dve.max(top8[:, m, :], logit[:, m, :]).then_inc(R["tops"], 1)
            need_alone(dve, dve_passed, R["tops"], (a.pair + 1) * 2)
            for m in range(2):
                dve.max_index(top8_no[:, m, :], top8[:, m, :], logit[:, m, :]).then_inc(R["no_ready"], 1)
            dve.tensor_tensor(gap[:, pp, :], top8[:, :, 1], top8[:, :, 0], ALU.subtract).then_inc(R["gap_ready"], 1)
            dve.wait_ge(R["no_ready"], a.pair * 3 + 2)
            dve.tensor_copy(top_no[:, :, :], top8_no[:, :, 0:2]).then_inc(R["no_ready"], 1)
            dve.wait_ge(R["no_ready"], a.pair * 3 + 3)
            for k in range(2):
                dve.tensor_tensor(chosen[:, pp, k, :, :], expert_no[:, :].unsqueeze(1).to_broadcast([P, 2, NE]),
                                  top_no[:, :, k:k + 1].to_broadcast([P, 2, NE]), ALU.is_equal
                                  ).then_inc(R["choice_ready"], 1)
            dve.wait_ge(R["choice_ready"], a.pair * 3 + 2)
            dve.tensor_tensor(chosen_b[:, pp, :, :], chosen[:, pp, 0, :, :], chosen[:, pp, 1, :, :], ALU.add
                              ).then_inc(R["choice_ready"], 1)

        def route(a, b, pp):
            dve.wait_ge(R["counts_ready"], a.pair + 1)
            dve.tensor_tensor(place[:, :, :], counts[:, 0:2 * NE].rearrange("p (m e) -> p m e", m=2),
                              filled[:, :].unsqueeze(1).to_broadcast([P, 2, NE]), ALU.add
                              ).then_inc(R["place_ready"], 1)
            dve.wait_ge(R["place_ready"], a.pair + 1)
            dve.tensor_tensor(filled[:, :], filled[:, :], counts[:, 2 * NE:3 * NE], ALU.add
                              ).then_inc(R["filled_new"], 1)
            dve.tensor_tensor(place_of[:, :, :, :], chosen[:, pp, :, :, :],
                              place[:, :, :].unsqueeze(1).to_broadcast([P, 2, 2, NE]), ALU.mult
                              ).then_inc(R["place_sel"], 1)
            dve.wait_ge(R["place_sel"], a.pair + 1)
            dve.tensor_reduce(place_f[:, :, :], place_of[:, :, :, :], AX.X, ALU.add).then_inc(R["place_sum"], 1)
            dve.wait_ge(R["place_sum"], a.pair + 1)
            if a.sent is not None:
                dve.wait_ge(row_sent[a.slot], a.sent)
                dve.wait_ge(row_sent[b.slot], a.sent)
            dve.tensor_copy(place_i[:, pp, :, :], place_f[:, :, :]).then_inc(R["place_set"], 1)

        def turn(j, s):
            def tile(lag):
                t = Tile(j, s - lag)
                static = isinstance(j, int)
                t.twins_ok = not static or t.n >= 2
                t.quads_ok = not static or t.n >= 4
                t.at = t.n if static else bass.ds(t.n, 1)
                t.sent = t.quad * 32 if t.quads_ok else None
                return t
            ahead = tile(-2) if tile(-2).live else None
            if tile(0).live:
                xt_lo(tile(0))
            if tile(1).live:
                k_lo(tile(1))
            if tile(2).live:
                find_max(tile(2))
            if ahead:
                n = j * SKEW + s + 2 if isinstance(j, int) else None
                ln1_stats(ahead, {2: x_second, 8: x_rest}.get(n))
            if tile(2).live:
                neg_max_hi(tile(2))
            if tile(3).live:
                invert_sums(tile(3))
            if tile(2).live:
                neg_max_lo(tile(2))
            if tile(3).live:
                normalise(tile(3))
            if ahead:
                ln1_mean(ahead)
            if tile(1).live:
                q_lo(tile(1), 0, kq_bank)
            if tile(4).live:
                ln2_norm(tile(4))
            if s % 2 == 0 and tile(6).live:
                choose(tile(6), tile(5), (s - 6) // 2 % 2)
            if s % 2 == 1 and tile(7).live:
                route(tile(7), tile(6), (s - 7) // 2 % 2)
            if tile(1).live:
                q_lo(tile(1), 1, tr_bank)
            if tile(3).live:
                att_lo(tile(3))
            if tile(0).live:
                q_scale(tile(0))
            if tile(3).live:
                residual(tile(3))

        for n in range(2):
            t = Tile(0, n)
            t.at = n
            ln1_stats(t, x_first)
            ln1_mean(t)
        turns_sp(dve, turn)

        steps = [1]

        def step(ins):
            steps[0] += 1
            ins.then_inc(plan, 1)
            dve.wait_ge(plan, steps[0])

        dve.wait_ge(R["filled_new"], NT // 2)
        step(dve.tensor_tensor(count[:, :], filled[0:1, :], region_no[:, :], ALU.subtract))
        step(dve.tensor_scalar(count[:, :], count[:, :], float(P - 1), None, ALU.add))
        step(dve.tensor_copy(count_i[:, :], count[:, :]))
        step(dve.tensor_copy(pad_at[:, :], filled[0:1, :]))
        step(dve.tensor_scalar(tiles_i[:, :], count_i[:, :], 7, None, ALU.arith_shift_right))
        step(dve.tensor_copy(tiles[:, :], tiles_i[:, :]))
        step(dve.tensor_copy(cum[:, 0, :], tiles[:, :]))
        for n, d in enumerate((1, 2, 4)):
            step(dve.tensor_copy(cum[:, n + 1, 0:d], cum[:, n, 0:d]))
            step(dve.tensor_tensor(cum[:, n + 1, d:NE], cum[:, n, d:NE], cum[:, n, 0:NE - d], ALU.add))
        step(dve.tensor_tensor(past[:, :, :], slot_no[:, :].unsqueeze(2).to_broadcast([1, NSLOT, NE]),
                               cum[:, 3, :].unsqueeze(1).to_broadcast([1, NSLOT, NE]), ALU.is_ge))
        step(dve.tensor_tensor(past_n[:, :, :], past[:, :, :],
                               tiles[:, :].unsqueeze(1).to_broadcast([1, NSLOT, NE]), ALU.mult))
        step(dve.tensor_reduce(slot_e[:, 0, :], past[:, :, :], AX.X, ALU.add))
        step(dve.tensor_reduce(slot_e[:, 1, :], past_n[:, :, :], AX.X, ALU.add))
        step(dve.tensor_tensor(slot_e[:, 2, :], slot_no[:, :], slot_e[:, 1, :], ALU.subtract))
        step(dve.tensor_scalar(slot_e[:, 3, :], slot_e[:, 0, :], float(REG), None, ALU.mult))
        step(dve.scalar_tensor_tensor(slot_e[:, 1, :], slot_e[:, 2, :], float(P), slot_e[:, 3, :], ALU.mult, ALU.add))
        step(dve.tensor_scalar(slot_row[:, :], slot_e[:, 1, :], float(NE * REG), None, ALU.min))
        step(dve.tensor_scalar(slot_w[:, :], slot_e[:, 0, :], float(NE - 1), float(EW), ALU.min, ALU.mult))
        assert steps[0] == PLAN, steps[0]

        def hst_lo(m, p):
            dve.wait_ge(F["h2_h_ready"], m + 1)
            need(dve, F["gate_up"], m - 1)
            dve.tensor_tensor(hst_l[:, p, :, :], bank[:, p, 0:D].rearrange("p (c n) -> p c n", c=KC),
                              hst_h[:, p, :, :].bitcast(F32), ALU.subtract).then_inc(F["h2_l_ready"], 1)

        def gate_mult(m, p, r):
            dve.wait_ge(F["silu_ready"], m + 1)
            need(dve, F["act_transposed"], m - 1)
            dve.scalar_tensor_tensor(act_u[:, p, :], silu_g[:, p, :], hs[:, r, D + 1:D + 2], bank[:, 2 + p, FI:2 * FI],
                                     ALU.mult, ALU.mult).then_inc(F["act_ready"], 1)

        def au_lo(m, p):
            dve.wait_ge(F["au_h_ready"], m * 2 + 2)
            need(dve, F["y_done"], m - 1)
            dve.tensor_tensor(au_l[:, p, 0, :], bank[:, 4 + p, 0:P], au_h[:, p, 0, :].bitcast(F32),
                              ALU.subtract).then_inc(F["au_l_ready"], 1)
            dve.tensor_tensor(au_l[0:FB, p, 1, :], bank[0:FB, 4 + p, P:2 * P], au_h[0:FB, p, 1, :].bitcast(F32),
                              ALU.subtract).then_inc(F["au_l_ready"], 1)

        def turn2(j, r, static):
            i = j * RING + r
            if not static or i < NSLOT:
                hst_lo(i, r % 2)
            if not static or 0 <= i - 1 < NSLOT:
                gate_mult(i - 1, (r - 1) % 2, (r - 1) % RING)
            if not static or 0 <= i - 2 < NSLOT:
                au_lo(i - 2, r % 2)

        slots(dve, turn2)

        for g in range(NT // 2):
            dve.wait_ge(fin_loaded[g % 4], 32 * (g // 4 + 1))
            v = fin_in[:, g % 4, 0, :, :]
            dve.tensor_tensor(v, v, fin_in[:, g % 4, 1, :, :], ALU.add).then_inc(fin_sum1, 1)
            dve.wait_ge(fin_sum1, g + 1)
            dve.tensor_tensor(v, v, x1[:, 2 * g:2 * g + 2, :], ALU.add).then_inc(fin_sum2, 1)

    @block.tensor
    def _(pe):
        pe.wait_ge(pool_setup, SETUP_POOL)
        pe.wait_ge(dve_setup, SETUP_DVE)
        QM, KM, VM, OM = range(4)

        def three(dst, a_h, a_l, b_h, b_l, start, stop):
            pe.matmul(dst, a_h, b_h, start=start, stop=False)
            pe.matmul(dst, a_h, b_l, start=False, stop=False)
            return pe.matmul(dst, a_l, b_h, start=False, stop=stop)

        def project(dst, a_h, a_l, m):
            for c in range(KC):
                three(dst, a_h[:, c, :], a_l[:, c, :], wp_h[:, m, c, :], wp_l[:, m, c, :], c == 0, False)
            return pe.matmul(dst, ones_row[:, :], bias_hl[:, m * D:(m + 1) * D], start=False, stop=True)

        def tr_x(t):
            pe.wait_ge(S["xn_ready"], t.n + 1)
            need(pe, S["q1_l_ready"], t.n - 1)
            need(pe, S["ht_ready"], t.n - 4)
            for c in range(KC):
                ins = pe.transpose(tr_bank[:, c * P:(c + 1) * P], xn[:, t.par, c * P:(c + 1) * P], ident[:, :])
            ins.then_inc(S["x_transposed"], 1)

        def tr_k(t):
            pe.wait_ge(S["kn_ready"], t.n + 1)
            need(pe, S["q0_l_ready"], t.n)
            if t.counted is not None:
                pe.wait_ge(R["counts_ready"], t.counted)
            for c in range(KC):
                for q in range(2):
                    at = (c * 2 + q) * P
                    ins = pe.transpose(kq_bank[:, at:at + P], kn[:, t.par, q * D + c * P:q * D + (c + 1) * P], ident[:, :])
            ins.then_inc(S["k_transposed"], 1)

        def tr_q(t, c, dst):
            for g in range(NQ):
                at = c * NQ * QC + g * P
                ins = pe.transpose(dst[:, g * P:(g + 1) * P], qn[:, at:at + P], ident[:, :])
            ins.then_inc(S[f"q{c}_transposed"], 1)

        def tr_q0(t):
            pe.wait_ge(S["qn_ready"], t.n + 1)
            pe.wait_ge(S["k_l_ready"], t.n + 1)
            tr_q(t, 0, kq_bank)

        def tr_q1(t, x_read):
            pe.wait_ge(S["xt_l_ready"], x_read)
            tr_q(t, 1, tr_bank)

        def score_max(t):
            pe.wait_ge(S["k_h_ready"], t.n + 1)
            pe.wait_ge(S["q0_h_ready"], t.n + 1)
            pe.wait_ge(S["q1_h_ready"], t.n + 1)
            need(pe, S["probs_ready"], t.n)
            for b in range(NB):
                for c in range(KC):
                    for gh in range(NQ // 2):
                        at = ((b * KC + c) * NQ // 2 + gh) * P
                        ins = pe.matmul(score_bank[:, at:at + P], flat(qp_h[:, t.par, b, c, 2 * gh:2 * gh + 2, :]),
                                        flat(kp[:, t.par, 0, b, c, :, :]), start=True, stop=True)
            ins.then_inc(S["max_scored"], 1)

        def weigh(t):
            pe.wait_ge(S["probs_ready"], t.n + 1)
            pe.wait_ge(v_spread[t.par], (t.twins + 1) * 64)
            need(pe, S["at_l_ready"], t.n)
            need(pe, S["logit_ready"], t.n - 1)
            for b in range(NB):
                for g in range(NPAIR):
                    at = (b * NPAIR + g) * L
                    ins = pe.matmul(av_bank[b * L:(b + 1) * L, g * 2 * VW:(g + 1) * 2 * VW],
                                    probs[:, t.par, at:at + L],
                                    v_bd[:, t.par, b, :, g * VW:(g + 1) * VW], start=True, stop=True)
            ins.then_inc(S["weighed"], 1)

        def project_qkv(t):
            pe.wait_ge(S["xt_h_ready"], t.n + 1)
            pe.wait_ge(S["xt_l_ready"], t.n + 1)
            pe.wait_ge(S["ct_ready"], t.n + 1)
            need(pe, S["qn_ready"], t.n)
            need(pe, S["kn_ready"], t.n)
            project(k_bank[:, 0:D], ct_h[:, t.par], ct_l[:, t.par], KM).then_inc(S["k_projected"], 1)
            project(qv_bank[:, 0:D], xt_h[:, t.par], xt_l[:, t.par], QM)
            project(qv_bank[:, D:2 * D], ct_h[:, t.par], ct_l[:, t.par], VM).then_inc(S["projected"], 1)

        def tr_max(t):
            pe.wait_ge(S["neg_max_ready"], t.n + 1)
            need(pe, S["x1_ready"], t.n - 1)
            pe.transpose(mo_bank[0:2 * NH, 0:P // 2].bitcast(BF16), neg_max[:, t.par, :], ident_b[:, :]
                         ).then_inc(S["neg_max_transposed"], 1)

        def tr_att(t):
            pe.wait_ge(S["att_ready"], t.n + 1)
            for c in range(KC):
                ins = pe.transpose(av_bank[:, c * P:(c + 1) * P],
                                   att[:, t.par, c * 8:(c + 1) * 8, :].rearrange("p h d -> p (h d)"), ident[:, :])
            ins.then_inc(S["att_transposed"], 1)

        def tr_h(t):
            pe.wait_ge(S["row_ready"], t.n + 1)
            pe.wait_ge(S["xt_l_ready"], t.xt_read)
            pe.wait_ge(S["q1_l_ready"], t.q_read)
            for c in range(KC):
                ins = pe.transpose(tr_bank[:, c * P:(c + 1) * P], row[:, 0, t.slot, c * P:(c + 1) * P], ident[:, :])
            ins.then_inc(S["h_transposed"], 1)

        def score(t):
            pe.wait_ge(S["neg_max_t_ready"], t.n + 1)
            pe.wait_ge(S["k_l_ready"], t.n + 1)
            pe.wait_ge(S["q0_l_ready"], t.n + 1)
            pe.wait_ge(S["q1_l_ready"], t.n + 1)
            pe.wait_ge(S["max_found"], t.n + 1)
            for b in range(NB):
                for c in range(KC):
                    dst = score_bank[:, (b * KC + c) * NQ * L:(b * KC + c + 1) * NQ * L]
                    k_h, k_l = (flat(kp[:, t.par, n, b, c, :, :]) for n in range(2))
                    q_h, q_l = (flat(q[:, t.par, b, c, :, :]) for q in (qp_h, qp_l))
                    pe.matmul(dst, k_h, q_h, start=True, stop=False)
                    pe.matmul(dst, k_h, q_l, start=False, stop=False)
                    pe.matmul(dst, k_l, q_h, start=False, stop=False)
                    for gh in range(NQ // 2):
                        ins = pe.matmul(dst[:, gh * P:(gh + 1) * P], head_of[:, (b * KC + c) * NQ // 2 + gh, :],
                                        neg_max_t[:, t.par, :], start=False, stop=gh == NQ // 2 - 1)
            ins.then_inc(S["scored"], 1)

        def gate(t):
            pe.wait_ge(S["ht_ready"], t.n + 1)
            if t.att_read is not None:
                pe.wait_ge(S["at_l_ready"], t.att_read)
            need(pe, S["logit_ready"], t.n)
            for half in range(2):
                rows = slice(half * 64, half * 64 + 64)
                for c in range(KC):
                    ins = pe.matmul(av_bank[rows, 0:NE], ht[:, t.par, c, rows], gate_w[:, c, :],
                                    start=(c == 0), stop=(c == KC - 1))
            ins.then_inc(S["gated"], 1)

        def project_out(t):
            pe.wait_ge(S["at_h_ready"], t.n + 1)
            pe.wait_ge(S["at_l_ready"], t.n + 1)
            if t.max_read is not None:
                pe.wait_ge(S["neg_max_t_ready"], t.max_read)
            project(mo_bank[:, 0:D], at_h[:, t.par], at_l[:, t.par], OM).then_inc(S["o_projected"], 1)

        def count_rows(pair, pp, q_read):
            pe.wait_ge(R["choice_ready"], pair * 3 + 3)
            pe.wait_ge(S["q0_l_ready"], q_read)
            a, b = chosen_b[:, pp, 0, :], chosen_b[:, pp, 1, :]
            c = kq_bank
            pe.matmul(c[:, 0:NE], below[:, :], a, start=True, stop=True)
            pe.matmul(c[:, NE:2 * NE], below[:, :], b, start=True, stop=False)
            pe.matmul(c[:, NE:2 * NE], ones_b[:, :], a, start=False, stop=True)
            pe.matmul(c[:, 2 * NE:3 * NE], ones_b[:, :], a, start=True, stop=False)
            pe.matmul(c[:, 2 * NE:3 * NE], ones_b[:, :], b, start=False, stop=True).then_inc(R["routed"], 1)

        def turn(j, s):
            static = isinstance(j, int)
            i = j * SKEW + s

            def tile(lag):
                return Tile(j, s - lag)

            def seen(value):
                return min(value, NT) if static else value

            if tile(0).live:
                tr_x(tile(0))
            if tile(1).live:
                t = tile(1)
                t.counted = j * 2 + (s - 7) // 2 + 1 if s % 2 == 1 and (not static or i >= 7) else None
                tr_k(t)
            if tile(2).live:
                score_max(tile(2))
            if tile(3).live:
                weigh(tile(3))
            if tile(1).live:
                tr_q0(tile(1))
            if tile(0).live:
                project_qkv(tile(0))
            if tile(2).live:
                tr_max(tile(2))
            if tile(1).live:
                tr_q1(tile(1), seen(i + 1))
            if tile(3).live:
                tr_att(tile(3))
            if s % 2 == 0 and tile(6).live:
                count_rows(tile(6).pair, (s - 6) // 2 % 2, seen(i))
            if tile(2).live:
                score(tile(2))
            if tile(4).live:
                t = tile(4)
                t.xt_read, t.q_read = seen(i + 1), seen(i)
                tr_h(t)
            if tile(3).live:
                t = tile(3)
                t.max_read = seen(i - 1)
                project_out(t)
            if tile(4).live:
                t = tile(4)
                t.att_read = seen(i - 2)
                gate(t)

        turns_sp(pe, turn)

        def tr_hs(m, p, j, r):
            pe.wait_ge(hs_loaded[r], (j + 1) * 16)
            for c in range(KC):
                ins = pe.transpose(bank[:, p, c * P:(c + 1) * P], hs[:, r, c * P:(c + 1) * P], ident[:, :])
            ins.then_inc(F["h2_transposed"], 1)

        def weights_of(m):
            return pe.value_load(slot_w[0:1, bass.ds(m, 1)], min_val=0, max_val=(NE - 1) * EW)

        def gate_up(m, p, w):
            pe.wait_ge(F["h2_l_ready"], m + 1)
            for c in range(KC):
                w_h, w_l = (t[:, c * 2 * FI:][:, bass.ds(w, 2 * FI)] for t in (we_h, we_l))
                ins = three(bank[:, 2 + p, 0:2 * FI], hst_h[:, p, c, :], hst_l[:, p, c, :], w_h, w_l, c == 0, c == KC - 1)
            ins.then_inc(F["gate_up"], 1)

        def tr_act(m, p):
            pe.wait_ge(F["act_ready"], m + 1)
            pe.transpose(bank[:, 4 + p, 0:P], act_u[:, p, 0:FA], ident[:, :])
            pe.transpose(bank[0:FB, 4 + p, P:2 * P], act_u[:, p, FA:FI], ident[:, :]).then_inc(F["act_transposed"], 1)

        def down(m, p, w):
            pe.wait_ge(F["au_l_ready"], m * 2 + 2)
            need(pe, F["y_ready"], m - 1)
            for n, rows in enumerate((FA, FB)):
                w_h, w_l = (t[0:rows, 2 * KC * FI + n * D:][:, bass.ds(w, D)] for t in (we_h, we_l))
                ins = three(bank[:, 6 + p, 0:D], au_h[0:rows, p, n, :], au_l[0:rows, p, n, :], w_h, w_l, n == 0, n == 1)
            ins.then_inc(F["y_done"], 1)

        pe.wait_ge(plan, PLAN)
        pe.wait_ge(S["we_ready"], NT)
        pe.wait_ge(S["ht_ready"], NT)
        pe.wait_ge(R["filled_new"], NT // 2)

        found = {}

        def turn2(j, r, static):
            i = j * RING + r
            gates = not static or 0 <= i - 1 < NSLOT
            if gates:
                found[r] = weights_of(i - 1)
            if not static or i < NSLOT:
                tr_hs(i, r % 2, j, r)
            if not static or 0 <= i - 2 < NSLOT:
                tr_act(i - 2, r % 2)
            if gates:
                gate_up(i - 1, (r - 1) % 2, found[r])
            if not static or 0 <= i - 3 < NSLOT:
                down(i - 3, (r - 3) % 2, found[r - 2] if r >= 2 else weights_of(i - 3))

        slots(pe, turn2)


PLAN = 23


def turns_sp(eng, turn):
    first, last = 2, NT // SKEW - 1
    for j in range(first):
        for s in range(SKEW):
            turn(j, s)
    with eng.Fori(first, last) as j:
        for s in range(SKEW):
            turn(j, s)
    for i in range(last * SKEW, LAST):
        turn(i // SKEW, i % SKEW)


def slots(eng, turn):
    for r in range(RING):
        turn(0, r, True)
    with eng.Fori(1, NSLOT // RING) as j:
        for r in range(RING):
            turn(j, r, False)
    for r in range(3):
        turn(NSLOT // RING, r, True)


def kernel(**inputs):
    import concourse.bacc as bacc
    from concourse.bass_utils import run_bass_kernel_spmd

    def get(name):
        return np.ascontiguousarray(inputs[name])

    def weight(name):
        return get(name).T.reshape(KC, P, D).transpose(1, 0, 2)

    v_order = np.arange(D).reshape(NPAIR, 2, HD).transpose(1, 0, 2).reshape(D)
    w_v = weight("L0_xattn_v_img_w")[:, :, v_order]
    w_proj = np.stack([weight("L0_xattn_q_w"), weight("L0_xattn_k_img_w"), w_v, weight("L0_xattn_o_w")], 1)
    bias = np.concatenate([get("L0_xattn_q_b"), get("L0_xattn_k_img_b"), get("L0_xattn_v_img_b")[v_order],
                           get("L0_xattn_o_b")])
    w1 = get("L0_ffn_w1").reshape(NE, 2 * FI, KC, P).transpose(3, 0, 2, 1).reshape(P, NE, KC * 2 * FI)
    w2 = get("L0_ffn_w2").transpose(2, 0, 1)
    w2b = np.zeros((P, NE, D), w2.dtype)
    w2b[:FB] = w2[FA:]
    w_exp = np.concatenate([w1, w2[:FA], w2b], 2).reshape(P, NT, WS).transpose(1, 0, 2).reshape(NT * P, WS)
    ctx_t = get("ctx_2048").reshape(NT, P, KC, P).transpose(0, 3, 2, 1).reshape(NT * P, KC * P)
    w_gate = get("L0_ffn_gate_w").T.reshape(KC, P, NE).transpose(1, 0, 2).reshape(P, KC * NE)
    arrays = {
        "x": get("x").reshape(T, D),
        "ctx_t": ctx_t,
        "w_proj": w_proj.reshape(P, 4 * KC * D),
        "w_exp": w_exp,
        "w_gate": w_gate,
        "bias": np.stack([bias, bias]),
        "norm_q": get("L0_xattn_norm_q_w"),
        "norm_k": get("L0_xattn_norm_k_img_w"),
    }
    arrays = {n: np.ascontiguousarray(a) for n, a in arrays.items()}
    nc = bacc.Bacc("TRN2", target_bir_lowering=False, num_devices=1)
    args = [nc.dram_tensor(n, a.shape, mybir.dt.from_np(a.dtype), kind="ExternalInput").ap()
            for n, a in arrays.items()]
    out = nc.dram_tensor("out", (T, D), F32, kind="ExternalOutput").ap()
    build(nc, *args, out)
    r = run_bass_kernel_spmd(nc, [arrays], core_ids=[0])
    return r.results[0]["out"].reshape(B, L, D)
```

```python
from contextlib import ExitStack

import numpy as np

import concourse.bass as bass
from concourse import mybir

ALU = mybir.AluOpType
ACT = mybir.ActivationFunctionType
AX = mybir.AxisListType
F32 = mybir.dt.float32
F32R = mybir.dt.float32r
F16 = mybir.dt.float16
BF16 = mybir.dt.bfloat16
I32 = mybir.dt.int32
U32 = mybir.dt.uint32

P = 128
B, L, D = 64, 64, 256
NH, HD = 16, 16
NE, FI = 8, 176
KC = D // P
NB = P // L
T = B * L
NT = T // P
NPAIR = NH // 2
NQ = NPAIR // KC
KX = D + HD
VW = HD + 1
IMG_LEN = 257
assert L <= IMG_LEN

REG = T + P
ROWS = NE * REG + P
ROW = D + 2
NSLOT = 72
RING = 12
YRING = 4
assert NSLOT * P >= 2 * T + NE * (P - 1) - P + 1 and NSLOT % RING == 0 and RING % YRING == 0
EW = 2 * KC * FI + 2 * D
FA, FB = P, FI - P
WS = NE * EW // NT
assert WS * NT == NE * EW

SKEW = 4
LAST = NT + 7


class Tile:

    def __init__(self, j, s):
        self.n = j * SKEW + s
        self.slot = s % SKEW
        self.par = s % 2
        self.quad = j + s // SKEW
        self.pair = j * 2 + s // 2
        self.live = not isinstance(j, int) or 0 <= self.n < NT
        self.twins = j * 2 + s // 2


def need(eng, sem, value):
    if isinstance(value, int) and value <= 0:
        return
    eng.wait_ge(sem, value)


def need_alone(eng, passed, sem, value):
    need(eng, sem, value)
    if not isinstance(value, int):
        eng.sem_inc(passed, 1)


def build(nc, x, ctx_t, w_proj, w_exp, w_gate, bias, norm_q, norm_k, out):
    sorted_rows = nc.dram_tensor("sorted_rows", (ROWS, ROW), F32, kind="Internal").ap()
    expert_out = nc.dram_tensor("expert_out", (2 * T, D), F32, kind="Internal").ap()
    with ExitStack() as stack:
        build_in(nc, stack, x, ctx_t, w_proj, w_exp, w_gate, bias, norm_q, norm_k, out,
                 sorted_rows, expert_out)


def build_in(nc, stack, x, ctx_t, w_proj, w_exp, w_gate, bias, norm_q, norm_k, out,
             sorted_rows, expert_out):
    def sb(name, shape, dt):
        return stack.enter_context(nc.sbuf_tensor(name, shape, dt))

    def sem(name):
        return stack.enter_context(nc.semaphore(name))

    bank = stack.enter_context(nc.psum_tensor("bank", [P, 8, 512], F32))

    ident = sb("ident", [P, P], F32)
    ident_b = sb("ident_b", [P, P], BF16)
    below = sb("below", [P, P], BF16)
    ones_b = sb("ones_b", [P, P], BF16)
    head_of = sb("head_of", [32, NPAIR, P], BF16)
    expert_no = sb("expert_no", [P, NE], F32)
    slot_no = sb("slot_no", [1, NSLOT], F32)
    result_row = sb("result_row", [P, 2, NT], I32)
    half_neg = sb("half_neg", [P, 2], F32)
    one_neg = sb("one_neg", [P, 2], F32)
    zero_one = sb("zero_one", [2, 2], F32)
    ones_row_f = sb("ones_row_f", [2, P], F32)
    ones_row = sb("ones_row", [2, P], F32R)
    bias_hl = sb("bias_hl", [2, 4 * D], F32R)
    wp_h = sb("wp_h", [P, 4, KC, D], F32R)
    wp_l = sb("wp_l", [P, 4, KC, D], F32R)
    gate_w = sb("gate_w", [P, KC, NE], F32)
    qk_norm = sb("qk_norm", [P, D], F32)
    we_f = sb("we_f", [P, 2, WS], F32)
    we_h = sb("we_h", [P, NE * EW], F32R)
    we_l = sb("we_l", [P, NE * EW], F32R)

    x1 = sb("x1", [P, NT, D], F32)
    ctx_in = sb("ctx_in", [P, 2, KC * P], F32)
    stats = sb("stats", [P, 2, 6], F32)
    mean_var = sb("mean_var", [P, 2, 2], F32)
    veps = sb("veps", [P, 2, 1], F32)
    rstd = sb("rstd", [P, 2, 1], F32)
    shift = sb("shift", [P, 2, 1], F32)
    xn = sb("xn", [P, 2, D], F32)
    xt_h = sb("xt_h", [P, 2, KC, P], F32R)
    xt_l = sb("xt_l", [P, 2, KC, P], F32R)
    ct_h = sb("ct_h", [P, 2, KC, P], F32R)
    ct_l = sb("ct_l", [P, 2, KC, P], F32R)
    square = sb("square", [P, 2, D], BF16)
    sumsq = sb("sumsq", [P, 2, 2], F32)
    ms_eps = sb("ms_eps", [P, 2, 2], F32)
    r_qk = sb("r_qk", [P, 2, 2], F32)
    v_sb = sb("v_sb", [P, 2, 2, NPAIR, VW], F32)
    v_bd = sb("v_bd", [P, 2, NB, 2, NPAIR * VW], F32)
    qp_h = sb("qp_h", [P, 2, NB, KC, NQ, L], F16)
    qp_l = sb("qp_l", [P, 2, NB, KC, NQ, L], F16)
    late = sb("late", [P, 4096], F32)
    qn = late[:, 0:D]
    kn = late[:, D:D + 2 * 2 * KX].rearrange("p (b x) -> p b x", b=2)
    kp = late[:, D + 4 * KX:D + 4 * KX + 4 * 2 * P].bitcast(F16).rearrange(
        "p (u n b c q l) -> p u n b c q l", u=2, n=2, b=NB, c=KC, q=2)
    row_max = sb("row_max", [P, 2, NH], F32)
    neg_max = sb("neg_max", [P, 2, 2 * NH], BF16)
    neg_max_t = sb("neg_max_t", [2 * NH, 2, P], BF16)
    probs = sb("probs", [P, 2, NB * NPAIR * L], F32)
    wp_f = probs[:, :, :].rearrange("p a b -> p (a b)")
    r_sum = sb("r_sum", [P, 2, NH], F32)
    att = sb("att", [P, 2, NH, HD], F32)
    at_h = sb("at_h", [P, 2, KC, P], F32R)
    at_l = sb("at_l", [P, 2, KC, P], F32R)
    stats2 = sb("stats2", [P, 2, 6], F32)
    mean_var2 = sb("mean_var2", [P, 2, 2], F32)
    veps2 = sb("veps2", [P, 2, 1], F32)
    rstd2 = sb("rstd2", [P, 2, 1], F32)
    row = sb("row", [P, 2, SKEW, ROW], F32)
    ht = sb("ht", [P, 2, KC, P], F32)
    logit = sb("logit", [P, 2, NE], F32)
    top8 = sb("top8", [P, 2, 8], F32)
    top8_no = sb("top8_no", [P, 2, 8], U32)
    top_no = sb("top_no", [P, 2, 2], F32)
    gap = sb("gap", [P, 2, 2], F32)
    e_gap = sb("e_gap", [P, 2, 2], F32)
    one_e = sb("one_e", [P, 2], F32)
    chosen = sb("chosen", [P, 2, 2, 2, NE], F32)
    chosen_b = sb("chosen_b", [P, 2, 2, NE], BF16)
    counts = sb("counts", [P, 3 * NE], F32)
    filled = sb("filled", [P, NE], F32)
    place = sb("place", [P, 2, NE], F32)
    place_of = sb("place_of", [P, 2, 2, NE], F32)
    place_f = sb("place_f", [P, 2, 2], F32)
    place_i = sb("place_i", [P, 2, 2, 2], I32)

    pad_rows = sb("pad_rows", [P, ROW], F32)
    region_no = sb("region_no", [1, NE], F32)
    upto = sb("upto", [1, NE, NE], F32)
    tables = square[0:1, :, :].rearrange("p a d -> p (a d)").bitcast(I32)
    slot_row, slot_w = tables[:, 0:NSLOT], tables[:, NSLOT:2 * NSLOT]

    k_norm = row[:, 1, 0, 0:D]
    bias_f = row[0:2, 0, :, 0:D]

    def words(t, pattern):
        return t.rearrange(pattern)

    hs = late[:, 0:RING * ROW].rearrange("p (r d) -> p r d", r=RING)
    hst_h, hst_l, au_h, au_l = xt_h, xt_l, at_h, at_l
    silu_g = xn[:, :, 0:FI]
    act_u = words(v_sb[:, :, :, :, :], "p a b c d -> p a (b c d)")[:, :, 0:FI]
    y_sb = words(probs[:, :, :], "p a b -> p (a b)")[:, 0:YRING * D].rearrange("p (r d) -> p r d", r=YRING)
    past = words(we_f[0:1, :, :], "p a b -> p (a b)")[:, 0:NSLOT * NE].rearrange("p (s e) -> p s e", e=NE)
    past_n = words(v_bd[0:1, :, :, :, :], "p a b c d -> p (a b c d)")[:, 0:NSLOT * NE].rearrange("p (s e) -> p s e", e=NE)
    plan_f = words(ctx_in[0:1, :, :], "p a b -> p (a b)")
    slot_e = plan_f[:, 0:3 * NSLOT].rearrange("p (a s) -> p a s", a=3)
    cum_of, cum, tiles, tiles_i, count_i, pad_at = (
        plan_f[:, 3 * NSLOT:][:, n * NE:(n + rows) * NE] for n, rows in ((0, NE), (8, 2), (10, 1), (11, 1), (12, 1), (13, 1)))
    cum_of = cum_of.rearrange("p (e f) -> p e f", e=NE)
    cum = cum.rearrange("p (a e) -> p a e", a=2)
    tiles_i, count_i, pad_at = tiles_i.bitcast(I32), count_i.bitcast(I32), pad_at.bitcast(I32)
    fin_in = [we[:, n * 4 * D:(n + 1) * 4 * D].bitcast(F32).rearrange("p (k m d) -> p k m d", k=2, m=2)
              for we in (we_h, we_l) for n in range(NT // 4)]

    count_cols = slice(P, P + 3 * NE)

    def flat(t):
        return t.rearrange("p q l -> p (q l)")

    def k_parts(t, part):
        return kp[:, t.par, part].rearrange("p b c q l -> p (c q) b l")

    def q_part(dst, t, g):
        return dst[g * 2 * HD:(g + 1) * 2 * HD, t.par, :, :, g, :].rearrange("p b c l -> p c b l")

    def q_bank(g):
        return kq_bank[g * 2 * HD:(g + 1) * 2 * HD, 0:D].rearrange("p (c b l) -> p c b l", c=KC, b=NB)

    x_first, x_second, x_third, x_rest = sem("x_first"), sem("x_second"), sem("x_third"), sem("x_rest")
    w_loaded = [sem("w_qk_loaded"), sem("w_vo_loaded")]
    bias_loaded, norms_loaded, gate_w_loaded = sem("bias_loaded"), sem("norms_loaded"), sem("gate_w_loaded")
    ctx_loaded = [sem(f"ctx_loaded{p}") for p in range(2)]
    we_loaded = [sem(f"we_loaded{p}") for p in range(2)]
    v_spread = [sem(f"v_spread{p}") for p in range(2)]
    row_sent = [sem(f"row_sent{s}") for s in range(SKEW)]
    pads_sent = sem("pads_sent")
    sp_passed, pool_passed, dve_passed, pe_passed = (sem(n) for n in ("sp_passed", "pool_passed", "dve_passed", "pe_passed"))
    pool_setup = sem("pool_setup")
    dve_setup = sem("dve_setup")
    q_cleared = sem("q_cleared")
    w_hi_ready, bias_parts_ready = sem("w_hi_ready"), sem("bias_parts_ready")
    names = """ln1_stats ln1_mean ln1_veps ln1_rstd ln1_shift xn_ready x_transposed xt_h_ready xt_l_ready
        ct_h_ready ct_ready k_projected projected v_ready q_squared k_squared qk_veps qk_rstd qn_ready kn_ready
        k_transposed k_h_ready k_l_ready q_transposed q_h_ready q_l_ready max_scored max_found neg_hi_ready neg_max_ready
        neg_max_transposed neg_max_t_ready scored probs_ready weighed sum_inverted att_ready
        att_transposed at_h_ready at_l_ready o_projected x1_ready ln2_stats ln2_mean ln2_veps
        ln2_rstd row_ready row2_ready h_transposed ht_ready gated logit_ready we_h_ready we_ready ids_set""".split()
    S = {n: sem(n) for n in names}
    pair_names = "tops no_ready gap_ready choice_ready e_gap_ready routed counts_ready place_ready filled_new place_sel place_sum place_set weight_set1 weight_set2 weight_set3".split()
    R = {n: sem(n) for n in pair_names}
    plan = sem("plan")
    hs_loaded = [sem(f"hs_loaded{r}") for r in range(RING)]
    y_sent = [sem(f"y_sent{r}") for r in range(YRING)]
    names2 = """h2_transposed h2_h_ready h2_l_ready gate_up silu_ready act_ready act_transposed
        au_h_ready au_l_ready y_done y_ready""".split()
    F = {n: sem(n) for n in names2}
    fin_loaded = [sem(f"fin_loaded{g}") for g in range(NT // 2)]
    fin_stored = sem("fin_stored")
    fin_sum1, fin_sum2 = sem("fin_sum1"), sem("fin_sum2")

    tr_bank = bank[:, 0, :]
    qv_bank = bank[:, 1, :]
    k_bank = bank[:, 2, :]
    kq_bank = bank[:, 3, :]
    score_bank = bank[:, 4:6, :].rearrange("p a b -> p (a b)")
    av_bank = bank[:, 6, :]
    mo_bank = bank[:, 7, :]

    block = stack.enter_context(nc.Block())

    SETUP_POOL = 21
    SETUP_POOL_FIRST = 6
    SETUP_DVE = 10
    SETUP_DVE_QK = 8
    WQK = 2 * KC * D

    def send_pads(eng, first):
        eng.wait_ge(plan, 1)
        for e in range(first, NE, 2):
            at = eng.value_load(pad_at[0:1, e:e + 1], min_val=0, max_val=NE * REG)
            eng.dma_start(sorted_rows[bass.ds(at, P), :], pad_rows[:, :]).then_inc(pads_sent, 16)

    @block.sync
    def _(sp):
        x_v = x.rearrange("(t p) d -> p t d", p=P)
        sp.dma_start(x1[:, 0:2, :], x_v[:, 0:2, :]).then_inc(x_first, 16)
        sp.dma_start(wp_f[:, 0:WQK], w_proj[:, 0:WQK]).then_inc(w_loaded[0], 16)
        sp.dma_start(ctx_in[:, 0, :], ctx_t[0:P, :]).then_inc(ctx_loaded[0], 16)
        sp.dma_start(bias_f, bias.rearrange("r (m d) -> r m d", m=4)).then_inc(bias_loaded, 16)
        sp.dma_start(wp_f[:, WQK:2 * WQK], w_proj[:, WQK:2 * WQK]).then_inc(w_loaded[1], 16)
        sp.dma_start(qk_norm[:, :], norm_q.partition_broadcast(P)).then_inc(norms_loaded, 16)
        sp.dma_start(k_norm, norm_k.partition_broadcast(P)).then_inc(norms_loaded, 16)
        sp.dma_start(ctx_in[:, 1, :], ctx_t[P:2 * P, :]).then_inc(ctx_loaded[1], 16)
        sp.dma_start(we_f[:, 0, :], w_exp[0:P, :]).then_inc(we_loaded[0], 16)
        sp.dma_start(x1[:, 2:8, :], x_v[:, 2:8, :]).then_inc(x_second, 16)
        sp.dma_start(we_f[:, 1, :], w_exp[P:2 * P, :]).then_inc(we_loaded[1], 16)
        sp.dma_start(gate_w[:, :, :], w_gate.rearrange("p (c e) -> p c e", c=KC)).then_inc(gate_w_loaded, 16)

        def load_ctx(t):
            need_alone(sp, sp_passed, S["ct_ready"], t.n - 1)
            sp.dma_start(ctx_in[:, t.par, :], ctx_t[bass.ds(t.n * P, P), :]).then_inc(ctx_loaded[t.par], 16)

        def load_weights(t):
            need_alone(sp, sp_passed, S["we_ready"], t.n - 1)
            sp.dma_start(we_f[:, t.par, :], w_exp[bass.ds(t.n * P, P), :]).then_inc(we_loaded[t.par], 16)

        def spread_v(t):
            need_alone(sp, sp_passed, S["v_ready"], t.n + 1)
            need_alone(sp, sp_passed, S["weighed"], t.n - 1)
            for b in range(NB):
                for q in range(2):
                    sp.dma_start(v_bd[q * L:(q + 1) * L, t.par, b, q, :],
                                 v_sb[b * L:(b + 1) * L, t.par, q, :, :].rearrange("p g d -> p (g d)")
                                 ).then_inc(v_spread[t.par], 16)

        sp.wait_ge(dve_setup, SETUP_DVE)
        sp.wait_ge(pool_setup, SETUP_POOL)
        sp.dma_start(sorted_rows[NE * REG:ROWS, :], pad_rows[:, :]).then_inc(pads_sent, 16)

        def turn(j, s):
            if Tile(j, s + 2).live:
                load_ctx(Tile(j, s + 2))
            if Tile(j, s + 1).live and (not isinstance(j, int) or j * SKEW + s + 1 >= 2):
                load_weights(Tile(j, s + 1))
            if Tile(j, s).live:
                spread_v(Tile(j, s))
            if isinstance(j, int) and j * SKEW + s == 1:
                sp.dma_start(x1[:, 8:16, :], x_v[:, 8:16, :]).then_inc(x_third, 16)
            if isinstance(j, int) and j * SKEW + s in (3, 5):
                at = 16 if s == 3 else 24
                sp.dma_start(x1[:, at:at + 8, :], x_v[:, at:at + 8, :]).then_inc(x_rest, 16)

        turns_sp(sp, turn)

        send_pads(sp, 0)
        sp.wait_ge(plan, PLAN)

        def row_of(slot):
            return sp.value_load(slot_row[0:1, bass.ds(slot, 1)], min_val=0, max_val=NE * REG)

        def load_slot(r, at):
            sp.dma_start(hs[:, r, :], sorted_rows[bass.ds(at, P), :]).then_inc(hs_loaded[r], 16)

        first_rows = [row_of(r) for r in range(RING)]
        sp.wait_ge(pads_sent, 16 * (NE + 1))
        for s in range(SKEW):
            sp.wait_ge(row_sent[s], 2 * 16 * (NT // SKEW))
        for r, at in enumerate(first_rows):
            load_slot(r, at)
        with sp.Fori(1, NSLOT // RING) as j:
            for r in range(RING):
                need_alone(sp, sp_passed, y_sent[r % YRING], ((j - 1) * (RING // YRING) + r // YRING + 1) * 16)
                load_slot(r, row_of(j * RING + r))
        for r in range(YRING):
            sp.wait_ge(y_sent[r], 16 * NSLOT // YRING)

        ev = expert_out.rearrange("(k t p) d -> p k t d", k=2, p=P)
        for g in range(NT // 2):
            for k in range(2):
                sp.dma_start(fin_in[g][:, k, :, :], ev[:, k, 2 * g:2 * g + 2, :]).then_inc(fin_loaded[g], 16)
        sp.wait_ge(fin_stored, 16 * (NT // 2))

    @block.gpsimd
    def _(pool):
        done = [0]

        def setup(ins):
            done[0] += 1
            ins.then_inc(pool_setup, 1)

        def after():
            pool.wait_ge(pool_setup, done[0])

        def ctx_lo(t):
            need_alone(pool, pool_passed, S["ct_h_ready"], t.n + 1)
            need_alone(pool, pool_passed, S["projected"], t.n - 1)
            src = ctx_in[:, t.par, :].rearrange("p (c n) -> p c n", c=KC)
            pool.tensor_tensor(ct_l[:, t.par, :, :], src, ct_h[:, t.par, :, :].bitcast(F32),
                               ALU.subtract).then_inc(S["ct_ready"], 1)

        def weights_lo(t):
            need_alone(pool, pool_passed, S["we_h_ready"], t.n + 1)
            cols = bass.ds(t.n * WS, WS)
            pool.tensor_tensor(we_l[:, cols], we_f[:, t.par, :], we_h[:, cols].bitcast(F32),
                               ALU.subtract).then_inc(S["we_ready"], 1)

        def inv_sqrt(t, out_, tmp, in_, scale, eps, ready, mid, done_):
            need_alone(pool, pool_passed, ready, t.n + 1)
            pool.tensor_scalar(tmp, in_, scale, eps, ALU.mult, ALU.add).then_inc(mid, 1)
            need_alone(pool, pool_passed, mid, t.n + 1)
            pool.tensor_tensor(out_, tmp, half_neg[:, 0:tmp.shape[1]], ALU.pow).then_inc(done_, 1)

        def ln1(t):
            need_alone(pool, pool_passed, S["xn_ready"], t.n - 1)
            inv_sqrt(t, rstd[:, t.par, :], veps[:, t.par, :], mean_var[:, t.par, 1:2], 1.0, 1e-5,
                     S["ln1_mean"], S["ln1_veps"], S["ln1_rstd"])
            need_alone(pool, pool_passed, S["ln1_rstd"], t.n + 1)
            pool.tensor_scalar(shift[:, t.par, :], mean_var[:, t.par, 0:1], rstd[:, t.par, :], -1.0, ALU.mult, ALU.mult
                               ).then_inc(S["ln1_shift"], 1)

        def qk_rms(t):
            need_alone(pool, pool_passed, S["qn_ready"], t.n - 1)
            need_alone(pool, pool_passed, S["kn_ready"], t.n - 1)
            need_alone(pool, pool_passed, S["q_squared"], t.n + 1)
            inv_sqrt(t, r_qk[:, t.par, :], ms_eps[:, t.par, :], sumsq[:, t.par, :], 1.0 / D, 1e-6,
                     S["k_squared"], S["qk_veps"], S["qk_rstd"])

        def ln2(t):
            need_alone(pool, pool_passed, S["row_ready"], t.n - 1)
            inv_sqrt(t, rstd2[:, t.par, :], veps2[:, t.par, :], mean_var2[:, t.par, 1:2], 1.0, 1e-5,
                     S["ln2_mean"], S["ln2_veps"], S["ln2_rstd"])

        def weights(a, b, pp):
            need_alone(pool, pool_passed, R["e_gap_ready"], a.pair + 1)
            need_alone(pool, pool_passed, S["row2_ready"], b.n + 1)
            w = row[:, :, a.slot:a.slot + 2, D + 1:D + 2].rearrange("p k m d -> p k (m d)")
            pool.tensor_scalar(one_e[:, :], e_gap[:, pp, :], 1.0, 1.0, ALU.mult, ALU.add).then_inc(R["weight_set1"], 1)
            need_alone(pool, pool_passed, R["weight_set1"], a.pair + 1)
            pool.tensor_tensor(w[:, 0, :], one_e[:, :], one_neg[:, :], ALU.pow).then_inc(R["weight_set2"], 1)
            need_alone(pool, pool_passed, R["weight_set2"], a.pair + 1)
            pool.tensor_tensor(w[:, 1, :], e_gap[:, pp, :], w[:, 0, :], ALU.mult).then_inc(R["weight_set3"], 1)

        def send(t):
            need_alone(pool, pool_passed, S["row2_ready"], t.n + 1)
            pool.tensor_copy(row[:, :, t.slot, D:D + 1].bitcast(I32), result_row[:, :, bass.ds(t.n, 1)]
                             ).then_inc(S["ids_set"], 1)
            need_alone(pool, pool_passed, S["ids_set"], t.n + 1)
            need_alone(pool, pool_passed, R["place_set"], t.pair + 1)
            need_alone(pool, pool_passed, R["weight_set3"], t.pair + 1)
            for k in range(2):
                pool.indirect_dma_start(
                    sorted_rows, bass.IndirectOffsetOnAxis(ap=place_i[:, t.slot // 2, k, t.par:t.par + 1], axis=0),
                    row[:, k, t.slot, :], None, bounds_check=ROWS - 1, oob_is_err=False
                ).then_inc(row_sent[t.slot], 16)

        def turn(j, s):
            if Tile(j, s + 1).live:
                ctx_lo(Tile(j, s + 1))
            if Tile(j, s + 2).live:
                ln1(Tile(j, s + 2))
            if Tile(j, s).live:
                qk_rms(Tile(j, s))
            if s % 2 == 1 and Tile(j, s - 7).live:
                weights(Tile(j, s - 7), Tile(j, s - 6), (s - 7) // 2 % 2)
            if Tile(j, s - 7).live:
                send(Tile(j, s - 7))
            if Tile(j, s - 3).live:
                ln2(Tile(j, s - 3))
            if Tile(j, s).live:
                weights_lo(Tile(j, s))

        setup(pool.memset(ident[:, :], 0.0))
        setup(pool.memset(half_neg[:, :], -0.5))
        setup(pool.memset(one_neg[:, :], -1.0))
        setup(pool.iota(zero_one[:, 1:2], [[0, 1]], base=0, channel_multiplier=1,
                        allow_small_or_imprecise_dtypes=True))
        pool.wait_ge(pool_setup, 1)
        setup(pool.affine_select(out=ident[:, :], in_=ident[:, :], compare_op=ALU.not_equal, fill=1.0,
                                 base=0, pattern=[[-1, P]], channel_multiplier=1))
        setup(pool.memset(ones_b[:, :], 1.0))
        assert done[0] == SETUP_POOL_FIRST, done[0]
        setup(pool.memset(below[:, :], 0.0))
        setup(pool.memset(head_of[:, :, :], 0.0))
        setup(pool.memset(upto[:, :, :], 1.0))
        after()
        setup(pool.affine_select(out=below[:, :], in_=below[:, :], compare_op=ALU.is_ge, fill=1.0,
                                 base=0, pattern=[[-1, P]], channel_multiplier=1))
        setup(pool.affine_select(out=upto[:, :, :], in_=upto[:, :, :], compare_op=ALU.is_ge, fill=0.0,
                                 base=0, pattern=[[1, NE], [-1, NE]], channel_multiplier=0))
        ln1(Tile(0, 0))
        ln1(Tile(0, 1))
        ctx_lo(Tile(0, 0))
        for base in (0, -NH):
            after()
            v = head_of[:, :, :].rearrange("r g (q m) -> r g q m", q=2)
            setup(pool.affine_select(out=v, in_=v, compare_op=ALU.not_equal, fill=1.0, base=base,
                                     pattern=[[-2, NPAIR], [-1, 2], [0, L]], channel_multiplier=1))
        setup(pool.tensor_copy(ident_b[:, :], ident[:, :]))
        setup(pool.iota(expert_no[:, :], [[1, NE]], base=0, channel_multiplier=0,
                        allow_small_or_imprecise_dtypes=True))
        setup(pool.iota(slot_no[:, :], [[1, NSLOT]], base=0, channel_multiplier=0,
                        allow_small_or_imprecise_dtypes=True))
        setup(pool.iota(filled[:, :], [[REG, NE]], base=0, channel_multiplier=0,
                        allow_small_or_imprecise_dtypes=True))
        setup(pool.iota(region_no[:, :], [[REG, NE]], base=0, channel_multiplier=0,
                        allow_small_or_imprecise_dtypes=True))
        setup(pool.iota(result_row[:, :, :], [[T, 2], [P, NT]], base=0, channel_multiplier=1))
        setup(pool.memset(pad_rows[:, :], 0.0))
        after()
        setup(pool.iota(pad_rows[:, D:D + 1].bitcast(I32), [[0, 1]], base=2 * T, channel_multiplier=1))
        assert done[0] == SETUP_POOL, done[0]
        for q in (qp_h, qp_l):
            pool.memset(q[:, :, :, :, :, :].rearrange("p u b c g l -> p (u b c g l)").bitcast(F32), 0.0
                        ).then_inc(q_cleared, 1)
        turns_sp(pool, turn)

        def send_y(j, r):
            need_alone(pool, pool_passed, F["y_ready"], j * RING + r + 1)
            pool.indirect_dma_start(
                expert_out, bass.IndirectOffsetOnAxis(ap=hs[:, r, D:D + 1].bitcast(U32), axis=0),
                y_sb[:, r % YRING, :], None, bounds_check=2 * T - 1, oob_is_err=False
            ).then_inc(y_sent[r % YRING], 16)

        with pool.Fori(0, NSLOT // RING) as j:
            for r in range(RING):
                send_y(j, r)

    @block.scalar
    def _(act):
        def xt_hi(t):
            act.wait_ge(S["x_transposed"], t.n + 1)
            need(act, S["projected"], t.n - 1)
            act.copy(xt_h[:, t.par, :, :], tr_bank[:, 0:D].rearrange("p (c n) -> p c n", c=KC)
                     ).then_inc(S["xt_h_ready"], 1)

        def ln1_norm(t):
            act.wait_ge(S["ln1_shift"], t.n + 1)
            need(act, S["x_transposed"], t.n - 1)
            act.activation(xn[:, t.par, :], x1[:, t.at, :], ACT.Identity, bias=shift[:, t.par, :],
                           scale=rstd[:, t.par, :]).then_inc(S["xn_ready"], 1)

        def k_hi(t):
            act.wait_ge(S["k_transposed"], t.n + 1)
            need(act, S["scored"], t.n - 1)
            act.copy(k_parts(t, 0), kq_bank.rearrange("p (x b l) -> p x b l", b=NB, l=L)
                     ).then_inc(S["k_h_ready"], 1)

        def q_hi(t):
            act.wait_ge(S["q_transposed"], t.n + 1)
            if t.first:
                act.wait_ge(q_cleared, 2)
            need(act, S["scored"], t.n - 1)
            for g in range(NQ):
                act.copy(q_part(qp_h, t, g), q_bank(g)).then_inc(S["q_h_ready"], 1)

        def ctx_hi(t):
            act.wait_ge(ctx_loaded[t.par], (t.twins + 1) * 16)
            need(act, S["projected"], t.n - 1)
            act.copy(ct_h[:, t.par, :, :], ctx_in[:, t.par, :].rearrange("p (c n) -> p c n", c=KC)
                     ).then_inc(S["ct_h_ready"], 1)

        def weights_hi(t):
            act.wait_ge(we_loaded[t.par], (t.twins + 1) * 16)
            act.copy(we_h[:, bass.ds(t.n * WS, WS)], we_f[:, t.par, :]).then_inc(S["we_h_ready"], 1)

        def row_copy(t):
            act.wait_ge(S["row_ready"], t.n + 1)
            if t.quads_ok:
                act.wait_ge(row_sent[t.slot], t.quad * 32)
            act.copy(row[:, 1, t.slot, 0:D], row[:, 0, t.slot, 0:D]).then_inc(S["row2_ready"], 1)

        def neg_max_rows(t):
            act.wait_ge(S["neg_max_transposed"], t.n + 1)
            need(act, S["scored"], t.n - 1)
            act.copy(neg_max_t[:, t.par, :], mo_bank[0:2 * NH, 0:P // 2].bitcast(BF16)
                     ).then_inc(S["neg_max_t_ready"], 1)

        def k_square(t):
            act.wait_ge(S["k_projected"], t.n + 1)
            need(act, S["k_squared"], t.n)
            need(act, S["qk_veps"], t.n - 1)
            act.activation(square[:, 1, :], k_bank[:, 0:D], ACT.Square,
                           accum_out=sumsq[:, t.par, 1:2]).then_inc(S["k_squared"], 1)

        def q_square(t):
            act.wait_ge(S["projected"], t.n + 1)
            need(act, S["q_squared"], t.n)
            act.activation(square[:, 0, :], qv_bank[:, 0:D], ACT.Square,
                           accum_out=sumsq[:, t.par, 0:1]).then_inc(S["q_squared"], 1)

        def v_copy(t):
            if t.twins_ok:
                act.wait_ge(v_spread[t.par], t.twins * 64)
            else:
                act.wait_ge(dve_setup, SETUP_DVE)
            act.copy(v_sb[:, t.par, :, :, 0:HD],
                     qv_bank[:, D:2 * D].rearrange("p (q g d) -> p q g d", q=2, g=NPAIR)
                     ).then_inc(S["v_ready"], 1)

        def att_hi(t):
            act.wait_ge(S["att_transposed"], t.n + 1)
            need(act, S["o_projected"], t.n - 1)
            act.copy(at_h[:, t.par, :, :], av_bank[:, 0:D].rearrange("p (c n) -> p c n", c=KC)
                     ).then_inc(S["at_h_ready"], 1)

        def ht_copy(t):
            act.wait_ge(S["h_transposed"], t.n + 1)
            need(act, S["gated"], t.n - 1)
            act.copy(ht[:, t.par, :, :], tr_bank[:, 0:D].rearrange("p (c n) -> p c n", c=KC)
                     ).then_inc(S["ht_ready"], 1)

        def softmax_exp(t):
            act.wait_ge(S["scored"], t.n + 1)
            need(act, S["weighed"], t.n - 1)
            act.activation(probs[:, t.par, :], score_bank, ACT.Exp).then_inc(S["probs_ready"], 1)

        def k_scale(t):
            act.wait_ge(S["qk_rstd"], t.n + 1)
            need(act, S["k_transposed"], t.n - 1)
            dst = kn[:, t.par, :].rearrange("p (q x) -> p q x", q=2)[:, :, 0:D].rearrange(
                "p q (g r d) -> p q g r d", g=NPAIR, r=2)[:, :, :, 0, :]
            act.activation(dst, k_bank[:, 0:D].rearrange("p (g q d) -> p q g d", g=NPAIR, q=2), ACT.Copy,
                           scale=r_qk[:, t.par, 1:2]).then_inc(S["kn_ready"], 1)

        def logits_copy(t):
            act.wait_ge(S["gated"], t.n + 1)
            if t.choice is not None:
                act.wait_ge(R["no_ready"], t.choice)
            act.copy(logit[:, t.par, :], av_bank[:, 0:NE]).then_inc(S["logit_ready"], 1)

        def counts_copy(pair, used, gated):
            act.wait_ge(R["routed"], pair + 1)
            if gated is not None:
                act.wait_ge(S["gated"], gated)
            if used:
                act.wait_ge(R["filled_new"], pair)
                act.wait_ge(R["place_ready"], pair)
            act.copy(counts[:, :], av_bank[:, count_cols]).then_inc(R["counts_ready"], 1)

        def gap_exp(pair, pp):
            act.wait_ge(R["gap_ready"], pair + 1)
            act.activation(e_gap[:, pp, :], gap[:, pp, :], ACT.Exp).then_inc(R["e_gap_ready"], 1)

        def turn(j, s):
            def tile(lag):
                t = Tile(j, s - lag)
                static = isinstance(j, int)
                t.twins_ok = not static or t.n >= 2
                t.quads_ok = not static or t.n >= 4
                t.at = t.n if static else bass.ds(t.n, 1)
                return t
            if tile(0).live:
                xt_hi(tile(0))
            if tile(1).live:
                k_hi(tile(1))
            if tile(-1).live:
                ln1_norm(tile(-1))
            if tile(-1).live:
                ctx_hi(tile(-1))
            if tile(1).live:
                t = tile(1)
                t.first = isinstance(j, int) and t.n == 0
                q_hi(t)
            if tile(2).live:
                neg_max_rows(tile(2))
            if tile(0).live:
                k_square(tile(0))
            if tile(0).live:
                q_square(tile(0))
            if tile(3).live:
                att_hi(tile(3))
            if tile(0).live:
                v_copy(tile(0))
            if tile(0).live:
                weights_hi(tile(0))
                k_scale(tile(0))
            if tile(4).live:
                row_copy(tile(4))
            if tile(4).live:
                ht_copy(tile(4))
            if tile(2).live:
                softmax_exp(tile(2))
            if s % 2 == 0 and tile(6).live:
                counts_copy(tile(6).pair, not isinstance(j, int) or tile(6).n >= 2,
                            tile(4).n + 1 if tile(4).live else None)
                gap_exp(tile(6).pair, (s - 6) // 2 % 2)
            if tile(4).live:
                t = tile(4)
                chosen_for = (j * 2 + (s - 6) // 2 + 1) * 3
                t.choice = chosen_for if not isinstance(j, int) or t.n >= 2 else None
                logits_copy(t)

        def split_hi(n):
            act.wait_ge(w_loaded[n], 16)
            act.copy(wp_h[:, 2 * n:2 * n + 2, :, :].rearrange("p m c n -> p (m c n)"), wp_f[:, n * WQK:(n + 1) * WQK]
                     ).then_inc(w_hi_ready, 1)

        t = Tile(0, 0)
        t.at = 0
        split_hi(0)
        ctx_hi(t)
        act.wait_ge(bias_loaded, 16)
        act.copy(bias_hl[:, :].rearrange("r (m d) -> r m d", m=4), bias_f).then_inc(bias_parts_ready, 1)
        act.wait_ge(pool_setup, SETUP_POOL_FIRST)
        act.activation(bias_f, bias_f, ACT.Copy, scale=zero_one[:, 1:2]).then_inc(bias_parts_ready, 1)
        ln1_norm(t)
        split_hi(1)
        turns_sp(act, turn)
        send_pads(act, 1)

        def hst_hi(m, p):
            act.wait_ge(F["h2_transposed"], m + 1)
            need(act, F["gate_up"], m - 1)
            act.copy(hst_h[:, p, :, :], bank[:, p, 0:D].rearrange("p (c n) -> p c n", c=KC)
                     ).then_inc(F["h2_h_ready"], 1)

        def silu(m, p):
            act.wait_ge(F["gate_up"], m + 1)
            need(act, F["act_ready"], m - 1)
            act.activation(silu_g[:, p, :], bank[:, 2 + p, 0:FI], ACT.Silu).then_inc(F["silu_ready"], 1)

        def au_hi(m, p):
            act.wait_ge(F["act_transposed"], m + 1)
            need(act, F["y_done"], m - 1)
            act.copy(au_h[:, p, 0, :], bank[:, 4 + p, 0:P]).then_inc(F["au_h_ready"], 1)
            act.copy(au_h[0:FB, p, 1, :], bank[0:FB, 4 + p, P:2 * P]).then_inc(F["au_h_ready"], 1)

        def y_copy(m, r, reuse, q):
            act.wait_ge(F["y_done"], m + 1)
            if reuse is not None:
                act.wait_ge(y_sent[r], reuse)
            act.copy(y_sb[:, r, :], bank[:, 6 + q, 0:D]).then_inc(F["y_ready"], 1)

        def turn2(j, r, static):
            i = j * RING + r
            if not static or i < NSLOT:
                hst_hi(i, r % 2)
            if not static or 0 <= i - 1 < NSLOT:
                silu(i - 1, (r - 1) % 2)
            if not static or 0 <= i - 2 < NSLOT:
                au_hi(i - 2, r % 2)
            if not static or 0 <= i - 3 < NSLOT:
                m = i - 3
                sent_before = (j * (RING // YRING) + (r - 3) // YRING) * 16
                y_copy(m, (r - 3) % YRING, sent_before if not static or m >= YRING else None, (r - 3) % 2)

        slots(act, turn2)

        ov = out.rearrange("(t p) d -> p t d", p=P)
        for g in range(NT // 2):
            act.wait_ge(fin_sum2, g + 1)
            act.dma_start(ov[:, 2 * g:2 * g + 2, :], fin_in[g][:, 0, :, :]).then_inc(fin_stored, 16)

    @block.vector
    def _(dve):
        done = [0]

        def setup(ins):
            done[0] += 1
            ins.then_inc(dve_setup, 1)

        def after():
            dve.wait_ge(dve_setup, done[0])

        bias_h4 = bias_hl[:, :].rearrange("r (m d) -> r m d", m=4)
        setup(dve.memset(ones_row_f[:, :], 1.0))
        setup(dve.memset(v_sb[:, :, :, :, :], 1.0))
        setup(dve.memset(v_bd[:, :, :, :, :], 0.0))
        setup(dve.memset(late[:, D:D + 4 * KX], 0.0))
        after()
        setup(dve.tensor_copy(ones_row[:, :], ones_row_f[:, :]))

        def split_lo(n):
            dve.wait_ge(w_hi_ready, n + 1)
            setup(dve.tensor_tensor(wp_l[:, 2 * n:2 * n + 2, :, :].rearrange("p m c n -> p (m c n)"),
                                    wp_f[:, n * WQK:(n + 1) * WQK],
                                    wp_h[:, 2 * n:2 * n + 2, :, :].rearrange("p m c n -> p (m c n)").bitcast(F32),
                                    ALU.subtract))

        def split_biases():
            dve.wait_ge(pool_setup, SETUP_POOL_FIRST)
            setup(dve.tensor_scalar(zero_one[:, 0:1], zero_one[:, 1:2], -2.0, 1.0, ALU.mult, ALU.add))
            after()
            dve.wait_ge(bias_parts_ready, 2)
            setup(dve.scalar_tensor_tensor(bias_h4, bias_h4.bitcast(F32), zero_one[:, 0:1], bias_f, ALU.mult, ALU.add))

        def join_norms():
            dve.wait_ge(norms_loaded, 32)
            setup(dve.scalar_tensor_tensor(qk_norm[:, :], qk_norm[:, :], HD ** -0.5, k_norm, ALU.mult, ALU.mult))

        def ln1_stats(t, loaded):
            if loaded is not None:
                dve.wait_ge(loaded, 32 if loaded is x_rest else 16)
            dve.bn_stats(stats[:, t.par, :], x1[:, t.at, :]).then_inc(S["ln1_stats"], 1)

        def ln1_mean(t):
            need(dve, S["xn_ready"], t.n - 1)
            need_alone(dve, dve_passed, S["ln1_stats"], t.n + 1)
            dve.bn_aggr(mean_var[:, t.par, :], stats[:, t.par, :]).then_inc(S["ln1_mean"], 1)

        def xt_lo(t):
            dve.wait_ge(S["xt_h_ready"], t.n + 1)
            need(dve, S["projected"], t.n - 1)
            dve.tensor_tensor(xt_l[:, t.par, :, :], tr_bank[:, 0:D].rearrange("p (c n) -> p c n", c=KC),
                              xt_h[:, t.par, :, :].bitcast(F32), ALU.subtract).then_inc(S["xt_l_ready"], 1)

        def k_lo(t):
            dve.wait_ge(S["k_h_ready"], t.n + 1)
            need(dve, S["scored"], t.n - 1)
            dve.tensor_tensor(k_parts(t, 1), kq_bank.rearrange("p (x b l) -> p x b l", b=NB, l=L), k_parts(t, 0), ALU.subtract).then_inc(S["k_l_ready"], 1)

        def q_lo(t):
            dve.wait_ge(S["q_h_ready"], NQ * t.n + NQ)
            need(dve, S["scored"], t.n - 1)
            for g in range(NQ):
                dve.tensor_tensor(q_part(qp_l, t, g), q_bank(g), q_part(qp_h, t, g), ALU.subtract
                                  ).then_inc(S["q_l_ready"], 1)

        def find_max(t):
            dve.wait_ge(S["max_scored"], t.n + 1)
            dve.tensor_reduce(row_max[:, t.par, :], score_bank.rearrange("p (h k) -> p h k", h=NH),
                              AX.X, ALU.max).then_inc(S["max_found"], 1)

        def neg_max_hi(t):
            dve.wait_ge(S["max_found"], t.n + 1)
            need(dve, S["neg_max_transposed"], t.n - 1)
            dve.tensor_scalar(neg_max[:, t.par, 0:NH], row_max[:, t.par, :], -1.0, None, ALU.mult
                              ).then_inc(S["neg_hi_ready"], 1)

        def neg_max_lo(t):
            dve.wait_ge(S["neg_hi_ready"], t.n + 1)
            dve.scalar_tensor_tensor(neg_max[:, t.par, NH:2 * NH], row_max[:, t.par, :], -1.0,
                                     neg_max[:, t.par, 0:NH], ALU.mult, ALU.subtract
                                     ).then_inc(S["neg_max_ready"], 1)

        def invert_sums(t):
            dve.wait_ge(S["weighed"], t.n + 1)
            v = av_bank[:, 0:NH * VW].rearrange("p (h d) -> p h d", h=NH)
            dve.reciprocal(r_sum[:, t.par, :], v[:, :, HD:VW].rearrange("p h d -> p (h d)")).then_inc(S["sum_inverted"], 1)

        def normalise(t):
            v = av_bank[:, 0:NH * VW].rearrange("p (h d) -> p h d", h=NH)
            dve.wait_ge(S["sum_inverted"], t.n + 1)
            need(dve, S["att_transposed"], t.n - 1)
            dve.tensor_tensor(att[:, t.par, :, :], v[:, :, 0:HD],
                              r_sum[:, t.par, :].unsqueeze(2).to_broadcast([P, NH, HD]), ALU.mult
                              ).then_inc(S["att_ready"], 1)

        def att_lo(t):
            dve.wait_ge(S["at_h_ready"], t.n + 1)
            need(dve, S["o_projected"], t.n - 1)
            dve.tensor_tensor(at_l[:, t.par, :, :], av_bank[:, 0:D].rearrange("p (c n) -> p c n", c=KC),
                              at_h[:, t.par, :, :].bitcast(F32), ALU.subtract).then_inc(S["at_l_ready"], 1)

        def q_scale(t):
            dve.wait_ge(S["qk_rstd"], t.n + 1)
            dve.wait_ge(S["v_ready"], t.n + 1)
            need(dve, S["q_transposed"], t.n)
            dve.scalar_tensor_tensor(qn, qv_bank[:, 0:D], r_qk[:, t.par, 0:1], qk_norm[:, :], ALU.mult, ALU.mult).then_inc(S["qn_ready"], 1)

        def residual(t):
            dve.wait_ge(S["o_projected"], t.n + 1)
            dve.tensor_tensor(x1[:, t.at, :], mo_bank[:, 0:D], x1[:, t.at, :], ALU.add).then_inc(S["x1_ready"], 1)
            need_alone(dve, dve_passed, S["x1_ready"], t.n + 1)
            dve.bn_stats(stats2[:, t.par, :], x1[:, t.at, :]).then_inc(S["ln2_stats"], 1)
            need(dve, S["row_ready"], t.n - 1)
            need_alone(dve, dve_passed, S["ln2_stats"], t.n + 1)
            dve.bn_aggr(mean_var2[:, t.par, :], stats2[:, t.par, :]).then_inc(S["ln2_mean"], 1)

        def ln2_norm(t):
            dve.wait_ge(S["ln2_rstd"], t.n + 1)
            if t.quads_ok:
                dve.wait_ge(row_sent[t.slot], t.quad * 32)
            dve.tensor_scalar(row[:, 0, t.slot, 0:D], x1[:, t.at, :], mean_var2[:, t.par, 0:1], rstd2[:, t.par, :],
                              ALU.subtract, ALU.mult).then_inc(S["row_ready"], 1)

        def choose(a, b, pp):
            if a.first:
                dve.wait_ge(pool_setup, SETUP_POOL)
            need_alone(dve, dve_passed, S["logit_ready"], b.n + 1)
            for m in range(2):
                dve.max(top8[:, m, :], logit[:, m, :]).then_inc(R["tops"], 1)
            need_alone(dve, dve_passed, R["tops"], (a.pair + 1) * 2)
            for m in range(2):
                dve.max_index(top8_no[:, m, :], top8[:, m, :], logit[:, m, :]).then_inc(R["no_ready"], 1)
            dve.tensor_tensor(gap[:, pp, :], top8[:, :, 1], top8[:, :, 0], ALU.subtract).then_inc(R["gap_ready"], 1)
            dve.wait_ge(R["no_ready"], a.pair * 3 + 2)
            dve.tensor_copy(top_no[:, :, :], top8_no[:, :, 0:2]).then_inc(R["no_ready"], 1)
            dve.wait_ge(R["no_ready"], a.pair * 3 + 3)
            for k in range(2):
                dve.tensor_tensor(chosen[:, pp, k, :, :], expert_no[:, :].unsqueeze(1).to_broadcast([P, 2, NE]),
                                  top_no[:, :, k:k + 1].to_broadcast([P, 2, NE]), ALU.is_equal
                                  ).then_inc(R["choice_ready"], 1)
            dve.wait_ge(R["choice_ready"], a.pair * 3 + 2)
            dve.tensor_tensor(chosen_b[:, pp, :, :], chosen[:, pp, 0, :, :], chosen[:, pp, 1, :, :], ALU.add
                              ).then_inc(R["choice_ready"], 1)

        def route(a, b, pp):
            dve.wait_ge(R["counts_ready"], a.pair + 1)
            dve.tensor_tensor(place[:, :, :], counts[:, 0:2 * NE].rearrange("p (m e) -> p m e", m=2),
                              filled[:, :].unsqueeze(1).to_broadcast([P, 2, NE]), ALU.add
                              ).then_inc(R["place_ready"], 1)
            dve.wait_ge(R["place_ready"], a.pair + 1)
            dve.tensor_tensor(filled[:, :], filled[:, :], counts[:, 2 * NE:3 * NE], ALU.add
                              ).then_inc(R["filled_new"], 1)
            dve.tensor_tensor(place_of[:, :, :, :], chosen[:, pp, :, :, :],
                              place[:, :, :].unsqueeze(1).to_broadcast([P, 2, 2, NE]), ALU.mult
                              ).then_inc(R["place_sel"], 1)
            dve.wait_ge(R["place_sel"], a.pair + 1)
            dve.tensor_reduce(place_f[:, :, :], place_of[:, :, :, :], AX.X, ALU.add).then_inc(R["place_sum"], 1)
            dve.wait_ge(R["place_sum"], a.pair + 1)
            if a.sent is not None:
                dve.wait_ge(row_sent[a.slot], a.sent)
                dve.wait_ge(row_sent[b.slot], a.sent)
            dve.tensor_copy(place_i[:, pp, :, :], place_f[:, :, :]).then_inc(R["place_set"], 1)

        def turn(j, s):
            def tile(lag):
                t = Tile(j, s - lag)
                static = isinstance(j, int)
                t.twins_ok = not static or t.n >= 2
                t.quads_ok = not static or t.n >= 4
                t.at = t.n if static else bass.ds(t.n, 1)
                t.sent = t.quad * 32 if t.quads_ok else None
                return t
            ahead = tile(-2) if tile(-2).live else None
            if tile(0).live:
                xt_lo(tile(0))
            if isinstance(j, int) and j == s == 0:
                rest_of_setup()
            if tile(1).live:
                k_lo(tile(1))
            if tile(2).live:
                find_max(tile(2))
            if ahead:
                n = j * SKEW + s + 2 if isinstance(j, int) else None
                ln1_stats(ahead, {2: x_second, 8: x_third, 9: x_rest}.get(n))
            if tile(2).live:
                neg_max_hi(tile(2))
            if tile(3).live:
                invert_sums(tile(3))
            if tile(2).live:
                neg_max_lo(tile(2))
            if tile(3).live:
                normalise(tile(3))
            if ahead:
                ln1_mean(ahead)
            if tile(1).live:
                q_lo(tile(1))
            routed_first = s % 2 == 1 and tile(7).live and isinstance(j, int) and not tile(3).live
            if routed_first:
                route(tile(7), tile(6), (s - 7) // 2 % 2)
            if tile(4).live:
                ln2_norm(tile(4))
            if tile(3).live:
                att_lo(tile(3))
            if s % 2 == 0 and tile(6).live:
                a = tile(6)
                a.first = isinstance(j, int) and a.n == 0
                choose(a, tile(5), (s - 6) // 2 % 2)
            if s % 2 == 1 and tile(7).live and not routed_first:
                route(tile(7), tile(6), (s - 7) // 2 % 2)
            if tile(0).live:
                q_scale(tile(0))
            if tile(3).live:
                residual(tile(3))

        for n in range(2):
            t = Tile(0, n)
            t.at = n
            ln1_stats(t, x_first)
            ln1_mean(t)
        split_lo(0)
        split_biases()
        assert done[0] == SETUP_DVE_QK, done[0]

        def rest_of_setup():
            join_norms()
            split_lo(1)
            assert done[0] == SETUP_DVE, done[0]

        turns_sp(dve, turn)

        steps = [0]

        def step(ins):
            steps[0] += 1
            ins.then_inc(plan, 1)

        def stepped():
            dve.wait_ge(plan, steps[0])

        dve.wait_ge(R["filled_new"], NT // 2)
        step(dve.tensor_copy(pad_at[:, :], filled[0:1, :]))
        step(dve.scalar_tensor_tensor(count_i[:, :], filled[0:1, :], float(P - 1), region_no[:, :],
                                      ALU.add, ALU.subtract))
        stepped()
        step(dve.tensor_scalar(tiles_i[:, :], count_i[:, :], 7, None, ALU.arith_shift_right))
        stepped()
        step(dve.tensor_copy(tiles[:, :], tiles_i[:, :]))
        stepped()
        step(dve.tensor_tensor(cum_of[:, :, :], upto[:, :, :], tiles[:, :].unsqueeze(1).to_broadcast([1, NE, NE]),
                               ALU.mult))
        step(dve.tensor_scalar(cum[:, 1, :], tiles[:, :], -float(P), float(REG), ALU.mult, ALU.add))
        stepped()
        step(dve.tensor_reduce(cum[:, 0, :], cum_of[:, :, :], AX.X, ALU.add))
        stepped()
        step(dve.tensor_tensor(past[:, :, :], slot_no[:, :].unsqueeze(2).to_broadcast([1, NSLOT, NE]),
                               cum[:, 0, :].unsqueeze(1).to_broadcast([1, NSLOT, NE]), ALU.is_ge))
        stepped()
        step(dve.tensor_tensor(past_n[:, :, :], past[:, :, :],
                               cum[:, 1, :].unsqueeze(1).to_broadcast([1, NSLOT, NE]), ALU.mult))
        step(dve.tensor_reduce(slot_e[:, 0, :], past[:, :, :], AX.X, ALU.add))
        stepped()
        step(dve.tensor_reduce(slot_e[:, 1, :], past_n[:, :, :], AX.X, ALU.add))
        step(dve.tensor_scalar(slot_w[:, :], slot_e[:, 0, :], float(NE - 1), float(EW), ALU.min, ALU.mult))
        stepped()
        step(dve.scalar_tensor_tensor(slot_e[:, 2, :], slot_no[:, :], float(P), slot_e[:, 1, :], ALU.mult, ALU.add))
        stepped()
        step(dve.tensor_scalar(slot_row[:, :], slot_e[:, 2, :], float(NE * REG), None, ALU.min))
        assert steps[0] == PLAN, steps[0]

        def hst_lo(m, p):
            dve.wait_ge(F["h2_h_ready"], m + 1)
            need(dve, F["gate_up"], m - 1)
            dve.tensor_tensor(hst_l[:, p, :, :], bank[:, p, 0:D].rearrange("p (c n) -> p c n", c=KC),
                              hst_h[:, p, :, :].bitcast(F32), ALU.subtract).then_inc(F["h2_l_ready"], 1)

        def gate_mult(m, p, r):
            dve.wait_ge(F["silu_ready"], m + 1)
            need(dve, F["act_transposed"], m - 1)
            dve.scalar_tensor_tensor(act_u[:, p, :], silu_g[:, p, :], hs[:, r, D + 1:D + 2], bank[:, 2 + p, FI:2 * FI],
                                     ALU.mult, ALU.mult).then_inc(F["act_ready"], 1)

        def au_lo(m, p):
            dve.wait_ge(F["au_h_ready"], m * 2 + 2)
            need(dve, F["y_done"], m - 1)
            dve.tensor_tensor(au_l[:, p, 0, :], bank[:, 4 + p, 0:P], au_h[:, p, 0, :].bitcast(F32),
                              ALU.subtract).then_inc(F["au_l_ready"], 1)
            dve.tensor_tensor(au_l[0:FB, p, 1, :], bank[0:FB, 4 + p, P:2 * P], au_h[0:FB, p, 1, :].bitcast(F32),
                              ALU.subtract).then_inc(F["au_l_ready"], 1)

        def turn2(j, r, static):
            i = j * RING + r
            if not static or i < NSLOT:
                hst_lo(i, r % 2)
            if not static or 0 <= i - 1 < NSLOT:
                gate_mult(i - 1, (r - 1) % 2, (r - 1) % RING)
            if not static or 0 <= i - 2 < NSLOT:
                au_lo(i - 2, r % 2)

        slots(dve, turn2)

        for g in range(NT // 2):
            dve.wait_ge(fin_loaded[g], 32)
            v = fin_in[g][:, 0, :, :]
            dve.tensor_tensor(v, v, fin_in[g][:, 1, :, :], ALU.add).then_inc(fin_sum1, 1)
            dve.wait_ge(fin_sum1, g + 1)
            dve.tensor_tensor(v, v, x1[:, 2 * g:2 * g + 2, :], ALU.add).then_inc(fin_sum2, 1)

    @block.tensor
    def _(pe):
        pe.wait_ge(pool_setup, SETUP_POOL_FIRST)
        QM, KM, VM, OM = range(4)

        def three(dst, a_h, a_l, b_h, b_l, start, stop):
            pe.matmul(dst, a_h, b_h, start=start, stop=False)
            pe.matmul(dst, a_h, b_l, start=False, stop=False)
            return pe.matmul(dst, a_l, b_h, start=False, stop=stop)

        def project(dst, a_h, a_l, m):
            for c in range(KC):
                three(dst, a_h[:, c, :], a_l[:, c, :], wp_h[:, m, c, :], wp_l[:, m, c, :], c == 0, False)
            return pe.matmul(dst, ones_row[:, :], bias_hl[:, m * D:(m + 1) * D], start=False, stop=True)

        def tr_x(t):
            pe.wait_ge(S["xn_ready"], t.n + 1)
            need(pe, S["xt_l_ready"], t.n)
            need(pe, S["ht_ready"], t.n - 4)
            for c in range(KC):
                ins = pe.transpose(tr_bank[:, c * P:(c + 1) * P], xn[:, t.par, c * P:(c + 1) * P], ident[:, :])
            ins.then_inc(S["x_transposed"], 1)

        def tr_k(t):
            pe.wait_ge(S["kn_ready"], t.n + 1)
            need(pe, S["q_l_ready"], NQ * t.n)
            for c in range(KC):
                for q in range(2):
                    at = (c * 2 + q) * P
                    ins = pe.transpose(kq_bank[:, at:at + P], kn[:, t.par, q * D + c * P:q * D + (c + 1) * P], ident[:, :])
            ins.then_inc(S["k_transposed"], 1)

        def tr_q(t):
            pe.wait_ge(S["qn_ready"], t.n + 1)
            pe.wait_ge(S["k_l_ready"], t.n + 1)
            for c in range(KC):
                ins = pe.transpose(kq_bank[:, c * P:(c + 1) * P], qn[:, c * P:(c + 1) * P], ident[:, :])
            ins.then_inc(S["q_transposed"], 1)

        def score_max(t):
            pe.wait_ge(S["k_h_ready"], t.n + 1)
            pe.wait_ge(S["q_h_ready"], NQ * t.n + NQ)
            need(pe, S["probs_ready"], t.n)
            if t.first:
                pe.wait_ge(pool_setup, SETUP_POOL)
            for b in range(NB):
                for c in range(KC):
                    for gh in range(NQ // 2):
                        at = ((b * KC + c) * NQ // 2 + gh) * P
                        ins = pe.matmul(score_bank[:, at:at + P], flat(qp_h[:, t.par, b, c, 2 * gh:2 * gh + 2, :]),
                                        flat(kp[:, t.par, 0, b, c, :, :]), start=True, stop=True)
            ins.then_inc(S["max_scored"], 1)

        def weigh(t):
            pe.wait_ge(S["probs_ready"], t.n + 1)
            pe.wait_ge(v_spread[t.par], (t.twins + 1) * 64)
            need(pe, S["at_l_ready"], t.n)
            need(pe, S["logit_ready"], t.n - 1)
            for b in range(NB):
                for g in range(NPAIR):
                    at = (b * NPAIR + g) * L
                    ins = pe.matmul(av_bank[b * L:(b + 1) * L, g * 2 * VW:(g + 1) * 2 * VW],
                                    probs[:, t.par, at:at + L],
                                    v_bd[:, t.par, b, :, g * VW:(g + 1) * VW], start=True, stop=True)
            ins.then_inc(S["weighed"], 1)

        def project_kq(t):
            pe.wait_ge(S["ct_ready"], t.n + 1)
            need(pe, S["qn_ready"], t.n)
            need(pe, S["kn_ready"], t.n)
            if t.first:
                pe.wait_ge(dve_setup, SETUP_DVE_QK)
            project(k_bank[:, 0:D], ct_h[:, t.par], ct_l[:, t.par], KM).then_inc(S["k_projected"], 1)
            pe.wait_ge(S["xt_h_ready"], t.n + 1)
            pe.wait_ge(S["xt_l_ready"], t.n + 1)
            project(qv_bank[:, 0:D], xt_h[:, t.par], xt_l[:, t.par], QM)

        def project_v(t):
            if t.first:
                pe.wait_ge(dve_setup, SETUP_DVE)
            project(qv_bank[:, D:2 * D], ct_h[:, t.par], ct_l[:, t.par], VM).then_inc(S["projected"], 1)

        def tr_max(t):
            pe.wait_ge(S["neg_max_ready"], t.n + 1)
            need(pe, S["x1_ready"], t.n - 1)
            pe.transpose(mo_bank[0:2 * NH, 0:P // 2].bitcast(BF16), neg_max[:, t.par, :], ident_b[:, :]
                         ).then_inc(S["neg_max_transposed"], 1)

        def tr_att(t):
            pe.wait_ge(S["att_ready"], t.n + 1)
            for c in range(KC):
                ins = pe.transpose(av_bank[:, c * P:(c + 1) * P],
                                   att[:, t.par, c * 8:(c + 1) * 8, :].rearrange("p h d -> p (h d)"), ident[:, :])
            ins.then_inc(S["att_transposed"], 1)

        def tr_h(t):
            pe.wait_ge(S["row_ready"], t.n + 1)
            pe.wait_ge(S["xt_l_ready"], t.xt_read)
            for c in range(KC):
                ins = pe.transpose(tr_bank[:, c * P:(c + 1) * P], row[:, 0, t.slot, c * P:(c + 1) * P], ident[:, :])
            ins.then_inc(S["h_transposed"], 1)

        def score(t):
            pe.wait_ge(S["neg_max_t_ready"], t.n + 1)
            pe.wait_ge(S["k_l_ready"], t.n + 1)
            pe.wait_ge(S["q_l_ready"], NQ * t.n + NQ)
            pe.wait_ge(S["max_found"], t.n + 1)
            for b in range(NB):
                for c in range(KC):
                    dst = score_bank[:, (b * KC + c) * NQ * L:(b * KC + c + 1) * NQ * L]
                    k_h, k_l = (flat(kp[:, t.par, n, b, c, :, :]) for n in range(2))
                    q_h, q_l = (flat(q[:, t.par, b, c, :, :]) for q in (qp_h, qp_l))
                    pe.matmul(dst, k_h, q_h, start=True, stop=False)
                    pe.matmul(dst, k_h, q_l, start=False, stop=False)
                    pe.matmul(dst, k_l, q_h, start=False, stop=False)
                    for gh in range(NQ // 2):
                        ins = pe.matmul(dst[:, gh * P:(gh + 1) * P], head_of[:, (b * KC + c) * NQ // 2 + gh, :],
                                        neg_max_t[:, t.par, :], start=False, stop=gh == NQ // 2 - 1)
            ins.then_inc(S["scored"], 1)

        def gate(t):
            pe.wait_ge(S["ht_ready"], t.n + 1)
            if t.att_read is not None:
                pe.wait_ge(S["at_l_ready"], t.att_read)
            need(pe, S["logit_ready"], t.n)
            if t.first:
                pe.wait_ge(gate_w_loaded, 16)
            for half in range(2):
                rows = slice(half * 64, half * 64 + 64)
                for c in range(KC):
                    ins = pe.matmul(av_bank[rows, 0:NE], ht[:, t.par, c, rows], gate_w[:, c, :],
                                    start=(c == 0), stop=(c == KC - 1))
            ins.then_inc(S["gated"], 1)

        def project_out(t):
            pe.wait_ge(S["at_h_ready"], t.n + 1)
            pe.wait_ge(S["at_l_ready"], t.n + 1)
            if t.max_read is not None:
                pe.wait_ge(S["neg_max_t_ready"], t.max_read)
            project(mo_bank[:, 0:D], at_h[:, t.par], at_l[:, t.par], OM).then_inc(S["o_projected"], 1)

        def count_rows(pair, pp, att_read):
            pe.wait_ge(R["choice_ready"], pair * 3 + 3)
            pe.wait_ge(S["at_l_ready"], att_read)
            a, b = chosen_b[:, pp, 0, :], chosen_b[:, pp, 1, :]
            c = av_bank[:, count_cols]
            pe.matmul(c[:, 0:NE], below[:, :], a, start=True, stop=True)
            pe.matmul(c[:, NE:2 * NE], below[:, :], b, start=True, stop=False)
            pe.matmul(c[:, NE:2 * NE], ones_b[:, :], a, start=False, stop=True)
            pe.matmul(c[:, 2 * NE:3 * NE], ones_b[:, :], a, start=True, stop=False)
            pe.matmul(c[:, 2 * NE:3 * NE], ones_b[:, :], b, start=False, stop=True).then_inc(R["routed"], 1)

        def turn(j, s):
            static = isinstance(j, int)
            i = j * SKEW + s

            def tile(lag):
                return Tile(j, s - lag)

            def seen(value):
                return min(value, NT) if static else value

            if tile(0).live:
                tr_x(tile(0))
            if tile(1).live:
                tr_k(tile(1))
            if tile(2).live:
                t = tile(2)
                t.first = static and i == 2
                score_max(t)
            if tile(3).live:
                weigh(tile(3))
            if tile(1).live:
                tr_q(tile(1))
            if tile(0).live:
                t = tile(0)
                t.first = static and i == 0
                project_kq(t)
            if tile(2).live:
                tr_max(tile(2))
            if tile(0).live:
                t = tile(0)
                t.first = static and i == 0
                project_v(t)
            if tile(3).live:
                tr_att(tile(3))
            if tile(2).live:
                score(tile(2))
            if tile(4).live:
                t = tile(4)
                t.xt_read = seen(i + 1)
                tr_h(t)
            if tile(3).live:
                t = tile(3)
                t.max_read = seen(i - 1)
                project_out(t)
            if s % 2 == 0 and tile(6).live:
                count_rows(tile(6).pair, (s - 6) // 2 % 2, seen(i - 2))
            if tile(4).live:
                t = tile(4)
                t.att_read = seen(i - 2)
                t.first = static and i == 4
                gate(t)

        turns_sp(pe, turn)

        def tr_hs(m, p, j, r):
            pe.wait_ge(hs_loaded[r], (j + 1) * 16)
            for c in range(KC):
                ins = pe.transpose(bank[:, p, c * P:(c + 1) * P], hs[:, r, c * P:(c + 1) * P], ident[:, :])
            ins.then_inc(F["h2_transposed"], 1)

        def weights_of(m):
            return pe.value_load(slot_w[0:1, bass.ds(m, 1)], min_val=0, max_val=(NE - 1) * EW)

        def gate_up(m, p, w):
            pe.wait_ge(F["h2_l_ready"], m + 1)
            for c in range(KC):
                w_h, w_l = (t[:, c * 2 * FI:][:, bass.ds(w, 2 * FI)] for t in (we_h, we_l))
                ins = three(bank[:, 2 + p, 0:2 * FI], hst_h[:, p, c, :], hst_l[:, p, c, :], w_h, w_l, c == 0, c == KC - 1)
            ins.then_inc(F["gate_up"], 1)

        def tr_act(m, p):
            pe.wait_ge(F["act_ready"], m + 1)
            pe.transpose(bank[:, 4 + p, 0:P], act_u[:, p, 0:FA], ident[:, :])
            pe.transpose(bank[0:FB, 4 + p, P:2 * P], act_u[:, p, FA:FI], ident[:, :]).then_inc(F["act_transposed"], 1)

        def down(m, p, w, last):
            pe.wait_ge(F["au_l_ready"], m * 2 + 2)
            if last:
                pe.wait_ge(F["y_ready"], m - 1)
            for n, rows in enumerate((FA, FB)):
                w_h, w_l = (t[0:rows, 2 * KC * FI + n * D:][:, bass.ds(w, D)] for t in (we_h, we_l))
                ins = three(bank[:, 6 + p, 0:D], au_h[0:rows, p, n, :], au_l[0:rows, p, n, :], w_h, w_l, n == 0, n == 1)
            ins.then_inc(F["y_done"], 1)

        pe.wait_ge(plan, PLAN)
        pe.wait_ge(S["we_ready"], NT)
        pe.wait_ge(S["ht_ready"], NT)
        pe.wait_ge(R["filled_new"], NT // 2)

        found = {}

        def turn2(j, r, static):
            i = j * RING + r
            gates = not static or 0 <= i - 1 < NSLOT
            if gates:
                found[r] = weights_of(i - 1)
            if not static or i < NSLOT:
                tr_hs(i, r % 2, j, r)
            if not static or 0 <= i - 2 < NSLOT:
                tr_act(i - 2, r % 2)
            if gates:
                gate_up(i - 1, (r - 1) % 2, found[r])
            if not static or 0 <= i - 3 < NSLOT:
                down(i - 3, (r - 3) % 2, found[r - 2] if r >= 2 else weights_of(i - 3), not gates)

        slots(pe, turn2)


PLAN = 14


def turns_sp(eng, turn):
    first, last = 2, NT // SKEW - 1
    for j in range(first):
        for s in range(SKEW):
            turn(j, s)
    with eng.Fori(first, last) as j:
        for s in range(SKEW):
            turn(j, s)
    for i in range(last * SKEW, LAST):
        turn(i // SKEW, i % SKEW)


def slots(eng, turn):
    for r in range(RING):
        turn(0, r, True)
    with eng.Fori(1, NSLOT // RING) as j:
        for r in range(RING):
            turn(j, r, False)
    for r in range(3):
        turn(NSLOT // RING, r, True)


def kernel(**inputs):
    import concourse.bacc as bacc
    from concourse.bass_utils import run_bass_kernel_spmd

    def get(name):
        return np.ascontiguousarray(inputs[name])

    def weight(name):
        return get(name).T.reshape(KC, P, D).transpose(1, 0, 2)

    v_order = np.arange(D).reshape(NPAIR, 2, HD).transpose(1, 0, 2).reshape(D)
    w_v = weight("L0_xattn_v_img_w")[:, :, v_order]
    w_proj = np.stack([weight("L0_xattn_q_w"), weight("L0_xattn_k_img_w"), w_v, weight("L0_xattn_o_w")], 1)
    bias = np.concatenate([get("L0_xattn_q_b"), get("L0_xattn_k_img_b"), get("L0_xattn_v_img_b")[v_order],
                           get("L0_xattn_o_b")])
    w1 = get("L0_ffn_w1").reshape(NE, 2 * FI, KC, P).transpose(3, 0, 2, 1).reshape(P, NE, KC * 2 * FI)
    w2 = get("L0_ffn_w2").transpose(2, 0, 1)
    w2b = np.zeros((P, NE, D), w2.dtype)
    w2b[:FB] = w2[FA:]
    w_exp = np.concatenate([w1, w2[:FA], w2b], 2).reshape(P, NT, WS).transpose(1, 0, 2).reshape(NT * P, WS)
    ctx_t = get("ctx_2048").reshape(NT, P, KC, P).transpose(0, 3, 2, 1).reshape(NT * P, KC * P)
    w_gate = get("L0_ffn_gate_w").T.reshape(KC, P, NE).transpose(1, 0, 2).reshape(P, KC * NE)
    arrays = {
        "x": get("x").reshape(T, D),
        "ctx_t": ctx_t,
        "w_proj": w_proj.reshape(P, 4 * KC * D),
        "w_exp": w_exp,
        "w_gate": w_gate,
        "bias": np.stack([bias, bias]),
        "norm_q": get("L0_xattn_norm_q_w"),
        "norm_k": get("L0_xattn_norm_k_img_w"),
    }
    arrays = {n: np.ascontiguousarray(a) for n, a in arrays.items()}
    nc = bacc.Bacc("TRN2", target_bir_lowering=False, num_devices=1)
    args = [nc.dram_tensor(n, a.shape, mybir.dt.from_np(a.dtype), kind="ExternalInput").ap()
            for n, a in arrays.items()]
    out = nc.dram_tensor("out", (T, D), F32, kind="ExternalOutput").ap()
    build(nc, *args, out)
    r = run_bass_kernel_spmd(nc, [arrays], core_ids=[0])
    return r.results[0]["out"].reshape(B, L, D)
```
